# Optimizing a Trainium2 kernel written in Bass

```python
import numpy as np
import jax
import jax.numpy as jnp

def _softmax(x, axis=-1):
    return jax.nn.softmax(x, axis=axis)

def _gelu(x):
    return jax.nn.gelu(x, approximate=True)

def _silu(x):
    return jax.nn.silu(x)

def _sigmoid(x):
    return jax.nn.sigmoid(x)

def _layernorm(x, axis=-1, eps=1e-05):
    m = jnp.mean(x, axis=axis, keepdims=True)
    v = jnp.var(x, axis=axis, keepdims=True)
    return (x - m) / jnp.sqrt(v + eps)

def _scatter_add(tgt, idx, src, axis=0):
    return tgt.at[idx].add(src)

def _segment_sum(src, seg, n):
    return jax.ops.segment_sum(src, seg, n)
kernel_name = 'mk_macaron_d2_jaxref_r8_72b3ab'

def setup_inputs(seed: int=0):
    np.random.seed(seed)
    _w = jnp.asarray

    def _L0_attn_setup():
        import jax, jax.numpy as jnp
        import numpy as np
        from jax import lax
        H = 16
        MB = 16
        LR = 1.0
        ROPE_BASE = 10000.0
        LN_EPS = 1e-05

        def _rotate_half(u):
            u1, u2 = jnp.split(u, 2, axis=-1)
            return jnp.concatenate([-u2, u1], axis=-1)
        key = jax.random.key(seed)
        ks = jax.random.split(key, 4)
        B, S, D = (4, 512, 256)
        x = jax.random.normal(ks[0], (B, S, D), dtype=jnp.float32)
        scale = 1.0 / np.sqrt(D)
        Wk = jax.random.normal(ks[1], (D, D), dtype=jnp.float32) * scale
        Wv = jax.random.normal(ks[2], (D, D), dtype=jnp.float32) * scale
        Wo = jax.random.normal(ks[3], (D, D), dtype=jnp.float32) * scale
        ln_gamma = jnp.ones((D,), dtype=jnp.float32)
        ln_beta = jnp.zeros((D,), dtype=jnp.float32)
        return {'x': x, 'Wk': Wk, 'Wv': Wv, 'Wo': Wo, 'ln_gamma': ln_gamma, 'ln_beta': ln_beta}
    _L0_attn_in = _L0_attn_setup()

    def _L0_ffn_setup():
        import jax, jax.numpy as jnp
        import numpy as np
        TOP_K = 2

        def moe_forward(x, w_gate_router, w_gate_proj, w_up_proj, w_down_proj):
            E = w_gate_router.shape[0]
            scores = jnp.einsum('bsd,ed->bse', x, w_gate_router)
            topk_scores, topk_idx = jax.lax.top_k(scores, TOP_K)
            topk_probs = jax.nn.softmax(topk_scores, axis=-1)
            weights = jnp.sum(topk_probs[..., None] * jax.nn.one_hot(topk_idx, E, dtype=x.dtype), axis=-2)
            gate = jnp.einsum('bsd,efd->bsef', x, w_gate_proj)
            up = jnp.einsum('bsd,efd->bsef', x, w_up_proj)
            hidden = jax.nn.silu(gate) * up
            out = jnp.einsum('bsef,edf,bse->bsd', hidden, w_down_proj, weights)
            return out
        key = jax.random.key(seed)
        k1, k2, k3, k4, k5 = jax.random.split(key, 5)
        B, S, D, E, F = (2, 128, 256, 8, 96)
        scale_in = 1.0 / np.sqrt(D)
        scale_ff = 1.0 / np.sqrt(F)
        return {'x': jax.random.normal(k1, (B, S, D), dtype=jnp.float32), 'w_gate_router': jax.random.normal(k2, (E, D), dtype=jnp.float32) * scale_in, 'w_gate_proj': jax.random.normal(k3, (E, F, D), dtype=jnp.float32) * scale_in, 'w_up_proj': jax.random.normal(k4, (E, F, D), dtype=jnp.float32) * scale_in, 'w_down_proj': jax.random.normal(k5, (E, D, F), dtype=jnp.float32) * scale_ff}
    _L0_ffn_in = _L0_ffn_setup()

    def _L1_attn_setup():
        import jax, jax.numpy as jnp
        import numpy as np
        import math
        B, S, HID = (2, 256, 256)
        NH = 16
        QK_NOPE, QK_ROPE, KV_RANK, Q_RANK, V_DIM = (64, 64, 64, 64, 64)
        Q_HEAD = QK_NOPE + QK_ROPE
        ROPE_BASE = 10000.0
        FACTOR = 40.0
        BETA_FAST, BETA_SLOW = (32.0, 1.0)
        ORIG_MAX = 512
        MSCALE = 0.707
        SOFTMAX_SCALE = Q_HEAD ** (-0.5)

        def yarn_get_mscale(scale, mscale=1.0):
            if scale <= 1:
                return 1.0
            return 0.1 * mscale * math.log(scale) + 1.0

        def yarn_cos_sin(seq_len, dim):
            exponents = np.arange(0, dim, 2, dtype=np.float64) / dim
            freq_extra = 1.0 / ROPE_BASE ** exponents
            freq_inter = 1.0 / (FACTOR * ROPE_BASE ** exponents)

            def corr_dim(num_rot):
                return dim * math.log(ORIG_MAX / (num_rot * 2 * math.pi)) / (2 * math.log(ROPE_BASE))
            low = max(math.floor(corr_dim(BETA_FAST)), 0)
            high = min(math.ceil(corr_dim(BETA_SLOW)), dim - 1)
            if low == high:
                high = high + 0.001
            ramp = np.clip((np.arange(dim // 2, dtype=np.float64) - low) / (high - low), 0.0, 1.0)
            inv_freq_mask = 1.0 - ramp
            inv_freq = freq_inter * (1.0 - inv_freq_mask) + freq_extra * inv_freq_mask
            t = np.arange(seq_len, dtype=np.float64)
            freqs = np.outer(t, inv_freq)
            msc = yarn_get_mscale(FACTOR, MSCALE) / yarn_get_mscale(FACTOR, 0.0)
            emb = np.concatenate([freqs, freqs], axis=-1)
            return (jnp.asarray(np.cos(emb) * msc, jnp.float32), jnp.asarray(np.sin(emb) * msc, jnp.float32))

        def rms_norm(x, w, eps=1e-06):
            xf = x.astype(jnp.float32)
            var = jnp.mean(xf * xf, axis=-1, keepdims=True)
            return (xf * jax.lax.rsqrt(var + eps)).astype(x.dtype) * w

        def rotate_half(x):
            x1, x2 = jnp.split(x, 2, axis=-1)
            return jnp.concatenate([-x2, x1], axis=-1)

        def apply_rope(x, cos, sin):
            b, h, s, d = x.shape
            x = x.reshape(b, h, s, d // 2, 2).transpose(0, 1, 2, 4, 3).reshape(b, h, s, d)
            return x * cos + rotate_half(x) * sin
        key = jax.random.key(seed)
        ks = jax.random.split(key, 8)
        sc = 0.02
        return {'hidden_states': jax.random.normal(ks[0], (B, S, HID), jnp.float32), 'wq_a': jax.random.normal(ks[1], (HID, Q_RANK), jnp.float32) * sc, 'q_a_norm_w': jnp.ones((Q_RANK,), jnp.float32), 'wq_b': jax.random.normal(ks[2], (Q_RANK, NH * Q_HEAD), jnp.float32) * sc, 'wkv_a': jax.random.normal(ks[3], (HID, KV_RANK + QK_ROPE), jnp.float32) * sc, 'kv_a_norm_w': jnp.ones((KV_RANK,), jnp.float32), 'wkv_b': jax.random.normal(ks[4], (KV_RANK, NH * (QK_NOPE + V_DIM)), jnp.float32) * sc, 'wo': jax.random.normal(ks[5], (NH * V_DIM, HID), jnp.float32) * sc}
    _L1_attn_in = _L1_attn_setup()

    def _L1_ffn_setup():
        import jax, jax.numpy as jnp
        import numpy as np
        TOP_K = 6
        CAP_FACTOR = 2

        def _shared_swiglu(x, wg, wu, wd):
            return jax.nn.silu(x @ wg.T) * (x @ wu.T) @ wd.T
        key = jax.random.key(seed)
        ks = jax.random.split(key, 8)
        B, S, D, E, F, FS = (4, 256, 256, 64, 176, 352)
        scale = jnp.float32(0.02)
        return {'hidden_states': jax.random.normal(ks[0], (B, S, D), jnp.float32), 'gate_w': jax.random.normal(ks[1], (E, D), jnp.float32) * scale, 'w_gate': jax.random.normal(ks[2], (E, F, D), jnp.float32) * scale, 'w_up': jax.random.normal(ks[3], (E, F, D), jnp.float32) * scale, 'w_down': jax.random.normal(ks[4], (E, D, F), jnp.float32) * scale, 'sh_gate': jax.random.normal(ks[5], (FS, D), jnp.float32) * scale, 'sh_up': jax.random.normal(ks[6], (FS, D), jnp.float32) * scale, 'sh_down': jax.random.normal(ks[7], (D, FS), jnp.float32) * scale}
    _L1_ffn_in = _L1_ffn_setup()
    _d = {'L0_attn_x': _L0_attn_in['x'], 'L0_attn_Wk': _L0_attn_in['Wk'], 'L0_attn_Wv': _L0_attn_in['Wv'], 'L0_attn_Wo': _L0_attn_in['Wo'], 'L0_attn_ln_gamma': _L0_attn_in['ln_gamma'], 'L0_attn_ln_beta': _L0_attn_in['ln_beta'], 'L0_ffn_w_gate_router': _L0_ffn_in['w_gate_router'], 'L0_ffn_w_gate_proj': _L0_ffn_in['w_gate_proj'], 'L0_ffn_w_up_proj': _L0_ffn_in['w_up_proj'], 'L0_ffn_w_down_proj': _L0_ffn_in['w_down_proj'], 'L1_attn_wq_a': _L1_attn_in['wq_a'], 'L1_attn_q_a_norm_w': _L1_attn_in['q_a_norm_w'], 'L1_attn_wq_b': _L1_attn_in['wq_b'], 'L1_attn_wkv_a': _L1_attn_in['wkv_a'], 'L1_attn_kv_a_norm_w': _L1_attn_in['kv_a_norm_w'], 'L1_attn_wkv_b': _L1_attn_in['wkv_b'], 'L1_attn_wo': _L1_attn_in['wo'], 'L1_ffn_gate_w': _L1_ffn_in['gate_w'], 'L1_ffn_w_gate': _L1_ffn_in['w_gate'], 'L1_ffn_w_up': _L1_ffn_in['w_up'], 'L1_ffn_w_down': _L1_ffn_in['w_down'], 'L1_ffn_sh_gate': _L1_ffn_in['sh_gate'], 'L1_ffn_sh_up': _L1_ffn_in['sh_up'], 'L1_ffn_sh_down': _L1_ffn_in['sh_down']}
    _x0 = _d['L0_attn_x']
    _d['L0_attn_x'] = jax.random.normal(jax.random.fold_in(jax.random.key(seed), 1), (2, 1024, 256), dtype=_x0.dtype)
    del _x0
    return _d

def reference(L0_attn_x, L0_attn_Wk, L0_attn_Wv, L0_attn_Wo, L0_attn_ln_gamma, L0_attn_ln_beta, L0_ffn_w_gate_router, L0_ffn_w_gate_proj, L0_ffn_w_up_proj, L0_ffn_w_down_proj, L1_attn_wq_a, L1_attn_q_a_norm_w, L1_attn_wq_b, L1_attn_wkv_a, L1_attn_kv_a_norm_w, L1_attn_wkv_b, L1_attn_wo, L1_ffn_gate_w, L1_ffn_w_gate, L1_ffn_w_up, L1_ffn_w_down, L1_ffn_sh_gate, L1_ffn_sh_up, L1_ffn_sh_down):

    def _L0_attn_ref(x, Wk, Wv, Wo, ln_gamma, ln_beta):
        import jax, jax.numpy as jnp
        import numpy as np
        from jax import lax
        H = 16
        MB = 16
        LR = 1.0
        ROPE_BASE = 10000.0
        LN_EPS = 1e-05

        def _rotate_half(u):
            u1, u2 = jnp.split(u, 2, axis=-1)
            return jnp.concatenate([-u2, u1], axis=-1)
        B, S, Dm = x.shape
        Dh = Dm // H
        k = (x @ Wk.T).reshape(B, S, H, Dh).transpose(0, 2, 1, 3)
        v = (x @ Wv.T).reshape(B, S, H, Dh).transpose(0, 2, 1, 3)
        inv_freq = 1.0 / ROPE_BASE ** (jnp.arange(0, Dh, 2, dtype=jnp.float32) / Dh)
        t = jnp.arange(S, dtype=jnp.float32)
        freqs = t[:, None] * inv_freq[None, :]
        emb = jnp.concatenate([freqs, freqs], axis=-1)
        cos, sin = (jnp.cos(emb), jnp.sin(emb))
        k = k * cos + _rotate_half(k) * sin
        nmb = S // MB
        k_c = k.reshape(B, H, nmb, MB, Dh).transpose(2, 0, 1, 3, 4)
        v_c = v.reshape(B, H, nmb, MB, Dh).transpose(2, 0, 1, 3, 4)
        W0 = jnp.broadcast_to(jnp.eye(Dh, dtype=x.dtype), (B, H, Dh, Dh))
        inv_n = 2.0 / (MB * Dh)

        def step(W, kv):
            kc, vc = kv
            z = jnp.einsum('bhsd,bhde->bhse', kc, W)
            grad = jnp.einsum('bhsd,bhse->bhde', kc, (z - vc) * inv_n)
            return (W - LR * grad, z)
        _, zs = lax.scan(step, W0, (k_c, v_c))
        out = zs.transpose(1, 2, 0, 3, 4).reshape(B, H, S, Dh)
        out = out.transpose(0, 2, 1, 3).reshape(B, S, Dm)
        mu = jnp.mean(out, axis=-1, keepdims=True)
        var = jnp.var(out, axis=-1, keepdims=True)
        out = (out - mu) * lax.rsqrt(var + LN_EPS) * ln_gamma + ln_beta
        return out @ Wo.T

    def _L0_ffn_ref(x, w_gate_router, w_gate_proj, w_up_proj, w_down_proj):
        import jax, jax.numpy as jnp
        import numpy as np
        TOP_K = 2

        def moe_forward(x, w_gate_router, w_gate_proj, w_up_proj, w_down_proj):
            E = w_gate_router.shape[0]
            scores = jnp.einsum('bsd,ed->bse', x, w_gate_router)
            topk_scores, topk_idx = jax.lax.top_k(scores, TOP_K)
            topk_probs = jax.nn.softmax(topk_scores, axis=-1)
            weights = jnp.sum(topk_probs[..., None] * jax.nn.one_hot(topk_idx, E, dtype=x.dtype), axis=-2)
            gate = jnp.einsum('bsd,efd->bsef', x, w_gate_proj)
            up = jnp.einsum('bsd,efd->bsef', x, w_up_proj)
            hidden = jax.nn.silu(gate) * up
            out = jnp.einsum('bsef,edf,bse->bsd', hidden, w_down_proj, weights)
            return out
        return moe_forward(x, w_gate_router, w_gate_proj, w_up_proj, w_down_proj)

    def _L1_attn_ref(hidden_states, wq_a, q_a_norm_w, wq_b, wkv_a, kv_a_norm_w, wkv_b, wo):
        import jax, jax.numpy as jnp
        import numpy as np
        import math
        B, S, HID = (2, 256, 256)
        NH = 16
        QK_NOPE, QK_ROPE, KV_RANK, Q_RANK, V_DIM = (64, 64, 64, 64, 64)
        Q_HEAD = QK_NOPE + QK_ROPE
        ROPE_BASE = 10000.0
        FACTOR = 40.0
        BETA_FAST, BETA_SLOW = (32.0, 1.0)
        ORIG_MAX = 512
        MSCALE = 0.707
        SOFTMAX_SCALE = Q_HEAD ** (-0.5)

        def yarn_get_mscale(scale, mscale=1.0):
            if scale <= 1:
                return 1.0
            return 0.1 * mscale * math.log(scale) + 1.0

        def yarn_cos_sin(seq_len, dim):
            exponents = np.arange(0, dim, 2, dtype=np.float64) / dim
            freq_extra = 1.0 / ROPE_BASE ** exponents
            freq_inter = 1.0 / (FACTOR * ROPE_BASE ** exponents)

            def corr_dim(num_rot):
                return dim * math.log(ORIG_MAX / (num_rot * 2 * math.pi)) / (2 * math.log(ROPE_BASE))
            low = max(math.floor(corr_dim(BETA_FAST)), 0)
            high = min(math.ceil(corr_dim(BETA_SLOW)), dim - 1)
            if low == high:
                high = high + 0.001
            ramp = np.clip((np.arange(dim // 2, dtype=np.float64) - low) / (high - low), 0.0, 1.0)
            inv_freq_mask = 1.0 - ramp
            inv_freq = freq_inter * (1.0 - inv_freq_mask) + freq_extra * inv_freq_mask
            t = np.arange(seq_len, dtype=np.float64)
            freqs = np.outer(t, inv_freq)
            msc = yarn_get_mscale(FACTOR, MSCALE) / yarn_get_mscale(FACTOR, 0.0)
            emb = np.concatenate([freqs, freqs], axis=-1)
            return (jnp.asarray(np.cos(emb) * msc, jnp.float32), jnp.asarray(np.sin(emb) * msc, jnp.float32))

        def rms_norm(x, w, eps=1e-06):
            xf = x.astype(jnp.float32)
            var = jnp.mean(xf * xf, axis=-1, keepdims=True)
            return (xf * jax.lax.rsqrt(var + eps)).astype(x.dtype) * w

        def rotate_half(x):
            x1, x2 = jnp.split(x, 2, axis=-1)
            return jnp.concatenate([-x2, x1], axis=-1)

        def apply_rope(x, cos, sin):
            b, h, s, d = x.shape
            x = x.reshape(b, h, s, d // 2, 2).transpose(0, 1, 2, 4, 3).reshape(b, h, s, d)
            return x * cos + rotate_half(x) * sin
        b, s, _ = hidden_states.shape
        q = rms_norm(hidden_states @ wq_a, q_a_norm_w) @ wq_b
        q = q.reshape(b, s, NH, Q_HEAD).transpose(0, 2, 1, 3)
        q_nope, q_pe = (q[..., :QK_NOPE], q[..., QK_NOPE:])
        ckv = hidden_states @ wkv_a
        compressed_kv, k_pe = (ckv[..., :KV_RANK], ckv[..., KV_RANK:])
        k_pe = k_pe.reshape(b, s, 1, QK_ROPE).transpose(0, 2, 1, 3)
        kv = rms_norm(compressed_kv, kv_a_norm_w) @ wkv_b
        kv = kv.reshape(b, s, NH, QK_NOPE + V_DIM).transpose(0, 2, 1, 3)
        k_nope, value_states = (kv[..., :QK_NOPE], kv[..., QK_NOPE:])
        cos, sin = yarn_cos_sin(s, QK_ROPE)
        cos, sin = (cos[None, None], sin[None, None])
        k_pe = jnp.broadcast_to(k_pe, (b, NH, s, QK_ROPE))
        q_pe = apply_rope(q_pe, cos, sin)
        k_pe = apply_rope(k_pe, cos, sin)
        query_states = jnp.concatenate([q_nope, q_pe], axis=-1)
        key_states = jnp.concatenate([k_nope, k_pe], axis=-1)
        attn = jnp.einsum('bhqd,bhkd->bhqk', query_states, key_states) * SOFTMAX_SCALE
        attn = jax.nn.softmax(attn.astype(jnp.float32), axis=-1).astype(query_states.dtype)
        out = jnp.einsum('bhqk,bhkd->bhqd', attn, value_states)
        out = out.transpose(0, 2, 1, 3).reshape(b, s, NH * V_DIM)
        return out @ wo

    def _L1_ffn_ref(hidden_states, gate_w, w_gate, w_up, w_down, sh_gate, sh_up, sh_down):
        import jax, jax.numpy as jnp
        import numpy as np
        TOP_K = 6
        CAP_FACTOR = 2

        def _shared_swiglu(x, wg, wu, wd):
            return jax.nn.silu(x @ wg.T) * (x @ wu.T) @ wd.T
        B, S, D = hidden_states.shape
        E = gate_w.shape[0]
        x = hidden_states.reshape(-1, D)
        N = x.shape[0]
        A = N * TOP_K
        C = CAP_FACTOR * ((A + E - 1) // E)
        scores = jax.nn.softmax(x @ gate_w.T, axis=-1)
        topk_w, topk_idx = jax.lax.top_k(scores, TOP_K)
        topk_w = topk_w / (topk_w.sum(-1, keepdims=True) + 1e-20)
        flat_e = topk_idx.reshape(-1)
        flat_w = topk_w.reshape(-1)
        order = jnp.argsort(flat_e)
        se = flat_e[order]
        st = order // TOP_K
        sw = flat_w[order]
        counts = jnp.bincount(flat_e, length=E)
        offsets = jnp.cumsum(counts) - counts
        pos = jnp.arange(A) - offsets[se]
        valid = pos < C
        pos_c = jnp.minimum(pos, C - 1)
        buf = jnp.zeros((E, C, D), x.dtype).at[se, pos_c].add(jnp.where(valid[:, None], x[st], jnp.zeros((), x.dtype)))
        g = jnp.einsum('ecd,efd->ecf', buf, w_gate)
        u = jnp.einsum('ecd,efd->ecf', buf, w_up)
        eo = jnp.einsum('ecf,edf->ecd', jax.nn.silu(g) * u, w_down)
        gathered = eo[se, pos_c] * (sw * valid.astype(sw.dtype))[:, None]
        y = jnp.zeros_like(x).at[st].add(gathered).reshape(B, S, D)
        return y + _shared_swiglu(hidden_states, sh_gate, sh_up, sh_down)
    x = L0_attn_x
    x = x + 0.5 * _L0_ffn_ref(_layernorm(x, axis=-1), L0_ffn_w_gate_router, L0_ffn_w_gate_proj, L0_ffn_w_up_proj, L0_ffn_w_down_proj)
    x = x + _L0_attn_ref(_layernorm(x, axis=-1), L0_attn_Wk, L0_attn_Wv, L0_attn_Wo, L0_attn_ln_gamma, L0_attn_ln_beta)
    x = x + 0.5 * _L0_ffn_ref(_layernorm(x, axis=-1), L0_ffn_w_gate_router, L0_ffn_w_gate_proj, L0_ffn_w_up_proj, L0_ffn_w_down_proj)
    x = x + 0.5 * _L1_ffn_ref(_layernorm(x, axis=-1), L1_ffn_gate_w, L1_ffn_w_gate, L1_ffn_w_up, L1_ffn_w_down, L1_ffn_sh_gate, L1_ffn_sh_up, L1_ffn_sh_down)
    x = x + _L1_attn_ref(_layernorm(x, axis=-1), L1_attn_wq_a, L1_attn_q_a_norm_w, L1_attn_wq_b, L1_attn_wkv_a, L1_attn_kv_a_norm_w, L1_attn_wkv_b, L1_attn_wo)
    x = x + 0.5 * _L1_ffn_ref(_layernorm(x, axis=-1), L1_ffn_gate_w, L1_ffn_w_gate, L1_ffn_w_up, L1_ffn_w_down, L1_ffn_sh_gate, L1_ffn_sh_up, L1_ffn_sh_down)
    return x

_drawn_inputs = setup_inputs


def setup_inputs(seed=0):
    import zlib

    import numpy as np

    out = dict(_drawn_inputs(seed))
    spreads = {'L0_attn_ln_gamma': (1.0, 0.2),
     'L0_attn_ln_beta': (0.0, 0.1),
     'L1_attn_q_a_norm_w': (1.0, 0.6),
     'L1_attn_kv_a_norm_w': (1.0, 0.6)}
    factors = {'L1_attn_wq_a': 8.0,
     'L1_attn_wq_b': 8.0,
     'L1_attn_wkv_a': 8.0,
     'L1_attn_wkv_b': 8.0,
     'L1_attn_wo': 8.0,
     'L1_ffn_gate_w': 8.0,
     'L1_ffn_w_gate': 8.0,
     'L1_ffn_w_up': 8.0,
     'L1_ffn_w_down': 8.0,
     'L1_ffn_sh_gate': 4.239,
     'L1_ffn_sh_up': 4.234,
     'L1_ffn_sh_down': 4.219}
    for name, (base, spread) in spreads.items():
        noise = np.random.default_rng([zlib.crc32(name.encode()), seed]).standard_normal(out[name].shape)
        drawn = base * np.exp(spread * noise) if base else spread * noise
        out[name] = jnp.asarray(drawn.astype(out[name].dtype))
    for name, factor in factors.items():
        out[name] = (out[name] * factor).astype(out[name].dtype)
    return out
```

```python
from contextlib import ExitStack

import concourse.bass as bass
import numpy as np
from concourse import mybir
from concourse.alu_op_type import AluOpType as ALU

F32 = mybir.dt.float32
BF16 = mybir.dt.bfloat16
U32 = mybir.dt.uint32
I32 = mybir.dt.int32
ACT = mybir.ActivationFunctionType
AX = mybir.AxisListType.X

P = 128
BATCH, SEQ, D = 2, 1024, 256
TOKENS = BATCH * SEQ
TILES = TOKENS // P
DK = D // P
GT = 4
GROUPS = TILES // GT
GW = GT * P
LN_EPS = 1e-5
RMS_EPS = 1e-6

E0, F0 = 8, 96
H0, DH0, MB = 16, 16, 16
STEPS0 = SEQ // MB
HG = 8
NBG = BATCH * (H0 // HG)
STEP_SCALE = 2.0 / (MB * DH0)
E1, F1, K1, FS = 64, 176, 6, 352
CAP = 2 * ((TOKENS * K1 + E1 - 1) // E1)
CT = CAP // P
FA, FB = P, F1 - P
UB = 64
FBM = UB + FB
SLOTS = E1 * CAP
SHARED = [(0, 128), (128, 128), (256, 96)]
NH, NOPE, ROPE, RANK, VD = 16, 64, 64, 64, 64
SM_SCALE = (NOPE + ROPE) ** -0.5
KT_TILES = SEQ // P


class Steps:

    def __init__(self, eng, sem, base=0):
        self.eng, self.sem, self.base, self.n = eng, sem, base, 0

    def then(self, ins, apart=None):
        ins.then_inc(self.sem, 1)
        self.n += 1
        if apart is None:
            self.eng.wait_ge(self.sem, self.base + self.n)
        else:
            wait_apart(self.eng, self.sem, self.base + self.n, apart)


def wait_apart(eng, sem, value, core):
    eng.wait_ge(sem, value)
    eng.memset(core.unused[:, :], 0.0)


def over_groups(eng, body):
    with eng.Fori(0, GROUPS - 1) as g:
        body(g, False)
    body(GROUPS - 1, True)


def over_pairs(eng, count, body):
    with eng.Fori(0, count // 2 - 1) as i:
        body(2 * i, 0, 0)
        body(2 * i + 1, 1, 0)
    body(count - 2, 0, 2)
    body(count - 1, 1, 1)


class Core:

    def __init__(self, nc, ctx, io):
        self.nc, self.ctx, self.io = nc, ctx, io
        sb = lambda name, shape, dt=F32: ctx.enter_context(nc.sbuf_tensor(name, shape, dt))
        self.X = sb("X", [P, TILES, D])
        self.ident = sb("ident", [P, P])
        self.eps = sb("eps", [P, 2])
        self.unused = sb("unused", [1, 1])
        self.zero = sb("zero", [P, CT * D])
        self.slots_x = nc.dram_tensor("slots_x", [SLOTS, D], F32).ap()
        self.slots_y = nc.dram_tensor("slots_y", [SLOTS, D], F32).ap()
        self.cleared = ctx.enter_context(nc.semaphore("cleared"))
        self.scores = [ctx.enter_context(nc.psum_tensor(f"banks{i}", [P, 1024], F32)) for i in range(2)]
        self.bank = [self.scores[i // 2][:, (i % 2) * 512:(i % 2 + 1) * 512] for i in range(4)]
        self.bank += [ctx.enter_context(nc.psum_tensor(f"bank{i}", [P, 512], F32))[:, :] for i in range(4, 8)]


    def semaphores(self, ctx, prefix):
        own = []

        def over():
            self.nc.clear_and_free_semaphores(own)
            self.nc.all_engine_barrier()

        def sem(name):
            own.append(self.nc.alloc_semaphore(f"{prefix}_{name}"))
            return own[-1]

        ctx.callback(over)
        return sem


class Norm:

    BANKS = (6, 7)

    def __init__(self, core, ctx, name, sem, src, scale=None, shift=None, keep_xt=True):
        nc = core.nc
        self.core, self.src, self.scale, self.shift, self.keep_xt = core, src, scale, shift, keep_xt
        sb = lambda n, shape, dt=F32: ctx.enter_context(nc.sbuf_tensor(f"{name}_{n}", shape, dt))
        self.stats = sb("ln_stats", [P, GT, 6])
        self.moments = sb("ln_moments", [P, GT, 2])
        self.std = sb("ln_std", [P, GT])
        self.rstd = sb("ln_rstd", [P, GT])
        self.xn = sb("xn", [P, GT, D])
        self.xg = sb("xg", [P, DK, GW])
        self.xt = sb("xt", [P, DK, TOKENS]) if keep_xt else None
        self.stats_done = sem("ln_stats_done")
        self.moments_done = sem("ln_moments_done")
        self.std_done = sem("ln_std_done")
        self.rstd_done = sem("ln_rstd_done")
        self.xn_done = sem("xn_done")
        self.turned = sem("xn_turned")
        self.xg_done = sem("xg_done")
        self.xt_done = sem("xt_done")

    def vector(self, dve, g, xn_free=None):
        for j in range(GT):
            dve.bn_stats(self.stats[:, j, :], self.src[:, GT * g + j, :]).then_inc(self.stats_done, 1)
        wait_apart(dve, self.stats_done, GT * g + GT, self.core)
        for j in range(GT):
            dve.bn_aggr(self.moments[:, j, :], self.stats[:, j, :]).then_inc(self.moments_done, 1)
        dve.wait_ge(self.std_done, g + 1)
        dve.reciprocal(self.rstd[:, :], self.std[:, :]).then_inc(self.rstd_done, 1)
        dve.wait_ge(self.rstd_done, g + 1)
        for s, v in xn_free or []:
            dve.wait_ge(s, v)
        for j in range(GT):
            last = dve.tensor_scalar(self.xn[:, j, :], self.src[:, GT * g + j, :], self.moments[:, j, 0:1],
                                     self.rstd[:, j:j + 1], ALU.subtract, ALU.mult)
        last.then_inc(self.xn_done, 1)

    def scalar_std(self, act, g):
        act.wait_ge(self.moments_done, GT * g + GT)
        act.activation(self.std[:, :], self.moments[:, :, 1], ACT.Sqrt,
                       bias=self.core.eps[:, 0:1]).then_inc(self.std_done, 1)

    def tensor(self, pe, g, banks_free=None):
        pe.wait_ge(self.xn_done, g + 1)
        for s, v in banks_free or []:
            pe.wait_ge(s, v)
        for k in range(DK):
            for j in range(GT):
                last = pe.transpose(self.core.bank[self.BANKS[k]][:, j * P:(j + 1) * P],
                                    self.xn[:, j, k * P:(k + 1) * P], self.core.ident[:, :])
        last.then_inc(self.turned, 1)

    def scalar_copies(self, act, g, xg_free=None):
        act.wait_ge(self.turned, g + 1)
        for s, v in xg_free or []:
            act.wait_ge(s, v)

        def copy(dst, k):
            if self.scale is None:
                return act.copy(dst, self.core.bank[self.BANKS[k]][:, :])
            return act.activation(dst, self.core.bank[self.BANKS[k]][:, :], ACT.Identity,
                                  bias=self.shift[:, k:k + 1], scale=self.scale[:, k:k + 1])

        for k in range(DK):
            last = copy(self.xg[:, k, :], k)
        last.then_inc(self.xg_done, 1)
        if self.keep_xt:
            for k in range(DK):
                last = copy(self.xt[:, k, bass.ds(GW * g, GW)], k)
            last.then_inc(self.xt_done, 1)

    def banks_read(self, g):
        return [(self.xt_done if self.keep_xt else self.xg_done, g + 1)]


def load_stage(core):
    nc, io = core.nc, core.io
    with ExitStack() as ctx:
        loaded = core.semaphores(ctx, "load")("loaded")
        block = ctx.enter_context(nc.Block())

        @block.sync
        def _(sp):
            x = io["x"].rearrange("(t p) d -> p t d", p=P)
            for q in range(4):
                sp.dma_start(core.X[:, 4 * q:4 * q + 4, :], x[:, 4 * q:4 * q + 4, :]).then_inc(loaded, 16)
            sp.dma_start(core.ident[:, :], io["ident"]).then_inc(loaded, 16)
            sp.wait_ge(loaded, 80)

        @block.vector
        def _(dve):
            dve.memset(core.zero[:, :], 0.0)
            dve.memset(core.eps[:, 0:1], LN_EPS)
            dve.memset(core.eps[:, 1:2], RMS_EPS)


def clear_slots(core, sp):
    view = core.slots_x.rearrange("(e p j) d -> e p (j d)", p=P, j=CT)
    with sp.Fori(0, E1) as e:
        sp.dma_start(view[bass.ds(e, 1), :, :].rearrange("a p n -> (a p) n"), core.zero[:, :]).then_inc(core.cleared, 16)


def store_stage(core):
    nc = core.nc
    with ExitStack() as ctx:
        stored = core.semaphores(ctx, "store")("stored")
        block = ctx.enter_context(nc.Block())

        @block.sync
        def _(sp):
            out = core.io["out"].rearrange("(t p) d -> p t d", p=P)
            for q in range(4):
                sp.dma_start(out[:, 4 * q:4 * q + 4, :], core.X[:, 4 * q:4 * q + 4, :]).then_inc(stored, 16)
            sp.wait_ge(stored, 64)


def small_moe_stage(core, name, clear=False):
    nc, io, X, B = core.nc, core.io, core.X, core.bank
    ROUTE = 10
    with ExitStack() as ctx:
        sb = lambda n, shape, dt=F32: ctx.enter_context(nc.sbuf_tensor(f"{name}_{n}", shape, dt))
        sem = core.semaphores(ctx, f"{name}")
        norm = Norm(core, ctx, name, sem, X)
        w_router = sb("w_router", [P, DK, E0])
        w_gate = sb("w_gate", [P, DK, E0, F0])
        w_up = sb("w_up", [P, DK, E0, F0])
        w_down = sb("w_down", [F0, E0, D])
        iota = sb("iota", [P, E0])
        score = sb("score", [P, GT, E0])
        best = sb("best", [P, GT, 8])
        best_at = sb("best_at", [P, GT, 8], U32)
        best_atf = sb("best_atf", [P, GT, 2])
        gap = sb("gap", [P, GT, 1])
        exp_gap = sb("exp_gap", [P, GT, 1])
        total = sb("total", [P, GT, 1])
        prob = sb("prob", [P, GT, 2])
        hot = sb("hot", [P, 2, GT, E0])
        weight = sb("weight", [P, GT, E0])
        silu = sb("silu", [F0, 2, GW])
        hidden = sb("hidden", [F0, 2, GW])

        weights_in = sem("weights_in")
        score_mm = sem("score_mm")
        score_read = sem("score_read")
        routing = sem("routing")
        exp_done = sem("exp_done")
        gate_up_mm = sem("gate_up_mm")
        silu_done = sem("silu_done")
        hidden_done = sem("hidden_done")
        down_mm = sem("down_mm")
        added = sem("added")

        block = ctx.enter_context(nc.Block())

        @block.sync
        def _(sp):
            for dst, src in ((w_router, "l0_router"), (w_gate, "l0_gate"), (w_up, "l0_up"),
                             (w_down, "l0_down"), (iota, "iota8")):
                sp.dma_start(dst[:], io[src]).then_inc(weights_in, 16)
            if clear:
                clear_slots(core, sp)

        @block.tensor
        def _(pe):
            def scores(g):
                pe.wait_ge(norm.xg_done, g + 1)
                for s, v in norm.banks_read(g):
                    pe.wait_ge(s, v)
                for j in range(GT):
                    for k in range(DK):
                        last = pe.matmul(B[6][:, j * E0:(j + 1) * E0], norm.xg[:, k, j * P:(j + 1) * P],
                                         w_router[:, k, :], start=(k == 0), stop=(k == DK - 1))
                last.then_inc(score_mm, 1)

            def gate_up(g, e):
                pe.wait_ge(hidden_done, E0 * g + e + 1)
                for w, b in ((w_gate, B[2 * (e % 2)]), (w_up, B[2 * (e % 2) + 1])):
                    for k in range(DK):
                        last = pe.matmul(b[0:F0, :], w[:, k, e, :], norm.xt[:, k, bass.ds(GW * g, GW)],
                                         start=(k == 0), stop=(k == DK - 1))
                last.then_inc(gate_up_mm, 1)

            def down(g, e):
                pe.wait_ge(hidden_done, E0 * g + e + 3)
                pe.wait_ge(added, E0 * g + e + 1)
                for j in range(GT):
                    last = pe.matmul(B[4 + j // 2][:, (j % 2) * D:(j % 2 + 1) * D],
                                     hidden[:, e % 2, j * P:(j + 1) * P], w_down[:, e, :], start=True, stop=True)
                last.then_inc(down_mm, 1)

            def group(g, last_group):
                scores(g)
                gate_up(g, 0)
                for e in range(E0):
                    if e + 1 < E0:
                        gate_up(g, e + 1)
                    down(g, e)
                if not last_group:
                    norm.tensor(pe, g + 1, [(score_read, g + 1)])

            norm.tensor(pe, 0)
            pe.wait_ge(weights_in, 80)
            over_groups(pe, group)

        @block.scalar
        def _(act):
            def group(g, last_group):
                act.wait_ge(routing, ROUTE * g + 4)
                act.activation(exp_gap[:, :, :], gap[:, :, :], ACT.Exp).then_inc(exp_done, 1)
                if not last_group:
                    norm.scalar_std(act, g + 1)
                for e in range(E0):
                    act.wait_ge(gate_up_mm, E0 * g + e + 1)
                    act.activation(silu[:, e % 2, :], B[2 * (e % 2)][0:F0, :], ACT.Silu).then_inc(silu_done, 1)
                if not last_group:
                    norm.scalar_copies(act, g + 1, [(score_mm, g + 1)])

            norm.scalar_std(act, 0)
            norm.scalar_copies(act, 0)
            over_groups(act, group)

        @block.vector
        def _(dve):
            def route(g):
                s = Steps(dve, routing, ROUTE * g)
                dve.wait_ge(score_mm, g + 1)
                dve.tensor_copy(score[:, :, :], B[6][:, 0:GT * E0].rearrange("p (j e) -> p j e", e=E0)
                                ).then_inc(score_read, 1)
                wait_apart(dve, score_read, g + 1, core)
                for j in range(GT):
                    last = dve.max(best[:, j, :], score[:, j, :])
                s.then(last, apart=core)
                for j in range(GT):
                    last = dve.max_index(best_at[:, j, :], best[:, j, :], score[:, j, :])
                s.then(last)
                s.then(dve.tensor_copy(best_atf[:, :, :], best_at[:, :, 0:2]))
                s.then(dve.tensor_tensor(gap[:, :, :], best[:, :, 1:2], best[:, :, 0:1], ALU.subtract))
                dve.wait_ge(exp_done, g + 1)
                s.then(dve.tensor_scalar(total[:, :, :], exp_gap[:, :, :], 1.0, 2.0, ALU.add, ALU.mult))
                s.then(dve.reciprocal(prob[:, :, 0:1], total[:, :, :]))
                s.then(dve.tensor_tensor(prob[:, :, 1:2], exp_gap[:, :, :], prob[:, :, 0:1], ALU.mult))
                for k in range(2):
                    last = dve.tensor_tensor(hot[:, k, :, :], iota[:, :].unsqueeze(1).to_broadcast([P, GT, E0]),
                                             best_atf[:, :, k:k + 1].to_broadcast([P, GT, E0]), ALU.is_equal)
                s.then(last)
                for k in range(2):
                    last = dve.tensor_tensor(hot[:, k, :, :], hot[:, k, :, :],
                                             prob[:, :, k:k + 1].to_broadcast([P, GT, E0]), ALU.mult)
                s.then(last)
                s.then(dve.tensor_tensor(weight[:, :, :], hot[:, 0, :, :], hot[:, 1, :, :], ALU.add))
                assert s.n == ROUTE

            def gated(g, e):
                dve.wait_ge(silu_done, E0 * g + e + 1)
                dve.tensor_tensor(hidden[:, e % 2, :], silu[:, e % 2, :], B[2 * (e % 2) + 1][0:F0, :],
                                  ALU.mult).then_inc(hidden_done, 1)

            def add(g, e):
                dve.wait_ge(down_mm, E0 * g + e + 1)
                dve.wait_ge(added, E0 * g + e + 1)
                for j in range(GT):
                    last = dve.scalar_tensor_tensor(X[:, GT * g + j, :], B[4 + j // 2][:, (j % 2) * D:(j % 2 + 1) * D],
                                                    weight[:, j, e:e + 1], X[:, GT * g + j, :], ALU.mult, ALU.add)
                last.then_inc(added, 1)

            def group(g, last_group):
                route(g)
                if not last_group:
                    norm.vector(dve, g + 1, [(norm.turned, g + 1)])
                gated(g, 0)
                for e in range(E0):
                    if e + 1 < E0:
                        gated(g, e + 1)
                    add(g, e)

            dve.sem_inc(hidden_done, 2)
            dve.sem_inc(added, 1)
            norm.vector(dve, 0)
            dve.wait_ge(weights_in, 80)
            over_groups(dve, group)


def ttt_stage(core):
    with ExitStack() as ctx:
        keys = ctx.enter_context(core.nc.sbuf_tensor("keys", [P, H0 // HG, TOKENS], F32))
        read = ctx.enter_context(core.nc.sbuf_tensor("read", [P, STEPS0, NBG, DH0], F32))
        v_dram = core.nc.dram_tensor("v_dram", [TOKENS, D], F32).ap()
        z_dram = core.nc.dram_tensor("z_dram", [TOKENS, D], F32).ap()
        ttt_project(core, keys, v_dram)
        ttt_scan(core, keys, read, v_dram, z_dram)
    ttt_output(core, z_dram)


def ttt_project(core, keys, v_dram):
    nc, io, B = core.nc, core.io, core.bank
    with ExitStack() as ctx:
        sb = lambda n, shape, dt=F32: ctx.enter_context(nc.sbuf_tensor(f"ttt_{n}", shape, dt))
        sem = core.semaphores(ctx, "ttt")
        norm = Norm(core, ctx, "ttt", sem, core.X)
        w_k = sb("w_k", [P, DK, D])
        w_k_rot = sb("w_k_rot", [P, DK, D])
        w_v = sb("w_v", [P, DK, D])
        cos = sb("cos", [P, TOKENS])
        sin = sb("sin", [P, TOKENS])
        turned_part = sb("turned_part", [P, 2, GW])
        values = sb("values", [P, GT, D])

        weights_in = sem("weights_in")
        keys_mm = sem("keys_mm")
        products = sem("products")
        keys_done = sem("keys_done")
        values_mm = sem("values_mm")
        values_read = sem("values_read")
        values_out = sem("values_out")
        block = ctx.enter_context(nc.Block())

        @block.sync
        def _(sp):
            for dst, src in ((w_k, "ttt_k"), (w_k_rot, "ttt_k_rot"), (w_v, "ttt_v"), (cos, "cos_a"), (sin, "sin_a")):
                sp.dma_start(dst[:], io[src]).then_inc(weights_in, 16)
            sp.sem_inc(values_out, 16)
            out = v_dram.rearrange("(t p) d -> p t d", p=P)
            with sp.Fori(0, GROUPS) as g:
                sp.wait_ge(values_read, g + 2)
                sp.dma_start(out[:, bass.ds(GT * g, GT), :], values[:, :, :]).then_inc(values_out, 16)
            sp.wait_ge(values_out, 16 * GROUPS + 16)

        @block.tensor
        def _(pe):
            def group(g, last_group):
                pe.wait_ge(norm.xt_done, g + 1)
                pe.wait_ge(products, g + 1)
                for w, b0 in ((w_k, 0), (w_k_rot, 2)):
                    for h in range(H0 // HG):
                        for k in range(DK):
                            last = pe.matmul(B[b0 + h][:, :], w[:, k, h * P:(h + 1) * P],
                                             norm.xt[:, k, bass.ds(GW * g, GW)], start=(k == 0), stop=(k == DK - 1))
                last.then_inc(keys_mm, 1)
                pe.wait_ge(values_read, g + 1)
                for j in range(GT):
                    for k in range(DK):
                        last = pe.matmul(B[4 + j // 2][:, (j % 2) * D:(j % 2 + 1) * D],
                                         norm.xg[:, k, j * P:(j + 1) * P], w_v[:, k, :],
                                         start=(k == 0), stop=(k == DK - 1))
                last.then_inc(values_mm, 1)
                if not last_group:
                    norm.tensor(pe, g + 1, norm.banks_read(g))

            norm.tensor(pe, 0)
            pe.wait_ge(weights_in, 80)
            over_groups(pe, group)

        @block.scalar
        def _(act):
            def group(g, last_group):
                if not last_group:
                    norm.scalar_std(act, g + 1)
                act.wait_ge(values_mm, g + 1)
                act.wait_ge(values_out, 16 * g + 16)
                for q in range(2):
                    last = act.copy(values[:, 2 * q:2 * q + 2, :],
                                    B[4 + q][:, :].rearrange("p (j d) -> p j d", d=D))
                last.then_inc(values_read, 1)
                if not last_group:
                    norm.scalar_copies(act, g + 1, [(values_mm, g + 1)])

            act.sem_inc(values_read, 1)
            norm.scalar_std(act, 0)
            norm.scalar_copies(act, 0)
            over_groups(act, group)

        @block.vector
        def _(dve):
            def group(g, last_group):
                if not last_group:
                    norm.vector(dve, g + 1, [(norm.turned, g + 1)])
                at = bass.ds(GW * g, GW)
                dve.wait_ge(keys_mm, g + 1)
                dve.wait_ge(keys_done, g + 1)
                for h in range(2):
                    dve.tensor_tensor(keys[:, h, at], B[h][:, :], cos[:, at], ALU.mult)
                    last = dve.tensor_tensor(turned_part[:, h, :], B[2 + h][:, :], sin[:, at], ALU.mult)
                last.then_inc(products, 1)
                dve.wait_ge(products, g + 2)
                dve.tensor_tensor(keys[:, :, at], keys[:, :, at], turned_part[:, :, :], ALU.add).then_inc(keys_done, 1)

            dve.sem_inc(products, 1)
            dve.sem_inc(keys_done, 1)
            norm.vector(dve, 0)
            dve.wait_ge(weights_in, 80)
            over_groups(dve, group)
            dve.wait_ge(keys_done, GROUPS + 1)


def ttt_scan(core, keys, read, v_dram, z_dram):
    nc, io, B = core.nc, core.io, core.bank
    with ExitStack() as ctx:
        sb = lambda n, shape, dt=F32: ctx.enter_context(nc.sbuf_tensor(f"scan_{n}", shape, dt))
        sem = core.semaphores(ctx, "scan")
        mask = sb("mask", [P, HG])
        k_fm = sb("k_fm", [P, 2, NBG, HG, MB])
        k_tm = sb("k_tm", [P, 2, NBG, P])
        state = sb("state", [P, NBG, DH0])
        error = sb("error", [P, NBG, DH0])

        loaded = sem("loaded")
        spread = sem("spread")
        turned = sem("turned")
        k_tm_done = sem("k_tm_done")
        z_mm = sem("z_mm")
        error_done = sem("error_done")
        change_mm = sem("change_mm")
        state_done = sem("state_done")
        stored = sem("stored")
        block = ctx.enter_context(nc.Block())

        def token_rows(dram, bg, h):
            view = dram.rearrange("(b t s) (g h e) -> g b h s t e", b=BATCH, s=MB, h=HG, e=DH0)
            return view[bg // BATCH, bg % BATCH, h]

        @block.sync
        def _(sp):
            sp.dma_start(mask[:, :], io["head_mask"]).then_inc(loaded, 16)
            sp.dma_start(state[:, :, :], io["w_start"].rearrange("p (b e) -> p b e", e=DH0)).then_inc(loaded, 16)
            for bg in range(NBG):
                for h in range(HG):
                    sp.dma_start(read[h * MB:(h + 1) * MB, :, bg, :], token_rows(v_dram, bg, h)).then_inc(loaded, 16)
            sp.wait_ge(state_done, STEPS0 + 1)
            for bg in range(NBG):
                for h in range(HG):
                    sp.dma_start(token_rows(z_dram, bg, h), read[h * MB:(h + 1) * MB, :, bg, :]).then_inc(stored, 16)
            sp.wait_ge(stored, 16 * NBG * HG)

        @block.vector
        def _(dve):
            kv = keys[:, :, :].rearrange("p h (b s) -> p (h b) s", b=BATCH)

            def spread_keys(t, par):
                src = kv[:, :, bass.ds(MB * t, MB)].unsqueeze(2).to_broadcast([P, NBG, HG, MB])
                m = mask[:, :].unsqueeze(1).unsqueeze(3).to_broadcast([P, NBG, HG, MB])
                dve.tensor_tensor(k_fm[:, par, :, :, :], src, m, ALU.mult).then_inc(spread, 1)

            def step(t, par, final):
                v = read[:, t, :, :]
                dve.wait_ge(z_mm, t + 1)
                z = B[0][:, 0:NBG * DH0].rearrange("p (b e) -> p b e", e=DH0)
                dve.tensor_tensor(error[:, :, :], z, v, ALU.subtract).then_inc(error_done, 1)
                if not final:
                    spread_keys(t + 2, par)
                dve.wait_ge(error_done, t + 1)
                dve.tensor_scalar(v, z, 1.0, None, ALU.mult)
                dve.wait_ge(change_mm, t + 1)
                dve.wait_ge(state_done, t + 1)
                dve.tensor_tensor(state[:, :, :], state[:, :, :],
                                  B[1][:, 0:NBG * DH0].rearrange("p (b e) -> p b e", e=DH0), ALU.add
                                  ).then_inc(state_done, 1)

            dve.wait_ge(loaded, 16 * (2 + NBG * HG))
            spread_keys(0, 0)
            spread_keys(1, 1)
            dve.sem_inc(state_done, 1)
            over_pairs(dve, STEPS0, step)

        @block.tensor
        def _(pe):
            def turn(t, par):
                pe.wait_ge(spread, t + 1)
                for bg in range(NBG):
                    last = pe.transpose(B[2 + par][:, bg * P:(bg + 1) * P],
                                        k_fm[:, par, bg, :, :].rearrange("p h s -> p (h s)"), core.ident[:, :])
                last.then_inc(turned, 1)

            def step(t, par, final):
                pe.wait_ge(state_done, t + 1)
                for bg in range(NBG):
                    last = pe.matmul(B[0][:, bg * DH0:(bg + 1) * DH0],
                                     k_fm[:, par, bg, :, :].rearrange("p h s -> p (h s)"), state[:, bg, :],
                                     start=True, stop=True)
                last.then_inc(z_mm, 1)
                if final != 1:
                    turn(t + 1, 1 - par)
                pe.wait_ge(k_tm_done, t + 1)
                pe.wait_ge(error_done, t + 1)
                for bg in range(NBG):
                    last = pe.matmul(B[1][:, bg * DH0:(bg + 1) * DH0], k_tm[:, par, bg, :], error[:, bg, :],
                                     start=True, stop=True)
                last.then_inc(change_mm, 1)

            turn(0, 0)
            over_pairs(pe, STEPS0, step)

        @block.scalar
        def _(act):
            def step(t, par, final):
                act.wait_ge(turned, t + 1)
                act.activation(k_tm[:, par, :, :], B[2 + par][:, :].rearrange("p (b k) -> p b k", k=P),
                               ACT.Copy, scale=-STEP_SCALE).then_inc(k_tm_done, 1)

            over_pairs(act, STEPS0, step)


def ttt_output(core, z_dram):
    nc, io, X, B = core.nc, core.io, core.X, core.bank
    with ExitStack() as ctx:
        sb = lambda n, shape, dt=F32: ctx.enter_context(nc.sbuf_tensor(f"tout_{n}", shape, dt))
        sem = core.semaphores(ctx, "tout")
        z = sb("z", [P, TILES, D])
        w_o = sb("w_o", [P, DK, D])
        gamma = sb("gamma", [P, DK])
        beta = sb("beta", [P, DK])
        norm = Norm(core, ctx, "tout", sem, z, scale=gamma, shift=beta, keep_xt=False)
        loaded = sem("loaded")
        out_mm = sem("out_mm")
        added = sem("added")
        block = ctx.enter_context(nc.Block())

        @block.sync
        def _(sp):
            sp.dma_start(z[:, :, :], z_dram.rearrange("(t p) d -> p t d", p=P)).then_inc(loaded, 16)
            for dst, src in ((w_o, "ttt_o"), (gamma, "ttt_gamma"), (beta, "ttt_beta")):
                sp.dma_start(dst[:], io[src]).then_inc(loaded, 16)

        @block.tensor
        def _(pe):
            def group(g, last_group):
                pe.wait_ge(norm.xg_done, g + 1)
                pe.wait_ge(added, g + 1)
                for j in range(GT):
                    for k in range(DK):
                        last = pe.matmul(B[j // 2][:, (j % 2) * D:(j % 2 + 1) * D],
                                         norm.xg[:, k, j * P:(j + 1) * P], w_o[:, k, :],
                                         start=(k == 0), stop=(k == DK - 1))
                last.then_inc(out_mm, 1)
                if not last_group:
                    norm.tensor(pe, g + 1, norm.banks_read(g))

            norm.tensor(pe, 0)
            pe.wait_ge(loaded, 64)
            over_groups(pe, group)

        @block.scalar
        def _(act):
            def group(g, last_group):
                if not last_group:
                    norm.scalar_std(act, g + 1)
                    norm.scalar_copies(act, g + 1, [(out_mm, g + 1)])

            norm.scalar_std(act, 0)
            act.wait_ge(loaded, 64)
            norm.scalar_copies(act, 0)
            over_groups(act, group)

        @block.vector
        def _(dve):
            def group(g, last_group):
                if not last_group:
                    norm.vector(dve, g + 1, [(norm.turned, g + 1)])
                dve.wait_ge(out_mm, g + 1)
                for q in range(2):
                    rows = X[:, bass.ds(GT * g + 2 * q, 2), :]
                    last = dve.tensor_tensor(rows, rows, B[q][:, :].rearrange("p (j d) -> p j d", d=D), ALU.add)
                last.then_inc(added, 1)

            dve.sem_inc(added, 1)
            dve.wait_ge(loaded, 64)
            norm.vector(dve, 0)
            over_groups(dve, group)


def big_moe_stage(core, name):
    nc = core.nc
    with ExitStack() as ctx:
        weight = ctx.enter_context(nc.sbuf_tensor(f"{name}_weight", [P, TILES, K1], F32))
        slot = ctx.enter_context(nc.sbuf_tensor(f"{name}_slot", [P, TILES, K1], U32))
        big_moe_route(core, name, weight, slot)
        big_moe_experts(core, name)
        big_moe_combine(core, name, weight, slot)


def big_moe_route(core, name, weight, slot):
    nc, io, X, B = core.nc, core.io, core.X, core.bank
    FIRST, SECOND = 14, 8
    ROUTE = FIRST + SECOND
    NOWHERE = 1.0e6
    NC = len(SHARED)
    with ExitStack() as ctx:
        sb = lambda n, shape, dt=F32: ctx.enter_context(nc.sbuf_tensor(f"{name}_r_{n}", shape, dt))
        sem = core.semaphores(ctx, f"{name}_r")
        norm = Norm(core, ctx, f"{name}_r", sem, X)
        w_router = sb("w_router", [P, DK, E1])
        w_gate = sb("w_gate", [P, DK, FS])
        w_up = sb("w_up", [P, DK, FS])
        w_down = sb("w_down", [P, NC, D])
        iota = sb("iota", [P, E1])
        earlier_f = sb("earlier_f", [P, P])
        earlier = sb("earlier", [P, P], BF16)
        ones = sb("ones", [P, P], BF16)
        score = sb("score", [P, GT, E1])
        top = sb("top", [P, GT, 1])
        total = sb("total", [P, GT, 1])
        inverse = sb("inverse", [P, GT, 1])
        best = sb("best", [P, GT, 8])
        best_at = sb("best_at", [P, GT, 8], U32)
        expert = sb("expert", [P, GT, K1])
        share = sb("share", [P, GT, K1])
        hot = sb("hot", [P, GT, K1, E1])
        taken = sb("taken", [P, GT, E1], BF16)
        before = sb("before", [P, E1])
        before_b = sb("before_b", [P, E1], BF16)
        group_sum = sb("group_sum", [P, E1])
        place = sb("place", [P, GT, K1])
        late = sb("late", [P, GT, K1])
        slot_f = sb("slot_f", [P, GT, K1])
        slot_now = sb("slot_now", [P, GT * K1], U32)
        silu = sb("silu", [P, 2, GW])
        hidden = sb("hidden", [P, NC, GW])

        weights_in = sem("weights_in")
        consts = sem("consts")
        score_mm = sem("score_mm")
        routing = sem("routing")
        exp_done = sem("exp_done")
        place_mm = sem("place_mm")
        slots_done = sem("slots_done")
        begun = sem("begun")
        scattered = sem("scattered")
        carried = sem("carried")
        gate_up_mm = sem("gate_up_mm")
        silu_done = sem("silu_done")
        hidden_done = sem("hidden_done")
        down_mm = sem("down_mm")
        added = sem("added")
        block = ctx.enter_context(nc.Block())

        @block.sync
        def _(sp):
            for dst, src in ((w_router, "l1_router"), (w_gate, "sh_gate"), (w_up, "sh_up"), (iota, "iota64"),
                             (earlier_f, "earlier")):
                sp.dma_start(dst[:], io[src]).then_inc(weights_in, 16)
            for c, (at, n) in enumerate(SHARED):
                sp.dma_start(w_down[0:n, c, :], io["sh_down"][at:at + n, :]).then_inc(weights_in, 16)

        @block.tensor
        def _(pe):
            def scores(g):
                pe.wait_ge(norm.xt_done, g + 1)
                for j in range(GT):
                    for k in range(DK):
                        last = pe.matmul(B[6][:, j * E1:(j + 1) * E1], norm.xg[:, k, j * P:(j + 1) * P],
                                         w_router[:, k, :], start=(k == 0), stop=(k == DK - 1))
                last.then_inc(score_mm, 1)

            def places(g):
                pe.wait_ge(routing, ROUTE * g + FIRST)
                pe.wait_ge(carried, 2 * g + 1)
                for j in range(GT):
                    out = B[7][:, j * E1:(j + 1) * E1]
                    pe.matmul(out, earlier[:, :], taken[:, j, :], start=True, stop=False)
                    for i in range(j):
                        pe.matmul(out, ones[:, :], taken[:, i, :], start=False, stop=False)
                    last = pe.matmul(out, ones[:, :], before_b[:, :], start=False, stop=True)
                last.then_inc(place_mm, 1)

            def gate_up(g, c):
                at, n = SHARED[c]
                pe.wait_ge(hidden_done, NC * g + (2 if c == 2 else 1))
                for w, b in ((w_gate, B[2 * (c % 2)]), (w_up, B[2 * (c % 2) + 1])):
                    for k in range(DK):
                        last = pe.matmul(b[0:n, :], w[:, k, at:at + n], norm.xt[:, k, bass.ds(GW * g, GW)],
                                         start=(k == 0), stop=(k == DK - 1))
                last.then_inc(gate_up_mm, 1)

            def down(g):
                pe.wait_ge(hidden_done, NC * g + NC + 1)
                pe.wait_ge(added, g + 1)
                for j in range(GT):
                    for c, (_, n) in enumerate(SHARED):
                        last = pe.matmul(B[4 + j // 2][:, (j % 2) * D:(j % 2 + 1) * D],
                                         hidden[0:n, c, j * P:(j + 1) * P], w_down[0:n, c, :],
                                         start=(c == 0), stop=(c == NC - 1))
                last.then_inc(down_mm, 1)

            def group(g, last_group):
                scores(g)
                gate_up(g, 0)
                gate_up(g, 1)
                places(g)
                gate_up(g, 2)
                down(g)
                if not last_group:
                    norm.tensor(pe, g + 1, [(slots_done, g + 1)])

            norm.tensor(pe, 0)
            pe.wait_ge(weights_in, 128)
            pe.wait_ge(consts, 2)
            over_groups(pe, group)

        @block.scalar
        def _(act):
            def group(g, last_group):
                act.wait_ge(routing, ROUTE * g + 3)
                act.activation(score[:, :, :], score[:, :, :], ACT.Exp).then_inc(exp_done, 1)
                for c, (_, n) in enumerate(SHARED):
                    act.wait_ge(gate_up_mm, NC * g + c + 1)
                    act.wait_ge(hidden_done, NC * g + (2 if c == 2 else 1))
                    act.activation(silu[0:n, c % 2, :], B[2 * (c % 2)][0:n, :], ACT.Silu).then_inc(silu_done, 1)
                if not last_group:
                    norm.scalar_std(act, g + 1)
                    norm.scalar_copies(act, g + 1, [(score_mm, g + 1)])

            norm.scalar_std(act, 0)
            norm.scalar_copies(act, 0)
            over_groups(act, group)

        @block.vector
        def _(dve):
            def route(g):
                s = Steps(dve, routing, ROUTE * g)
                dve.wait_ge(score_mm, g + 1)
                s.then(dve.tensor_copy(score[:, :, :], B[6][:, 0:GT * E1].rearrange("p (j e) -> p j e", e=E1)))
                s.then(dve.tensor_reduce(top[:, :, :], score[:, :, :], AX, ALU.max))
                s.then(dve.tensor_tensor(score[:, :, :], score[:, :, :], top[:, :, :].to_broadcast([P, GT, E1]),
                                         ALU.subtract))
                dve.wait_ge(exp_done, g + 1)
                s.then(dve.tensor_reduce(total[:, :, :], score[:, :, :], AX, ALU.add))
                s.then(dve.reciprocal(inverse[:, :, :], total[:, :, :]))
                s.then(dve.tensor_tensor(score[:, :, :], score[:, :, :], inverse[:, :, :].to_broadcast([P, GT, E1]),
                                         ALU.mult), apart=core)
                for j in range(GT):
                    last = dve.max(best[:, j, :], score[:, j, :])
                s.then(last, apart=core)
                for j in range(GT):
                    last = dve.max_index(best_at[:, j, :], best[:, j, :], score[:, j, :])
                s.then(last)
                s.then(dve.tensor_copy(expert[:, :, :], best_at[:, :, 0:K1]))
                s.then(dve.tensor_reduce(total[:, :, :], best[:, :, 0:K1], AX, ALU.add))
                s.then(dve.tensor_scalar(total[:, :, :], total[:, :, :], 1e-20, 2.0, ALU.add, ALU.mult))
                s.then(dve.reciprocal(inverse[:, :, :], total[:, :, :]))
                dve.tensor_tensor(share[:, :, :], best[:, :, 0:K1], inverse[:, :, :].to_broadcast([P, GT, K1]),
                                  ALU.mult)
                for j in range(GT):
                    last = dve.tensor_tensor(hot[:, j, :, :], iota[:, :].unsqueeze(1).to_broadcast([P, K1, E1]),
                                             expert[:, j, :].unsqueeze(2).to_broadcast([P, K1, E1]), ALU.is_equal)
                s.then(last)
                with nc.allow_low_precision("sums of ones"):
                    s.then(dve.tensor_reduce(taken[:, :, :], hot[:, :, :, :].rearrange("p j k e -> p j e k"),
                                             AX, ALU.add))
                assert s.n == FIRST
                dve.wait_ge(place_mm, g + 1)
                for j in range(GT):
                    at = B[7][:, j * E1:(j + 1) * E1].unsqueeze(1).to_broadcast([P, K1, E1])
                    last = dve.tensor_tensor(hot[:, j, :, :], hot[:, j, :, :], at, ALU.mult)
                s.then(last)
                s.then(dve.tensor_reduce(place[:, :, :], hot[:, :, :, :], AX, ALU.add))
                dve.scalar_tensor_tensor(slot_f[:, :, :], expert[:, :, :], float(CAP), place[:, :, :],
                                         ALU.mult, ALU.add)
                s.then(dve.tensor_scalar(late[:, :, :], place[:, :, :], float(CAP), None, ALU.is_ge))
                s.then(dve.scalar_tensor_tensor(slot_f[:, :, :], late[:, :, :], NOWHERE, slot_f[:, :, :],
                                                ALU.mult, ALU.add))
                s.then(dve.tensor_scalar(late[:, :, :], late[:, :, :], -1.0, 1.0, ALU.mult, ALU.add))
                s.then(dve.tensor_tensor(weight[:, bass.ds(GT * g, GT), :], share[:, :, :], late[:, :, :], ALU.mult))
                s.then(dve.tensor_copy(slot[:, bass.ds(GT * g, GT), :], slot_f[:, :, :]))
                s.then(dve.tensor_reduce(group_sum[:, :], taken[:, :, :].rearrange("p j e -> p e j"), AX, ALU.add))
                assert s.n == ROUTE
                dve.tensor_copy(slot_now[:, :].rearrange("p (j k) -> p j k", k=K1), slot_f[:, :, :]
                                ).then_inc(slots_done, 1)
                dve.tensor_tensor(before[:, :], before[:, :], group_sum[:, :], ALU.add).then_inc(carried, 1)
                dve.wait_ge(carried, 2 * g + 2)
                dve.tensor_copy(before_b[:, :], before[:, :]).then_inc(carried, 1)

            def group(g, last_group):
                route(g)
                dve.wait_ge(down_mm, g + 1)
                for c, (_, n) in enumerate(SHARED):
                    dve.wait_ge(silu_done, NC * g + c + 1)
                    dve.tensor_tensor(hidden[0:n, c, :], silu[0:n, c % 2, :], B[2 * (c % 2) + 1][0:n, :],
                                      ALU.mult).then_inc(hidden_done, 1)
                dve.wait_ge(down_mm, g + 2)
                for j in range(GT):
                    last = dve.scalar_tensor_tensor(X[:, GT * g + j, :], B[4 + j // 2][:, (j % 2) * D:(j % 2 + 1) * D],
                                                    0.5, X[:, GT * g + j, :], ALU.mult, ALU.add)
                last.then_inc(added, 1)
                if not last_group:
                    norm.vector(dve, g + 1, [(norm.turned, g + 1), (scattered, 16 * GT * K1 * (g + 1))])

            dve.sem_inc(hidden_done, 1)
            dve.sem_inc(added, 1)
            dve.sem_inc(down_mm, 1)
            norm.vector(dve, 0)
            dve.memset(ones[:, :], 1.0)
            dve.memset(before[:, :], 0.0)
            dve.memset(before_b[:, :], 0.0).then_inc(carried, 1)
            dve.wait_ge(weights_in, 128)
            dve.tensor_copy(earlier[:, :], earlier_f[:, :]).then_inc(consts, 1)
            dve.wait_ge(carried, 1)
            dve.sem_inc(consts, 1)
            over_groups(dve, group)
            dve.wait_ge(carried, 2 * GROUPS + 1)

        @block.gpsimd
        def _(pool):
            pool.wait_ge(core.cleared, 16 * E1)

            def group(g, last_group):
                pool.wait_ge(slots_done, g + 1)
                pool.sem_inc(begun, 1)
                for j in range(GT):
                    for k in range(K1):
                        at = slot_now[:, j * K1 + k:j * K1 + k + 1]
                        pool.indirect_dma_start(out=core.slots_x, out_offset=bass.IndirectOffsetOnAxis(ap=at, axis=0),
                                                in_=norm.xn[:, j, :], in_offset=None, bounds_check=SLOTS - 1,
                                                oob_is_err=False).then_inc(scattered, 16)

            over_groups(pool, group)
            pool.wait_ge(scattered, 16 * GT * K1 * GROUPS)


def big_moe_experts(core, name):
    nc, io, B = core.nc, core.io, core.bank
    with ExitStack() as ctx:
        sb = lambda n, shape, dt=F32: ctx.enter_context(nc.sbuf_tensor(f"{name}_e_{n}", shape, dt))
        sem = core.semaphores(ctx, f"{name}_e")
        x = [sb(f"x{i}", [P, CT, D]) for i in range(2)]
        w = [sb(f"w{i}", [P, DK, 2 * FA + FBM]) for i in range(2)]
        down_a = [sb(f"down_a{i}", [P, D]) for i in range(2)]
        down_b = [sb(f"down_b{i}", [FB, D]) for i in range(2)]
        xt = sb("xt", [P, 2, DK, CAP])
        silu_a = sb("silu_a", [P, CAP])
        silu_b = sb("silu_b", [FB, CAP])
        hidden_a = sb("hidden_a", [P, CAP])
        hidden_b = sb("hidden_b", [FB, CAP])
        y = [sb(f"y{i}", [P, CT, D]) for i in range(2)]

        loaded = [sem(f"loaded{i}") for i in range(2)]
        turned = sem("turned")
        xt_act = sem("xt_act")
        xt_dve = sem("xt_dve")
        a_mm = sem("a_mm")
        b_mm = sem("b_mm")
        silu_done = sem("silu_done")
        hidden_done = sem("hidden_done")
        down_mm = sem("down_mm")
        y_act = sem("y_act")
        y_dve = sem("y_dve")
        stored = [sem(f"stored{i}") for i in range(2)]
        block = ctx.enter_context(nc.Block())
        x_view = core.slots_x.rearrange("(e p j) d -> p e (j d)", p=P, j=CT)
        y_view = core.slots_y.rearrange("(e p j) d -> p e (j d)", p=P, j=CT)

        @block.sync
        def _(sp):
            def load(e, par, again):
                if again:
                    sp.wait_ge(down_mm, e + 1)
                flat = lambda t: t[:, :, :].rearrange("p a b -> p (a b)")
                sp.dma_start(flat(x[par]), x_view[:, e, :]).then_inc(loaded[par], 16)
                sp.dma_start(flat(w[par]), io["l1_gate_up"].rearrange("e p k f -> p e (k f)")[:, e, :]
                             ).then_inc(loaded[par], 16)
                rows = io["l1_down"].rearrange("e f d -> f e d")
                sp.dma_start(down_a[par][:, :], rows[0:FA, e, :]).then_inc(loaded[par], 16)
                sp.dma_start(down_b[par][:, :], rows[FA:F1, e, :]).then_inc(loaded[par], 16)

            def expert(e, par, left):
                sp.wait_ge(y_act, e + 2)
                sp.wait_ge(y_dve, e + 2)
                sp.dma_start(y_view[:, e, :], y[par][:, :, :].rearrange("p a b -> p (a b)")).then_inc(stored[par], 16)
                if not left:
                    load(e + 2, par, True)

            for par in range(2):
                sp.sem_inc(stored[par], 16)
                load(par, par, False)
            over_pairs(sp, E1, expert)
            for par in range(2):
                sp.wait_ge(stored[par], 16 * (E1 // 2) + 16)

        @block.tensor
        def _(pe):
            def turn(e, par, nth):
                pe.wait_ge(loaded[par], 64 * nth)
                for k in range(DK):
                    for j in range(CT):
                        last = pe.transpose(B[6 + k][:, j * P:(j + 1) * P], x[par][:, j, k * P:(k + 1) * P],
                                            core.ident[:, :])
                last.then_inc(turned, 1)

            def expert(e, par, left, nth):
                pe.wait_ge(xt_act, e + 1)
                pe.wait_ge(xt_dve, e + 1)
                pe.wait_ge(hidden_done, e + 1)
                for at, m, b, done in ((0, FA, B[0], None), (FA, FA, B[1], a_mm), (2 * FA, FBM, B[2], b_mm)):
                    for k in range(DK):
                        last = pe.matmul(b[0:m, 0:CAP], w[par][:, k, at:at + m], xt[:, par, k, :],
                                         start=(k == 0), stop=(k == DK - 1))
                    if done is not None:
                        last.then_inc(done, 1)
                if left != 1:
                    turn(e + 1, 1 - par, nth + 1 if par else nth)
                pe.wait_ge(hidden_done, e + 2)
                pe.wait_ge(y_act, e + 1)
                pe.wait_ge(y_dve, e + 1)
                for j in range(CT):
                    out = B[3 + j // 2][:, (j % 2) * D:(j % 2 + 1) * D]
                    pe.matmul(out, hidden_a[:, j * P:(j + 1) * P], down_a[par][:, :], start=True, stop=False)
                    last = pe.matmul(out, hidden_b[:, j * P:(j + 1) * P], down_b[par][:, :], start=False, stop=True)
                last.then_inc(down_mm, 1)

            pe.sem_inc(down_mm, 2)
            turn(0, 0, 1)
            with pe.Fori(0, E1 // 2 - 1) as i:
                expert(2 * i, 0, 0, i + 1)
                expert(2 * i + 1, 1, 0, i + 1)
            expert(E1 - 2, 0, 2, E1 // 2)
            expert(E1 - 1, 1, 1, E1 // 2)

        @block.scalar
        def _(act):
            def turn(e, par):
                act.wait_ge(turned, e + 1)
                act.copy(xt[:, par, 0, :], B[6][:, 0:CAP]).then_inc(xt_act, 1)

            def expert(e, par, left, nth):
                act.wait_ge(a_mm, e + 1)
                act.activation(silu_a[:, :], B[0][:, 0:CAP], ACT.Silu).then_inc(silu_done, 1)
                act.wait_ge(b_mm, e + 1)
                act.activation(silu_b[:, :], B[2][0:FB, 0:CAP], ACT.Silu).then_inc(silu_done, 1)
                if left != 1:
                    turn(e + 1, 1 - par)
                act.wait_ge(stored[par], 16 * nth)
                act.wait_ge(down_mm, e + 3)
                act.copy(y[par][:, 0:2, :], B[3][:, :].rearrange("p (j d) -> p j d", d=D)).then_inc(y_act, 1)

            act.sem_inc(y_act, 1)
            turn(0, 0)
            with act.Fori(0, E1 // 2 - 1) as i:
                expert(2 * i, 0, 0, i + 1)
                expert(2 * i + 1, 1, 0, i + 1)
            expert(E1 - 2, 0, 2, E1 // 2)
            expert(E1 - 1, 1, 1, E1 // 2)

        @block.vector
        def _(dve):
            def turn(e, par):
                dve.wait_ge(turned, e + 1)
                dve.tensor_copy(xt[:, par, 1, :], B[7][:, 0:CAP]).then_inc(xt_dve, 1)

            def expert(e, par, left, nth):
                dve.wait_ge(silu_done, 2 * e + 1)
                dve.tensor_tensor(hidden_a[:, :], silu_a[:, :], B[1][:, 0:CAP], ALU.mult)
                dve.wait_ge(silu_done, 2 * e + 2)
                dve.tensor_tensor(hidden_b[:, :], silu_b[:, :], B[2][UB:UB + FB, 0:CAP], ALU.mult
                                  ).then_inc(hidden_done, 1)
                if left != 1:
                    turn(e + 1, 1 - par)
                dve.wait_ge(stored[par], 16 * nth)
                dve.wait_ge(down_mm, e + 3)
                dve.tensor_copy(y[par][:, 2, :], B[4][:, 0:D]).then_inc(y_dve, 1)

            dve.sem_inc(y_dve, 1)
            dve.sem_inc(hidden_done, 1)
            turn(0, 0)
            with dve.Fori(0, E1 // 2 - 1) as i:
                expert(2 * i, 0, 0, i + 1)
                expert(2 * i + 1, 1, 0, i + 1)
            expert(E1 - 2, 0, 2, E1 // 2)
            expert(E1 - 1, 1, 1, E1 // 2)


def big_moe_combine(core, name, weight, slot):
    nc, X = core.nc, core.X
    with ExitStack() as ctx:
        sb = lambda n, shape, dt=F32: ctx.enter_context(nc.sbuf_tensor(f"{name}_c_{n}", shape, dt))
        sem = core.semaphores(ctx, f"{name}_c")
        at = [sb(f"at{i}", [P, K1], U32) for i in range(2)]
        rows = [sb(f"rows{i}", [P, K1, D]) for i in range(2)]
        begun = sem("begun")
        picked = sem("picked")
        gathered = [sem(f"gathered{i}") for i in range(2)]
        summed = sem("summed")
        block = ctx.enter_context(nc.Block())

        @block.gpsimd
        def _(pool):
            def tile(t, par, left, nth):
                pool.wait_ge(picked, t + 1)
                pool.sem_inc(begun, 1)
                for k in range(K1):
                    pool.indirect_dma_start(out=rows[par][:, k, :], out_offset=None, in_=core.slots_y,
                                            in_offset=bass.IndirectOffsetOnAxis(ap=at[par][:, k:k + 1], axis=0),
                                            bounds_check=SLOTS - 1, oob_is_err=False).then_inc(gathered[par], 16)

            with pool.Fori(0, TILES // 2) as i:
                tile(2 * i, 0, 0, i + 1)
                tile(2 * i + 1, 1, 0, i + 1)

        @block.vector
        def _(dve):
            def pick(t, par):
                dve.tensor_copy(at[par][:, :], slot[:, t, :]).then_inc(picked, 1)

            def tile(t, par, left, nth):
                dve.wait_ge(gathered[par], 16 * K1 * nth)
                for k in range(K1):
                    dve.wait_ge(summed, K1 * t + k + 1)
                    dve.scalar_tensor_tensor(X[:, t, :], rows[par][:, k, :], weight[:, t, k:k + 1], X[:, t, :],
                                             ALU.mult, ALU.add).then_inc(summed, 1)
                if not left:
                    dve.wait_ge(summed, K1 * t + K1 + 1)
                    pick(t + 2, par)

            dve.memset(rows[0][:, :, :], 0.0)
            dve.memset(rows[1][:, :, :], 0.0).then_inc(summed, 1)
            dve.wait_ge(summed, 1)
            pick(0, 0)
            pick(1, 1)
            with dve.Fori(0, TILES // 2 - 1) as i:
                tile(2 * i, 0, 0, i + 1)
                tile(2 * i + 1, 1, 0, i + 1)
            tile(TILES - 2, 0, 2, TILES // 2)
            tile(TILES - 1, 1, 1, TILES // 2)


def mla_stage(core):
    with ExitStack() as ctx:
        sb = lambda n, shape: ctx.enter_context(core.nc.sbuf_tensor(f"mla_{n}", shape, F32))
        latent = sb("latent", [P, TILES, RANK])
        keys = sb("keys", [P, TOKENS])
        q_latent = sb("q_latent", [P, TOKENS])
        q_weight = sb("q_weight", [RANK, NH, RANK + ROPE])
        q_swapped = sb("q_swapped", [RANK, NH, ROPE])
        o_weight = sb("o_weight", [P, NH // 2, D])
        mla_project(core, latent, keys, q_latent)
        mla_absorb(core, q_weight, q_swapped, o_weight)
        mla_attend(core, latent, keys, q_latent, q_weight, q_swapped, o_weight)


def mla_project(core, latent, keys, q_latent):
    nc, io, X, B = core.nc, core.io, core.X, core.bank
    W = 2 * RANK + ROPE
    CHAIN = 7
    with ExitStack() as ctx:
        sb = lambda n, shape, dt=F32: ctx.enter_context(nc.sbuf_tensor(f"mlap_{n}", shape, dt))
        sem = core.semaphores(ctx, "mlap")
        norm = Norm(core, ctx, "mlap", sem, X, keep_xt=False)
        w_a = sb("w_a", [P, DK, W])
        norm_w = sb("norm_w", [P, 2 * RANK])
        cos = sb("cos", [P, TILES, ROPE])
        sin = sb("sin", [P, TILES, ROPE])
        proj = sb("proj", [P, GT, W])
        square = sb("square", [P, GT, 2 * RANK])
        mean_sq = sb("mean_sq", [P, GT, 2])
        rms = sb("rms", [P, GT, 2])
        inverse = sb("inverse", [P, GT, 2])
        scaled = sb("scaled", [P, GT, 2 * RANK])
        q_n = sb("q_n", [P, GT, P])
        k_n = sb("k_n", [P, GT, RANK + ROPE])
        crossed = sb("crossed", [P, GT, ROPE])

        weights_in = sem("weights_in")
        proj_mm = sem("proj_mm")
        chain = sem("chain")
        rms_done = sem("rms_done")
        turned = sem("turned")
        copied = sem("copied")
        kept = sem("kept")
        block = ctx.enter_context(nc.Block())

        @block.sync
        def _(sp):
            for dst, src in ((w_a, "mla_a"), (norm_w, "mla_norms"), (cos, "cos_k"), (sin, "sin_k")):
                sp.dma_start(dst[:], io[src]).then_inc(weights_in, 16)

        @block.tensor
        def _(pe):
            def group(g, last_group):
                pe.wait_ge(norm.xg_done, g + 1)
                pe.wait_ge(chain, CHAIN * g + 1)
                for j in range(GT):
                    for k in range(DK):
                        last = pe.matmul(B[j // 2][:, (j % 2) * D:(j % 2) * D + W],
                                         norm.xg[:, k, j * P:(j + 1) * P], w_a[:, k, :],
                                         start=(k == 0), stop=(k == DK - 1))
                last.then_inc(proj_mm, 1)
                if not last_group:
                    norm.tensor(pe, g + 1, norm.banks_read(g))
                pe.wait_ge(chain, CHAIN * g + CHAIN + 1)
                pe.wait_ge(copied, g + 1)
                for j in range(GT):
                    pe.transpose(B[2][:, j * P:(j + 1) * P], q_n[:, j, :], core.ident[:, :])
                for j in range(GT):
                    last = pe.transpose(B[3][:, j * P:(j + 1) * P], k_n[:, j, :], core.ident[:, :])
                last.then_inc(turned, 1)

            pe.sem_inc(turned, 1)
            norm.tensor(pe, 0)
            pe.wait_ge(weights_in, 64)
            over_groups(pe, group)

        @block.scalar
        def _(act):
            def group(g, last_group):
                if not last_group:
                    norm.scalar_std(act, g + 1)
                    norm.scalar_copies(act, g + 1, [(proj_mm, g + 1)])
                act.wait_ge(chain, CHAIN * g + 4)
                act.activation(rms[:, :, :], mean_sq[:, :, :], ACT.Sqrt, bias=core.eps[:, 1:2],
                               scale=1.0 / RANK).then_inc(rms_done, 1)
                act.wait_ge(turned, g + 2)
                act.copy(q_latent[:, bass.ds(GW * g, GW)], B[2][:, :])
                act.copy(keys[:, bass.ds(GW * g, GW)], B[3][:, :]).then_inc(copied, 1)

            act.sem_inc(copied, 1)
            norm.scalar_std(act, 0)
            norm.scalar_copies(act, 0)
            over_groups(act, group)
            act.wait_ge(copied, GROUPS + 1)

        @block.gpsimd
        def _(pool):
            pool.sem_inc(kept, 1)
            with pool.Fori(0, GROUPS) as g:
                pool.wait_ge(chain, CHAIN * g + CHAIN + 1)
                pool.tensor_copy(latent[:, bass.ds(GT * g, GT), :], k_n[:, :, 0:RANK]).then_inc(kept, 1)
            pool.wait_ge(kept, GROUPS + 1)

        @block.vector
        def _(dve):
            def group(g, last_group):
                if not last_group:
                    norm.vector(dve, g + 1, [(norm.turned, g + 1)])
                s = Steps(dve, chain, CHAIN * g + 1)
                rows = bass.ds(GT * g, GT)
                dve.wait_ge(proj_mm, g + 1)
                for q in range(2):
                    last = dve.tensor_copy(proj[:, 2 * q:2 * q + 2, :],
                                           B[q][:, :].rearrange("p (j d) -> p j d", d=D)[:, :, 0:W])
                s.then(last)
                s.then(dve.tensor_tensor(square[:, :, :], proj[:, :, 0:2 * RANK], proj[:, :, 0:2 * RANK], ALU.mult))
                s.then(dve.tensor_reduce(mean_sq[:, :, :], square[:, :, :].rearrange("p j (n r) -> p j n r", r=RANK),
                                         AX, ALU.add))
                dve.wait_ge(turned, g + 1)
                dve.wait_ge(kept, g + 1)
                half = ROPE // 2
                pe_at = 2 * RANK
                dve.tensor_tensor(crossed[:, :, 0:half], proj[:, :, pe_at + half:pe_at + ROPE],
                                  sin[:, rows, 0:half], ALU.mult)
                dve.tensor_tensor(crossed[:, :, half:ROPE], proj[:, :, pe_at:pe_at + half],
                                  sin[:, rows, half:ROPE], ALU.mult)
                s.then(dve.tensor_tensor(k_n[:, :, RANK:], proj[:, :, pe_at:], cos[:, rows, :], ALU.mult))
                dve.tensor_tensor(k_n[:, :, RANK:], k_n[:, :, RANK:], crossed[:, :, :], ALU.add)
                dve.wait_ge(rms_done, g + 1)
                s.then(dve.reciprocal(inverse[:, :, :], rms[:, :, :]))
                s.then(dve.tensor_tensor(scaled[:, :, :].rearrange("p j (n r) -> p j n r", r=RANK),
                                         proj[:, :, 0:2 * RANK].rearrange("p j (n r) -> p j n r", r=RANK),
                                         inverse[:, :, :].unsqueeze(3).to_broadcast([P, GT, 2, RANK]), ALU.mult))
                wide = lambda w: w.unsqueeze(1).to_broadcast([P, GT, RANK])
                dve.tensor_tensor(q_n[:, :, 0:RANK], scaled[:, :, 0:RANK], wide(norm_w[:, 0:RANK]), ALU.mult)
                s.then(dve.tensor_tensor(k_n[:, :, 0:RANK], scaled[:, :, RANK:], wide(norm_w[:, RANK:]), ALU.mult))
                assert s.n == CHAIN

            dve.memset(q_n[:, :, :], 0.0).then_inc(chain, 1)
            norm.vector(dve, 0)
            dve.wait_ge(weights_in, 64)
            over_groups(dve, group)


def mla_absorb(core, q_weight, q_swapped, o_weight):
    nc, io, B = core.nc, core.io, core.bank
    with ExitStack() as ctx:
        sb = lambda n, shape, dt=F32: ctx.enter_context(nc.sbuf_tensor(f"mlab_{n}", shape, dt))
        sem = core.semaphores(ctx, "mlab")
        w_q = sb("w_q", [NOPE, NH, RANK])
        w_k = sb("w_k", [NOPE, NH, RANK])
        w_v = sb("w_v", [VD, NH, RANK])
        w_o = sb("w_o", [VD, NH, D])
        loaded = sem("loaded")
        q_mm = sem("q_mm")
        o_mm = sem("o_mm")
        block = ctx.enter_context(nc.Block())

        @block.sync
        def _(sp):
            for dst, src in ((w_q[:], "mla_q_nope"), (w_k[:], "mla_k"), (w_v[:], "mla_v"), (w_o[:], "mla_o"),
                             (q_weight[:, :, RANK:], "mla_q_pe"), (q_swapped[:], "mla_q_pe_swapped")):
                sp.dma_start(dst, io[src]).then_inc(loaded, 16)
            sp.wait_ge(loaded, 96)

        @block.tensor
        def _(pe):
            pe.wait_ge(loaded, 96)
            for h in range(NH):
                last = pe.matmul(B[h // 8][0:RANK, (h % 8) * RANK:(h % 8 + 1) * RANK], w_q[:, h, :], w_k[:, h, :],
                                 start=True, stop=True)
            last.then_inc(q_mm, 1)
            for h in range(NH):
                rows = slice(0, RANK) if h % 2 == 0 else slice(RANK, 2 * RANK)
                last = pe.matmul(B[2 + h // 4][rows, (h // 2 % 2) * D:(h // 2 % 2 + 1) * D], w_v[:, h, :], w_o[:, h, :],
                                 start=True, stop=True)
            last.then_inc(o_mm, 1)

        @block.vector
        def _(dve):
            dve.wait_ge(q_mm, 1)
            for q in range(2):
                dve.tensor_copy(q_weight[:, 8 * q:8 * q + 8, 0:RANK],
                                B[q][0:RANK, :].rearrange("r (h c) -> r h c", c=RANK))

        @block.scalar
        def _(act):
            act.wait_ge(o_mm, 1)
            for q in range(4):
                act.copy(o_weight[:, 2 * q:2 * q + 2, :], B[2 + q][:, :].rearrange("p (h d) -> p h d", d=D))


def mla_attend(core, latent, keys, q_latent, q_weight, q_swapped, o_weight):
    nc, io, X, B = core.nc, core.io, core.X, core.bank
    UB_ = GT * NH
    NKT = SEQ // P
    with ExitStack() as ctx:
        sb = lambda n, shape, dt=F32: ctx.enter_context(nc.sbuf_tensor(f"att_{n}", shape, dt))
        sem = core.semaphores(ctx, "att")
        cos = sb("cos", [P, SEQ])
        sin = sb("sin", [P, SEQ])
        q_w = [sb(f"q_w{i}", [P, RANK + ROPE]) for i in range(2)]
        q_s = [sb(f"q_s{i}", [P, RANK + ROPE]) for i in range(2)]
        crossed = sb("crossed", [P, GW])
        query = [sb(f"query{i}", [P, GW]) for i in range(2)]
        top = sb("top", [P, 2])
        bias = sb("bias", [P, 2])
        total = sb("total", [P, 2])
        inverse = sb("inverse", [P, 2])
        probs = [sb(f"probs{i}", [P, SEQ]) for i in range(2)]
        turned_probs = sb("turned_probs", [P, NKT, P])
        heads = sb("heads", [P, GT, NH * RANK])

        loaded = sem("loaded")
        zeroed = sem("zeroed")
        q_w_done = sem("q_w_done")
        cross_mm = sem("cross_mm")
        cross_done = sem("cross_done")
        query_mm = sem("query_mm")
        query_part = sem("query_part")
        query_done = sem("query_done")
        score_mm = sem("score_mm")
        top_done = sem("top_done")
        bias_done = sem("bias_done")
        exp_done = sem("exp_done")
        turned = sem("turned")
        turn_act = sem("turn_act")
        turn_dve = sem("turn_dve")
        average_mm = sem("average_mm")
        inverse_done = sem("inverse_done")
        heads_done = sem("heads_done")
        out_turned = sem("out_turned")
        out_act = sem("out_act")
        out_dve = sem("out_dve")
        out_mm = sem("out_mm")
        added = sem("added")
        block = ctx.enter_context(nc.Block())

        def over_blocks(eng, body):
            with eng.Fori(0, BATCH) as b:
                with eng.Fori(0, 2) as half:
                    body(2 * b + half, b, half)

        def over_heads(eng, n, body):
            with eng.Fori(0, NH // 2 - 1) as i:
                body(2 * i, NH * n + 2 * i, 0, False)
                body(2 * i + 1, NH * n + 2 * i + 1, 1, False)
            body(NH - 2, NH * n + NH - 2, 0, False)
            body(NH - 1, NH * n + NH - 1, 1, True)

        @block.sync
        def _(sp):
            sp.dma_start(cos[:, :], io["cos_q"]).then_inc(loaded, 16)
            sp.dma_start(sin[:, :], io["sin_q"]).then_inc(loaded, 16)

        @block.gpsimd
        def _(pool):
            for buffer in (*q_w, *q_s):
                last = pool.memset(buffer[:, :], 0.0)
            last.then_inc(zeroed, 1)
            pool.wait_ge(zeroed, 1)
            with pool.Fori(0, BATCH * 2) as n:
                def head(h, hh, par):
                    pool.wait_ge(query_mm, hh + 1)
                    pool.tensor_copy(q_w[par][0:RANK, :], q_weight[:, h, :])
                    pool.tensor_copy(q_s[par][0:RANK, RANK:], q_swapped[:, h, :]).then_inc(q_w_done, 1)

                with pool.Fori(0, NH // 2) as i:
                    head(2 * i, NH * n + 2 * i, 0)
                    head(2 * i + 1, NH * n + 2 * i + 1, 1)

        @block.tensor
        def _(pe):
            def cross(n, hh, par):
                pe.wait_ge(q_w_done, hh + 1)
                pe.wait_ge(query_done, hh + 1)
                pe.matmul(B[7][:, :], q_s[par][:, :], q_latent[:, bass.ds(GW * n, GW)],
                          start=True, stop=True).then_inc(cross_mm, 1)

            def project(n, hh, par):
                pe.wait_ge(cross_done, hh + 1)
                pe.matmul(B[7][:, :], q_w[par][:, :], q_latent[:, bass.ds(GW * n, GW)],
                          start=True, stop=True).then_inc(query_mm, 1)

            def scores(b, hh, par, j):
                u = GT * hh + j
                pe.wait_ge(query_done, hh + 2)
                pe.wait_ge(exp_done, u + 1)
                for c in range(2):
                    last = pe.matmul(B[2 * (j % 2) + c][:, :], query[par][:, j * P:(j + 1) * P],
                                     keys[:, bass.ds(SEQ * b + 512 * c, 512)], start=True, stop=True)
                last.then_inc(score_mm, 1)

            def turn(hh, j):
                u = GT * hh + j
                pe.wait_ge(exp_done, u + 3)
                pe.wait_ge(turn_act, u + 1)
                pe.wait_ge(turn_dve, u + 1)
                for c in range(NKT):
                    last = pe.transpose(B[4 + c // 4][:, (c % 4) * P:(c % 4 + 1) * P],
                                        probs[j % 2][:, c * P:(c + 1) * P], core.ident[:, :])
                last.then_inc(turned, 1)

            def average(b, hh, j):
                u = GT * hh + j
                pe.wait_ge(turn_act, u + 2)
                pe.wait_ge(turn_dve, u + 2)
                pe.wait_ge(heads_done, u + 1)
                for c in range(NKT):
                    last = pe.matmul(B[6][:, 0:RANK], turned_probs[:, c, :], latent[:, NKT * b + c, :],
                                     start=(c == 0), stop=(c == NKT - 1))
                last.then_inc(average_mm, 1)

            def block_of_queries(n, b, half):
                cross(n, NH * n, 0)
                project(n, NH * n, 0)
                scores(b, NH * n, 0, 0)
                scores(b, NH * n, 0, 1)

                def head(h, hh, par, last_head):
                    for j in range(GT):
                        turn(hh, j)
                        if j < 2:
                            scores(b, hh, par, j + 2)
                        elif not last_head:
                            scores(b, hh + 1, 1 - par, j - 2)
                        average(b, hh, j)
                        if j == 0 and not last_head:
                            cross(n, hh + 1, 1 - par)
                        if j == 1 and not last_head:
                            project(n, hh + 1, 1 - par)

                over_heads(pe, n, head)
                pe.wait_ge(heads_done, UB_ * n + UB_ + 1)
                for j in range(GT):
                    t = GT * n + j
                    pe.wait_ge(added, t + 1)
                    for c in range(NKT):
                        last = pe.transpose(B[4 + c // 4][:, (c % 4) * P:(c % 4 + 1) * P],
                                            heads[:, j, c * P:(c + 1) * P], core.ident[:, :])
                    last.then_inc(out_turned, 1)
                    pe.wait_ge(out_act, t + 1)
                    pe.wait_ge(out_dve, t + 1)
                    for c in range(NH // 2):
                        last = pe.matmul(B[6][:, 0:D], turned_probs[:, c, :], o_weight[:, c, :],
                                         start=(c == 0), stop=(c == NH // 2 - 1))
                    last.then_inc(out_mm, 1)
                pe.wait_ge(added, GT * n + GT + 1)

            pe.sem_inc(query_mm, 2)
            over_blocks(pe, block_of_queries)

        @block.scalar
        def _(act):
            def exps(hh, j):
                u = GT * hh + j
                act.wait_ge(bias_done, u + 1)
                act.activation(probs[j % 2][:, :], core.scores[j % 2][:, :], ACT.Exp, bias=bias[:, j % 2:j % 2 + 1],
                               scale=SM_SCALE, accum_out=total[:, j % 2:j % 2 + 1]).then_inc(exp_done, 1)

            def copy_turned(hh, j):
                u = GT * hh + j
                act.wait_ge(turned, u + 1)
                act.copy(turned_probs[:, 0:4, :], B[4][:, :].rearrange("p (c k) -> p c k", k=P)).then_inc(turn_act, 1)

            def block_of_queries(n, b, half):
                exps(NH * n, 0)
                exps(NH * n, 1)

                def head(h, hh, par, last_head):
                    for j in range(GT):
                        copy_turned(hh, j)
                        if j < 2:
                            exps(hh, j + 2)
                        elif not last_head:
                            exps(hh + 1, j - 2)

                over_heads(act, n, head)
                for j in range(GT):
                    act.wait_ge(out_turned, GT * n + j + 1)
                    act.copy(turned_probs[:, 0:4, :], B[4][:, :].rearrange("p (c k) -> p c k", k=P)).then_inc(out_act, 1)

            act.sem_inc(exp_done, 2)
            act.sem_inc(turn_act, 1)
            over_blocks(act, block_of_queries)

        @block.vector
        def _(dve):
            def cross(half, hh):
                dve.wait_ge(cross_mm, hh + 1)
                dve.tensor_tensor(crossed[RANK:P, :], B[7][RANK:P, :], sin[RANK:P, bass.ds(GW * half, GW)],
                                  ALU.mult).then_inc(cross_done, 1)

            def rotate(half, hh, par):
                dve.wait_ge(query_mm, hh + 3)
                dve.tensor_copy(query[par][0:RANK, :], B[7][0:RANK, :])
                dve.tensor_tensor(query[par][RANK:P, :], B[7][RANK:P, :], cos[RANK:P, bass.ds(GW * half, GW)],
                                  ALU.mult).then_inc(query_part, 1)
                dve.wait_ge(query_part, hh + 1)
                dve.tensor_tensor(query[par][RANK:P, :], query[par][RANK:P, :], crossed[RANK:P, :],
                                  ALU.add).then_inc(query_done, 1)

            def maxima(hh, j):
                u = GT * hh + j
                dve.wait_ge(score_mm, u + 1)
                dve.tensor_reduce(top[:, j % 2:j % 2 + 1], core.scores[j % 2][:, :], AX, ALU.max).then_inc(top_done, 1)
                dve.wait_ge(top_done, u + 1)
                dve.tensor_scalar(bias[:, j % 2:j % 2 + 1], top[:, j % 2:j % 2 + 1], -SM_SCALE, None,
                                  ALU.mult).then_inc(bias_done, 1)

            def block_of_queries(n, b, half):
                cross(half, NH * n)
                rotate(half, NH * n, 0)
                maxima(NH * n, 0)
                maxima(NH * n, 1)

                def head(h, hh, par, last_head):
                    for j in range(GT):
                        u = GT * hh + j
                        dve.wait_ge(turned, u + 1)
                        dve.tensor_copy(turned_probs[:, 4:8, :], B[5][:, :].rearrange("p (c k) -> p c k", k=P)
                                        ).then_inc(turn_dve, 1)
                        dve.reciprocal(inverse[:, j % 2:j % 2 + 1], total[:, j % 2:j % 2 + 1]).then_inc(inverse_done, 1)
                        if j < 2:
                            maxima(hh, j + 2)
                        elif not last_head:
                            maxima(hh + 1, j - 2)
                        dve.wait_ge(average_mm, u + 1)
                        dve.wait_ge(inverse_done, u + 1)
                        dve.tensor_scalar(heads[:, j, bass.ds(RANK * h, RANK)], B[6][:, 0:RANK],
                                          inverse[:, j % 2:j % 2 + 1], None, ALU.mult).then_inc(heads_done, 1)
                        if j == 0 and not last_head:
                            cross(half, hh + 1)
                        if j == 1 and not last_head:
                            rotate(half, hh + 1, 1 - par)

                over_heads(dve, n, head)
                for j in range(GT):
                    t = GT * n + j
                    dve.wait_ge(out_turned, t + 1)
                    dve.tensor_copy(turned_probs[:, 4:8, :], B[5][:, :].rearrange("p (c k) -> p c k", k=P)
                                    ).then_inc(out_dve, 1)
                    dve.wait_ge(out_mm, t + 1)
                    dve.tensor_tensor(X[:, t, :], X[:, t, :], B[6][:, 0:D], ALU.add).then_inc(added, 1)

            dve.sem_inc(query_done, 1)
            dve.sem_inc(turn_dve, 1)
            dve.sem_inc(heads_done, 1)
            dve.sem_inc(added, 1)
            dve.wait_ge(loaded, 32)
            over_blocks(dve, block_of_queries)


STAGES = [lambda c: small_moe_stage(c, "ffn_a", clear=True), ttt_stage, lambda c: small_moe_stage(c, "ffn_b"),
          lambda c: big_moe_stage(c, "moe_a"), mla_stage, lambda c: big_moe_stage(c, "moe_b")]


def macaron(nc, io):
    with ExitStack() as ctx:
        core = Core(nc, ctx, io)
        load_stage(core)
        for stage in STAGES:
            stage(core)
        store_stage(core)


def rope_tables():
    t = np.arange(SEQ, dtype=np.float32)
    inv = (1.0 / np.float32(10000.0) ** (np.arange(0, DH0, 2, dtype=np.float32) / np.float32(DH0))).astype(np.float32)
    freqs = (t[:, None] * inv[None, :]).astype(np.float32)
    cos0, sin0 = np.cos(freqs), np.sin(freqs)
    two = lambda a, b: np.concatenate([a, b], axis=1)
    cos_a = np.tile(two(cos0, cos0).T, (HG, BATCH))
    sin_a = np.tile(two(-sin0, sin0).T, (HG, BATCH))
    dim, factor, orig = ROPE, 40.0, 512
    ex = np.arange(0, dim, 2, dtype=np.float64) / dim
    extra, inter = 1.0 / 10000.0 ** ex, 1.0 / (factor * 10000.0 ** ex)
    corr = lambda rot: dim * np.log(orig / (rot * 2 * np.pi)) / (2 * np.log(10000.0))
    low, high = max(np.floor(corr(32.0)), 0), min(np.ceil(corr(1.0)), dim - 1)
    ramp = np.clip((np.arange(dim // 2) - low) / (high - low if high != low else 0.001), 0.0, 1.0)
    inv = inter * ramp + extra * (1.0 - ramp)
    fr = np.outer(np.arange(SEQ, dtype=np.float64), inv)
    msc = (0.1 * 0.707 * np.log(factor) + 1.0) / 1.0
    cos1, sin1 = (np.cos(fr) * msc).astype(np.float32), (np.sin(fr) * msc).astype(np.float32)
    tok = lambda a: a.reshape(KT_TILES, P, -1).transpose(1, 0, 2)
    return {
        "cos_a": cos_a, "sin_a": sin_a,
        "cos_q": np.tile(two(cos1, cos1).T, (2, 1)), "sin_q": np.tile(two(-sin1, sin1).T, (2, 1)),
        "cos_k": np.tile(tok(two(cos1, cos1)), (1, BATCH, 1)), "sin_k": np.tile(tok(two(-sin1, sin1)), (1, BATCH, 1)),
    }


def laid_out(i):
    rows = lambda w: w.reshape(DK, P, *w.shape[1:]).swapaxes(0, 1)
    half = DH0 // 2
    k_w = i["L0_attn_Wk"].reshape(H0, DH0, D)
    k_rot = np.concatenate([k_w[:, half:], k_w[:, :half]], axis=1).reshape(D, D)
    a = {
        "x": i["L0_attn_x"].reshape(TOKENS, D),
        "l0_router": rows(i["L0_ffn_w_gate_router"].T),
        "l0_gate": rows(i["L0_ffn_w_gate_proj"].transpose(2, 0, 1)),
        "l0_up": rows(i["L0_ffn_w_up_proj"].transpose(2, 0, 1)),
        "l0_down": i["L0_ffn_w_down_proj"].transpose(2, 0, 1),
        "ttt_k": rows(i["L0_attn_Wk"].T), "ttt_k_rot": rows(k_rot.T), "ttt_v": rows(i["L0_attn_Wv"].T),
        "ttt_o": rows(i["L0_attn_Wo"].T),
        "ttt_gamma": i["L0_attn_ln_gamma"].reshape(DK, P).T, "ttt_beta": i["L0_attn_ln_beta"].reshape(DK, P).T,
    }
    gate, up = i["L1_ffn_w_gate"].transpose(0, 2, 1), i["L1_ffn_w_up"].transpose(0, 2, 1)
    gap = np.zeros((E1, D, UB - FB), np.float32)
    packed = np.concatenate([gate[:, :, :FA], up[:, :, :FA], gate[:, :, FA:], gap, up[:, :, FA:]], axis=2)
    a["l1_gate_up"] = packed.reshape(E1, DK, P, 2 * FA + FBM).transpose(0, 2, 1, 3)
    a["l1_down"] = i["L1_ffn_w_down"].transpose(0, 2, 1)
    a["l1_router"] = rows(i["L1_ffn_gate_w"].T)
    a["sh_gate"] = rows(i["L1_ffn_sh_gate"].T)
    a["sh_up"] = rows(i["L1_ffn_sh_up"].T)
    a["sh_down"] = i["L1_ffn_sh_down"].T
    apart = np.concatenate([np.arange(0, ROPE, 2), np.arange(1, ROPE, 2)])
    swapped = np.roll(apart, ROPE // 2)
    wkv = i["L1_attn_wkv_a"]
    a["mla_a"] = rows(np.concatenate([i["L1_attn_wq_a"], wkv[:, :RANK], wkv[:, RANK:][:, apart]], axis=1))
    a["mla_norms"] = np.tile(np.concatenate([i["L1_attn_q_a_norm_w"], i["L1_attn_kv_a_norm_w"]])[None], (P, 1))
    wq = i["L1_attn_wq_b"].reshape(RANK, NH, NOPE + ROPE)
    kv = i["L1_attn_wkv_b"].reshape(RANK, NH, NOPE + VD)
    a["mla_q_nope"] = wq[:, :, :NOPE].transpose(2, 1, 0)
    a["mla_q_pe"] = wq[:, :, NOPE:][:, :, apart]
    a["mla_q_pe_swapped"] = wq[:, :, NOPE:][:, :, swapped]
    a["mla_k"] = kv[:, :, :NOPE].transpose(2, 1, 0)
    a["mla_v"] = kv[:, :, NOPE:].transpose(2, 1, 0)
    a["mla_o"] = i["L1_attn_wo"].reshape(NH, VD, D).transpose(1, 0, 2)
    a.update(rope_tables())
    a["ident"] = np.eye(P, dtype=np.float32)
    a["iota8"] = np.tile(np.arange(E0, dtype=np.float32), (P, 1))
    a["iota64"] = np.tile(np.arange(E1, dtype=np.float32), (P, 1))
    a["earlier"] = np.triu(np.ones((P, P), np.float32), 1)
    a["head_mask"] = np.kron(np.eye(HG, dtype=np.float32), np.ones((DH0, 1), np.float32))
    a["w_start"] = np.tile(np.eye(DH0, dtype=np.float32), (HG, NBG))
    return a


def kernel(**inputs):
    import concourse.bacc as bacc
    from concourse.bass_utils import run_bass_kernel_spmd

    nc = bacc.Bacc("TRN2", target_bir_lowering=False, num_devices=1)
    arrays = {f"in_{n}": np.ascontiguousarray(a) for n, a in laid_out({k: np.asarray(v) for k, v in inputs.items()}).items()}
    io = {n.removeprefix("in_"): nc.dram_tensor(n, a.shape, mybir.dt.from_np(a.dtype), kind="ExternalInput").ap()
          for n, a in arrays.items()}
    io["out"] = nc.dram_tensor("out", (TOKENS, D), F32, kind="ExternalOutput").ap()
    macaron(nc, io)
    r = run_bass_kernel_spmd(nc, [arrays], core_ids=[0])
    return r.results[0]["out"].reshape(BATCH, SEQ, D)
```

```python
from contextlib import ExitStack

import concourse.bass as bass
import numpy as np
from concourse import mybir
from concourse.alu_op_type import AluOpType as ALU

F32 = mybir.dt.float32
F32R = mybir.dt.float32r
BF16 = mybir.dt.bfloat16
U32 = mybir.dt.uint32
ACT = mybir.ActivationFunctionType
AX = mybir.AxisListType.X

P = 128
BATCH, SEQ, D = 2, 1024, 256
TOKENS = BATCH * SEQ
TILES = TOKENS // P
DK = D // P
GT = 4
GROUPS = TILES // GT
GW = GT * P
LN_EPS = 1e-5
RMS_EPS = 1e-6

E0, F0 = 8, 96
C0 = E0 * F0 // P
H0, DH0, MB = 16, 16, 16
STEPS0 = SEQ // MB
HG = 8
NBG = BATCH * (H0 // HG)
STEP_SCALE = 2.0 / (MB * DH0)
E1, F1, K1, FS = 64, 176, 6, 352
CAP = 2 * ((TOKENS * K1 + E1 - 1) // E1)
CT = CAP // P
FA, FB = P, F1 - P
UB = 64
FBM = UB + FB
SLOTS = E1 * CAP
SHARED = [(0, 128), (128, 128), (256, 96)]
NH, NOPE, ROPE, RANK, VD = 16, 64, 64, 64, 64
SM_SCALE = (NOPE + ROPE) ** -0.5
KT_TILES = SEQ // P


class Steps:

    def __init__(self, eng, sem, base=0):
        self.eng, self.sem, self.base, self.n = eng, sem, base, 0

    def then(self, ins, apart=None):
        ins.then_inc(self.sem, 1)
        self.n += 1
        if apart is None:
            self.eng.wait_ge(self.sem, self.base + self.n)
        else:
            wait_apart(self.eng, self.sem, self.base + self.n, apart)


def wait_apart(eng, sem, value, core):
    eng.wait_ge(sem, value)
    eng.memset(core.unused[:, :], 0.0)


def over_groups(eng, body):
    with eng.Fori(0, GROUPS - 1) as g:
        body(g, False)
    body(GROUPS - 1, True)


def over_buffered_groups(eng, body):
    body(0, 0, 1, False)
    with eng.Fori(0, GROUPS // 2 - 1) as i:
        body(2 * i + 1, 1, i + 1, False)
        body(2 * i + 2, 0, i + 2, False)
    body(GROUPS - 1, 1, GROUPS // 2, True)


def previous(par, nth):
    return nth if par else nth - 1


def following(par, nth):
    return nth + 1 if par else nth


def over_pairs(eng, count, body):
    with eng.Fori(0, count // 2 - 1) as i:
        body(2 * i, 0, 0)
        body(2 * i + 1, 1, 0)
    body(count - 2, 0, 2)
    body(count - 1, 1, 1)


class Core:

    def __init__(self, nc, ctx, io):
        self.nc, self.ctx, self.io = nc, ctx, io
        sb = lambda name, shape, dt=F32: ctx.enter_context(nc.sbuf_tensor(name, shape, dt))
        self.X = sb("X", [P, TILES, D])
        self.ident = sb("ident", [P, P])
        self.eps = sb("eps", [P, 2])
        self.unused = sb("unused", [1, 1])
        self.zero = sb("zero", [P, CT * D])
        self.slots_x = nc.dram_tensor("slots_x", [SLOTS, D], F32).ap()
        self.slots_y = nc.dram_tensor("slots_y", [SLOTS, D], F32).ap()
        self.cleared = ctx.enter_context(nc.semaphore("cleared"))
        self.scores = [ctx.enter_context(nc.psum_tensor(f"banks{i}", [P, 1024], F32)) for i in range(2)]
        self.bank = [self.scores[i // 2][:, (i % 2) * 512:(i % 2 + 1) * 512] for i in range(4)]
        self.bank += [ctx.enter_context(nc.psum_tensor(f"bank{i}", [P, 512], F32))[:, :] for i in range(4, 8)]


    def semaphores(self, ctx, prefix):
        own = []

        def over():
            self.nc.clear_and_free_semaphores(own)
            self.nc.all_engine_barrier()

        def sem(name):
            own.append(self.nc.alloc_semaphore(f"{prefix}_{name}"))
            return own[-1]

        ctx.callback(over)
        return sem


class Norm:

    BANKS = (6, 7)

    def __init__(self, core, ctx, name, sem, src, scale=None, shift=None, keep_xt=True, buffers=1, xt=None):
        nc = core.nc
        self.core, self.src, self.scale, self.shift, self.keep_xt = core, src, scale, shift, keep_xt
        sb = lambda n, shape, dt=F32: ctx.enter_context(nc.sbuf_tensor(f"{name}_{n}", shape, dt))
        self.stats = sb("ln_stats", [P, GT, 6])
        self.moments = sb("ln_moments", [P, GT, 2])
        self.std = sb("ln_std", [P, GT])
        self.rstd = sb("ln_rstd", [P, GT])
        self.xn = [sb(f"xn{i}", [P, GT, D]) for i in range(buffers)]
        self.xg = sb("xg", [P, DK, GW])
        self.xt = (xt or sb("xt", [P, DK, TOKENS])) if keep_xt else None
        self.stats_done = sem("ln_stats_done")
        self.moments_done = sem("ln_moments_done")
        self.std_done = sem("ln_std_done")
        self.rstd_done = sem("ln_rstd_done")
        self.xn_done = sem("xn_done")
        self.turned = sem("xn_turned")
        self.xg_done = sem("xg_done")
        self.xt_done = sem("xt_done")

    def vector(self, dve, g, xn_free=None, par=0):
        self.vector_moments(dve, g)
        self.vector_xn(dve, g, xn_free, par)

    def vector_moments(self, dve, g):
        for j in range(GT):
            dve.bn_stats(self.stats[:, j, :], self.src[:, GT * g + j, :]).then_inc(self.stats_done, 1)
        wait_apart(dve, self.stats_done, GT * g + GT, self.core)
        for j in range(GT):
            dve.bn_aggr(self.moments[:, j, :], self.stats[:, j, :]).then_inc(self.moments_done, 1)

    def vector_xn(self, dve, g, xn_free, par):
        dve.wait_ge(self.std_done, g + 1)
        dve.reciprocal(self.rstd[:, :], self.std[:, :]).then_inc(self.rstd_done, 1)
        dve.wait_ge(self.rstd_done, g + 1)
        for s, v in xn_free or []:
            dve.wait_ge(s, v)
        for j in range(GT):
            last = dve.tensor_scalar(self.xn[par][:, j, :], self.src[:, GT * g + j, :], self.moments[:, j, 0:1],
                                     self.rstd[:, j:j + 1], ALU.subtract, ALU.mult)
        last.then_inc(self.xn_done, 1)

    def scalar_std(self, act, g):
        act.wait_ge(self.moments_done, GT * g + GT)
        act.activation(self.std[:, :], self.moments[:, :, 1], ACT.Sqrt,
                       bias=self.core.eps[:, 0:1]).then_inc(self.std_done, 1)

    def tensor(self, pe, g, banks_free=None, par=0):
        pe.wait_ge(self.xn_done, g + 1)
        for s, v in banks_free or []:
            pe.wait_ge(s, v)
        for k in range(DK):
            for j in range(GT):
                last = pe.transpose(self.core.bank[self.BANKS[k]][:, j * P:(j + 1) * P],
                                    self.xn[par][:, j, k * P:(k + 1) * P], self.core.ident[:, :])
        last.then_inc(self.turned, 1)

    def scalar_copies(self, act, g, xg_free=None):
        act.wait_ge(self.turned, g + 1)
        for s, v in xg_free or []:
            act.wait_ge(s, v)

        def copy(dst, k):
            if self.scale is None:
                return act.copy(dst, self.core.bank[self.BANKS[k]][:, :])
            return act.activation(dst, self.core.bank[self.BANKS[k]][:, :], ACT.Identity,
                                  bias=self.shift[:, k:k + 1], scale=self.scale[:, k:k + 1])

        for k in range(DK):
            last = copy(self.xg[:, k, :], k)
        last.then_inc(self.xg_done, 1)
        if self.keep_xt:
            for k in range(DK):
                last = copy(self.xt[:, k, bass.ds(GW * g, GW)], k)
            last.then_inc(self.xt_done, 1)

    def banks_read(self, g):
        return [(self.xt_done if self.keep_xt else self.xg_done, g + 1)]


def load_stage(core):
    nc, io = core.nc, core.io
    with ExitStack() as ctx:
        loaded = core.semaphores(ctx, "load")("loaded")
        block = ctx.enter_context(nc.Block())

        @block.sync
        def _(sp):
            x = io["x"].rearrange("(t p) d -> p t d", p=P)
            for q in range(4):
                sp.dma_start(core.X[:, 4 * q:4 * q + 4, :], x[:, 4 * q:4 * q + 4, :]).then_inc(loaded, 16)
            sp.dma_start(core.ident[:, :], io["ident"]).then_inc(loaded, 16)
            sp.wait_ge(loaded, 80)

        @block.vector
        def _(dve):
            dve.memset(core.zero[:, :], 0.0)
            dve.memset(core.eps[:, 0:1], LN_EPS)
            dve.memset(core.eps[:, 1:2], RMS_EPS)


def clear_slots(core, sp):
    view = core.slots_x.rearrange("(e p j) d -> e p (j d)", p=P, j=CT)
    with sp.Fori(0, E1) as e:
        sp.dma_start(view[bass.ds(e, 1), :, :].rearrange("a p n -> (a p) n"), core.zero[:, :]).then_inc(core.cleared, 16)


def small_moe_stage(core, name, clear=False):
    nc, io, X, B = core.nc, core.io, core.X, core.bank
    FIRST, SECOND = 4, 8
    ROUTE = FIRST + SECOND
    with ExitStack() as ctx:
        sb = lambda n, shape, dt=F32: ctx.enter_context(nc.sbuf_tensor(f"{name}_{n}", shape, dt))
        two = lambda n, shape, dt=F32: [sb(f"{n}{i}", shape, dt) for i in range(2)]
        sem = core.semaphores(ctx, f"{name}")
        norm = Norm(core, ctx, name, sem, X, keep_xt=False)
        w_router = sb("w_router", [P, DK, E0])
        raw = [sb(f"raw{i}", [P, DK * C0 * P]) for i in range(3)]
        w_hi = [sb(f"w_hi{i}", [P, DK * C0 * P], F32R) for i in range(3)]
        w_lo = [sb(f"w_lo{i}", [P, DK * C0 * P], F32R) for i in range(3)]
        spread_f = sb("spread_f", [P, C0 * P])
        spread = sb("spread", [P, C0 * P], F32R)
        iota = sb("iota", [P, E0])
        xt_hi = two("xt_hi", [P, DK, GW], F32R)
        xt_lo = two("xt_lo", [P, DK, GW], F32R)
        score = sb("score", [P, GT, E0])
        best = sb("best", [P, GT, 8])
        best_at = sb("best_at", [P, GT, 8], U32)
        best_atf = sb("best_atf", [P, GT, 2])
        gap = sb("gap", [P, GT, 1])
        exp_gap = sb("exp_gap", [P, GT, 1])
        total = sb("total", [P, GT, 1])
        prob = sb("prob", [P, GT, 2])
        hot = sb("hot", [P, 2, GT, E0])
        weight = sb("weight", [P, GT, E0])
        halves = sb("halves", [P, GT, P])
        weight_t = sb("weight_t", [P, GW], F32R)
        silu = two("silu", [P, GW])
        hidden = two("hidden", [P, GW])
        hidden_hi = two("hidden_hi", [P, C0, GW], F32R)
        hidden_lo = two("hidden_lo", [P, C0, GW], F32R)

        small_in = sem("small_in")
        weights_in = sem("weights_in")
        spread_done = sem("spread_done")
        w_hi_done = sem("w_hi_done")
        w_lo_done = sem("w_lo_done")
        xt_hi_done = sem("xt_hi_done")
        xt_lo_done = sem("xt_lo_done")
        begun = sem("begun")
        score_mm = sem("score_mm")
        score_read = sem("score_read")
        routing = sem("routing")
        exp_done = sem("exp_done")
        weight_mm = sem("weight_mm")
        weight_done = sem("weight_done")
        gate_up_mm = sem("gate_up_mm")
        spread_mm = sem("spread_mm")
        silu_done = sem("silu_done")
        gated = sem("gated")
        weighted = sem("weighted")
        hi_done = sem("hi_done")
        lo_done = sem("lo_done")
        down_mm = sem("down_mm")
        added = sem("added")

        block = ctx.enter_context(nc.Block())

        @block.sync
        def _(sp):
            for dst, src in ((w_router, "l0_router"), (iota, "iota8"), (spread_f, "spread")):
                sp.dma_start(dst[:], io[src]).then_inc(small_in, 16)
            for i, src in enumerate(("l0_gate", "l0_up", "l0_down")):
                sp.dma_start(raw[i][:, :], io[src].rearrange("p k f -> p (k f)")).then_inc(weights_in, 16)
                sp.wait_ge(weights_in, 16 * i + 16)
            if clear:
                clear_slots(core, sp)

        @block.tensor
        def _(pe):
            def scores(g):
                pe.wait_ge(norm.xg_done, g + 1)
                for j in range(GT):
                    for k in range(DK):
                        last = pe.matmul(B[6][:, j * E0:(j + 1) * E0], norm.xg[:, k, j * P:(j + 1) * P],
                                         w_router[:, k, :], start=(k == 0), stop=(k == DK - 1))
                last.then_inc(score_mm, 1)

            def turn_weights(g):
                pe.wait_ge(routing, ROUTE * g + ROUTE + 1)
                for j in range(GT):
                    last = pe.transpose(B[7][:, j * P:(j + 1) * P], halves[:, j, :], core.ident[:, :])
                last.then_inc(weight_mm, 1)

            def gate_up(g, par, c):
                pe.wait_ge(gated, C0 * g + c + 1)
                if c == 0:
                    pe.wait_ge(xt_lo_done, g + 1)
                for i in range(2):
                    bank = B[2 * (c % 2) + i][:, :]
                    for k in range(DK):
                        at = slice((k * C0 + c) * P, (k * C0 + c + 1) * P)
                        for n, (w, x) in enumerate(((w_hi, xt_hi), (w_hi, xt_lo), (w_lo, xt_hi))):
                            last = pe.matmul(bank, w[i][:, at], x[par][:, k, :],
                                             start=(k == 0 and n == 0), stop=(k == DK - 1 and n == 2))
                last.then_inc(gate_up_mm, 1)
                if c == 0:
                    turn_weights(g)
                    pe.wait_ge(weight_done, g + 1)
                pe.wait_ge(weighted, C0 * g + c + 1)
                pe.matmul(B[5][:, :], spread[:, c * P:(c + 1) * P], weight_t[:, :], start=True, stop=True
                          ).then_inc(spread_mm, 1)

            def down(g, par, j):
                if j == 0:
                    pe.wait_ge(lo_done, C0 * g + C0)
                    pe.wait_ge(w_lo_done, 3)
                pe.wait_ge(added, GT * g + j + 1)
                for c in range(C0):
                    for n, (h, w) in enumerate(((hidden_hi, w_hi), (hidden_hi, w_lo), (hidden_lo, w_hi))):
                        last = pe.matmul(B[4][:, 0:D], h[par][:, c, j * P:(j + 1) * P], w[2][:, c * D:(c + 1) * D],
                                         start=(c == 0 and n == 0), stop=(c == C0 - 1 and n == 2))
                last.then_inc(down_mm, 1)

            def group(g, par, nth, last_group):
                first = isinstance(g, int) and g == 0
                for c in range(C0):
                    gate_up(g, par, c)
                    if c < GT and not first:
                        down(g - 1, 1 - par, c)
                    if c == 2 and not last_group:
                        norm.tensor(pe, g + 1, [(score_read, g + 1), (weight_done, g + 1)])
                    if c == 3 and not last_group:
                        scores(g + 1)

            norm.tensor(pe, 0)
            pe.wait_ge(small_in, 48)
            scores(0)
            pe.wait_ge(spread_done, 1)
            pe.wait_ge(w_lo_done, 2)
            over_buffered_groups(pe, group)
            for j in range(GT):
                down(GROUPS - 1, 1, j)

        @block.scalar
        def _(act):
            def split(g, par):
                norm.scalar_copies(act, g, None if isinstance(g, int) and g == 0 else [(score_mm, g), (xt_lo_done, g)])
                act.wait_ge(norm.xg_done, g + 1)
                act.copy(xt_hi[par][:, :, :], norm.xg[:, :, :]).then_inc(xt_hi_done, 1)

            def gap_exp(g):
                act.wait_ge(routing, ROUTE * g + FIRST + 1)
                act.activation(exp_gap[:, :, :], gap[:, :, :], ACT.Exp).then_inc(exp_done, 1)

            def copy_weights(g):
                act.wait_ge(weight_mm, g + 1)
                act.copy(weight_t[:, :], B[7][:, :]).then_inc(weight_done, 1)

            def group(g, par, nth, last_group):
                for c in range(C0):
                    n = C0 * g + c
                    if c == 0:
                        copy_weights(g)
                    if c == 4 and not last_group:
                        gap_exp(g + 1)
                    act.wait_ge(gate_up_mm, n + 1)
                    act.activation(silu[c % 2][:, :], B[2 * (c % 2)][:, :], ACT.Silu).then_inc(silu_done, 1)
                    act.wait_ge(weighted, n + 2)
                    act.copy(hidden_hi[par][:, c, :], hidden[c % 2][:, :]).then_inc(hi_done, 1)
                    if c == 0 and not last_group:
                        norm.scalar_std(act, g + 1)
                    if c == 2 and not last_group:
                        split(g + 1, 1 - par)

            norm.scalar_std(act, 0)
            split(0, 0)
            act.wait_ge(small_in, 48)
            act.copy(spread[:, :], spread_f[:, :]).then_inc(spread_done, 1)
            for i in range(3):
                if i == 2:
                    gap_exp(0)
                act.wait_ge(weights_in, 16 * i + 16)
                act.copy(w_hi[i][:, :], raw[i][:, :]).then_inc(w_hi_done, 1)
            over_buffered_groups(act, group)

        @block.gpsimd
        def _(pool):
            def split(g, par):
                pool.wait_ge(xt_hi_done, g + 1)
                pool.sem_inc(begun, 1)
                pool.tensor_tensor(xt_lo[par][:, :, :], norm.xg[:, :, :], xt_hi[par][:, :, :].bitcast(F32),
                                   ALU.subtract).then_inc(xt_lo_done, 1)

            def group(g, par, nth, last_group):
                if not last_group:
                    split(g + 1, 1 - par)

            split(0, 0)
            over_buffered_groups(pool, group)

        @block.vector
        def _(dve):
            def route_first(g):
                s = Steps(dve, routing, ROUTE * g + 1)
                dve.wait_ge(score_mm, g + 1)
                dve.tensor_copy(score[:, :, :], B[6][:, 0:GT * E0].rearrange("p (j e) -> p j e", e=E0)
                                ).then_inc(score_read, 1)
                wait_apart(dve, score_read, g + 1, core)
                for j in range(GT):
                    last = dve.max(best[:, j, :], score[:, j, :])
                s.then(last, apart=core)
                for j in range(GT):
                    last = dve.max_index(best_at[:, j, :], best[:, j, :], score[:, j, :])
                s.then(last)
                s.then(dve.tensor_copy(best_atf[:, :, :], best_at[:, :, 0:2]))
                s.then(dve.tensor_tensor(gap[:, :, :], best[:, :, 1:2], best[:, :, 0:1], ALU.subtract))
                assert s.n == FIRST

            def route_second(g):
                s = Steps(dve, routing, ROUTE * g + FIRST + 1)
                dve.wait_ge(exp_done, g + 1)
                s.then(dve.tensor_scalar(total[:, :, :], exp_gap[:, :, :], 1.0, 2.0, ALU.add, ALU.mult))
                s.then(dve.reciprocal(prob[:, :, 0:1], total[:, :, :]))
                s.then(dve.tensor_tensor(prob[:, :, 1:2], exp_gap[:, :, :], prob[:, :, 0:1], ALU.mult))
                for k in range(2):
                    last = dve.tensor_tensor(hot[:, k, :, :], iota[:, :].unsqueeze(1).to_broadcast([P, GT, E0]),
                                             best_atf[:, :, k:k + 1].to_broadcast([P, GT, E0]), ALU.is_equal)
                s.then(last)
                for k in range(2):
                    last = dve.tensor_tensor(hot[:, k, :, :], hot[:, k, :, :],
                                             prob[:, :, k:k + 1].to_broadcast([P, GT, E0]), ALU.mult)
                s.then(last)
                s.then(dve.tensor_tensor(weight[:, :, :], hot[:, 0, :, :], hot[:, 1, :, :], ALU.add))
                s.then(dve.tensor_copy(halves[:, :, 0:E0].bitcast(F32R), weight[:, :, :]))
                s.then(dve.tensor_tensor(halves[:, :, E0:2 * E0].bitcast(F32R), weight[:, :, :], halves[:, :, 0:E0],
                                         ALU.subtract))
                assert s.n == SECOND

            def chunk(g, par, c):
                n = C0 * g + c
                dve.wait_ge(silu_done, n + 1)
                dve.tensor_tensor(hidden[c % 2][:, :], silu[c % 2][:, :], B[2 * (c % 2) + 1][:, :], ALU.mult
                                  ).then_inc(gated, 1)
                dve.wait_ge(gated, n + 3)
                dve.wait_ge(spread_mm, n + 1)
                dve.tensor_tensor(hidden[c % 2][:, :], hidden[c % 2][:, :], B[5][:, :], ALU.mult
                                  ).then_inc(weighted, 1)
                dve.wait_ge(hi_done, n + 1)
                dve.tensor_tensor(hidden_lo[par][:, c, :], hidden[c % 2][:, :], hidden_hi[par][:, c, :].bitcast(F32),
                                  ALU.subtract).then_inc(lo_done, 1)

            def add(g, j):
                t = GT * g + j
                dve.wait_ge(down_mm, t + 1)
                dve.tensor_tensor(X[:, t, :], B[4][:, 0:D], X[:, t, :], ALU.add).then_inc(added, 1)

            def group(g, par, nth, last_group):
                first = isinstance(g, int) and g == 0
                for c in range(C0):
                    if c == 4 and not last_group:
                        route_first(g + 1)
                    if c == 5 and not last_group:
                        route_second(g + 1)
                    chunk(g, par, c)
                    if c < GT and not first:
                        add(g - 1, c)
                    if c == 0 and not last_group:
                        norm.vector(dve, g + 1, [(norm.turned, g + 1)])

            def split_weights(i):
                dve.wait_ge(w_hi_done, i + 1)
                dve.tensor_tensor(w_lo[i][:, :], raw[i][:, :], w_hi[i][:, :].bitcast(F32), ALU.subtract
                                  ).then_inc(w_lo_done, 1)

            dve.sem_inc(gated, 2)
            dve.sem_inc(weighted, 1)
            dve.sem_inc(added, 1)
            dve.memset(halves[:, :, :], 0.0).then_inc(routing, 1)
            norm.vector(dve, 0)
            dve.wait_ge(routing, 1)
            split_weights(0)
            split_weights(1)
            dve.wait_ge(small_in, 48)
            route_first(0)
            route_second(0)
            split_weights(2)
            over_buffered_groups(dve, group)
            for j in range(GT):
                add(GROUPS - 1, j)


def ttt_stage(core):
    with ExitStack() as ctx:
        keys = ctx.enter_context(core.nc.sbuf_tensor("keys", [P, H0 // HG, TOKENS], F32))
        read = ctx.enter_context(core.nc.sbuf_tensor("read", [P, STEPS0, BATCH, H0 // HG, DH0], F32))
        v_dram = core.nc.dram_tensor("v_dram", [TOKENS, D], F32).ap()
        z_dram = core.nc.dram_tensor("z_dram", [TOKENS, D], F32).ap()
        ttt_project(core, keys, read, v_dram)
        ttt_scan(core, keys, read, z_dram)
    ttt_output(core, z_dram)


def token_rows(dram, b, h):
    rows = dram.rearrange("(b t s) (h n) -> b h s t n", b=BATCH, s=MB, h=HG)[:, h]
    return rows[bass.ds(b, 1)].rearrange("a s t n -> (a s) t n")


def read_rows(read, b, h):
    rows = read[h * MB:(h + 1) * MB, :, :, :, :].rearrange("s t b g e -> s b t (g e)")
    return rows[:, bass.ds(b, 1)].rearrange("s a t n -> s (a t) n")


def ttt_project(core, keys, read, v_dram):
    nc, io, B = core.nc, core.io, core.bank
    with ExitStack() as ctx:
        sb = lambda n, shape, dt=F32: ctx.enter_context(nc.sbuf_tensor(f"ttt_{n}", shape, dt))
        sem = core.semaphores(ctx, "ttt")
        norm = Norm(core, ctx, "ttt", sem, core.X)
        w_k = sb("w_k", [P, DK, D])
        w_k_rot = sb("w_k_rot", [P, DK, D])
        w_v = sb("w_v", [P, DK, D])
        cos = sb("cos", [P, TOKENS])
        sin = sb("sin", [P, TOKENS])
        turned_part = sb("turned_part", [P, 2, GW])
        values = sb("values", [P, GT, D])

        weights_in = sem("weights_in")
        keys_mm = sem("keys_mm")
        products = sem("products")
        keys_done = sem("keys_done")
        values_mm = sem("values_mm")
        values_read = sem("values_read")
        values_out = sem("values_out")
        values_in = sem("values_in")
        block = ctx.enter_context(nc.Block())

        @block.sync
        def _(sp):
            for dst, src in ((w_k, "ttt_k"), (w_k_rot, "ttt_k_rot"), (w_v, "ttt_v"), (cos, "cos_a"), (sin, "sin_a")):
                sp.dma_start(dst[:], io[src]).then_inc(weights_in, 16)
            sp.sem_inc(values_out, 16)
            out = v_dram.rearrange("(t p) d -> p t d", p=P)
            per_batch = GROUPS // BATCH
            with sp.Fori(0, BATCH) as b:
                for i in range(per_batch):
                    g = per_batch * b + i
                    sp.wait_ge(values_read, g + 2)
                    sp.dma_start(out[:, bass.ds(GT * g, GT), :], values[:, :, :]).then_inc(values_out, 16)
                sp.wait_ge(values_out, 16 * per_batch * (b + 1) + 16)
                for h in range(HG):
                    sp.dma_start(read_rows(read, b, h), token_rows(v_dram, b, h)).then_inc(values_in, 16)
            sp.wait_ge(values_in, 16 * BATCH * HG)

        @block.tensor
        def _(pe):
            def group(g, last_group):
                pe.wait_ge(norm.xt_done, g + 1)
                pe.wait_ge(products, g + 1)
                for w, b0 in ((w_k, 0), (w_k_rot, 2)):
                    for h in range(H0 // HG):
                        for k in range(DK):
                            last = pe.matmul(B[b0 + h][:, :], w[:, k, h * P:(h + 1) * P],
                                             norm.xt[:, k, bass.ds(GW * g, GW)], start=(k == 0), stop=(k == DK - 1))
                last.then_inc(keys_mm, 1)
                pe.wait_ge(values_read, g + 1)
                for j in range(GT):
                    for k in range(DK):
                        last = pe.matmul(B[4 + j // 2][:, (j % 2) * D:(j % 2 + 1) * D],
                                         norm.xg[:, k, j * P:(j + 1) * P], w_v[:, k, :],
                                         start=(k == 0), stop=(k == DK - 1))
                last.then_inc(values_mm, 1)
                if not last_group:
                    norm.tensor(pe, g + 1, norm.banks_read(g))

            norm.tensor(pe, 0)
            pe.wait_ge(weights_in, 80)
            over_groups(pe, group)

        @block.scalar
        def _(act):
            def group(g, last_group):
                if not last_group:
                    norm.scalar_std(act, g + 1)
                act.wait_ge(values_mm, g + 1)
                act.wait_ge(values_out, 16 * g + 16)
                for q in range(2):
                    last = act.copy(values[:, 2 * q:2 * q + 2, :],
                                    B[4 + q][:, :].rearrange("p (j d) -> p j d", d=D))
                last.then_inc(values_read, 1)
                if not last_group:
                    norm.scalar_copies(act, g + 1, [(values_mm, g + 1)])

            act.sem_inc(values_read, 1)
            norm.scalar_std(act, 0)
            norm.scalar_copies(act, 0)
            over_groups(act, group)

        @block.vector
        def _(dve):
            def group(g, last_group):
                if not last_group:
                    norm.vector(dve, g + 1, [(norm.turned, g + 1)])
                at = bass.ds(GW * g, GW)
                dve.wait_ge(keys_mm, g + 1)
                dve.wait_ge(keys_done, g + 1)
                for h in range(2):
                    dve.tensor_tensor(keys[:, h, at], B[h][:, :], cos[:, at], ALU.mult)
                    last = dve.tensor_tensor(turned_part[:, h, :], B[2 + h][:, :], sin[:, at], ALU.mult)
                last.then_inc(products, 1)
                dve.wait_ge(products, g + 2)
                dve.tensor_tensor(keys[:, :, at], keys[:, :, at], turned_part[:, :, :], ALU.add).then_inc(keys_done, 1)

            dve.sem_inc(products, 1)
            dve.sem_inc(keys_done, 1)
            norm.vector(dve, 0)
            dve.wait_ge(weights_in, 80)
            over_groups(dve, group)
            dve.wait_ge(keys_done, GROUPS + 1)


def ttt_scan(core, keys, read, z_dram):
    nc, io, B = core.nc, core.io, core.bank
    SET = NBG // 2
    SETS = (slice(0, SET), slice(SET, NBG))
    Z_BANK, CHANGE_BANK = (0, 4), (1, 5)
    with ExitStack() as ctx:
        sb = lambda n, shape, dt=F32: ctx.enter_context(nc.sbuf_tensor(f"scan_{n}", shape, dt))
        sem = core.semaphores(ctx, "scan")
        mask = sb("mask", [P, HG])
        k_fm = sb("k_fm", [P, 2, NBG, HG * MB])
        k_tm = sb("k_tm", [P, 2, NBG, P])
        start = sb("start", [P, NBG, DH0])
        state = [sb(f"state{i}", [P, SET, DH0]) for i in range(2)]
        error = [sb(f"error{i}", [P, SET, DH0]) for i in range(2)]

        loaded = sem("loaded")
        spread = sem("spread")
        turned = sem("turned")
        z_mm = [sem(f"z_mm{i}") for i in range(2)]
        error_done = [sem(f"error_done{i}") for i in range(2)]
        change_mm = [sem(f"change_mm{i}") for i in range(2)]
        state_done = [sem(f"state_done{i}") for i in range(2)]
        stored = sem("stored")
        block = ctx.enter_context(nc.Block())

        @block.sync
        def _(sp):
            sp.dma_start(mask[:, :], io["head_mask"]).then_inc(loaded, 16)
            sp.dma_start(start[:, :, :], io["w_start"].rearrange("p (b e) -> p b e", e=DH0)).then_inc(loaded, 16)
            for part in range(2):
                steps = slice(STEPS0 // 2 * part, STEPS0 // 2 * (part + 1))
                for i in range(2):
                    sp.wait_ge(state_done[i], steps.stop + 1)
                for b in range(BATCH):
                    for h in range(HG):
                        sp.dma_start(token_rows(z_dram, b, h)[:, steps, :], read_rows(read, b, h)[:, steps, :]
                                     ).then_inc(stored, 16)
            sp.wait_ge(stored, 2 * 16 * BATCH * HG)

        @block.vector
        def _(dve):
            kv = keys[:, :, :].rearrange("p h (b s) -> p (h b) s", b=BATCH)

            def spread_keys(t, par):
                src = kv[:, :, bass.ds(MB * t, MB)].unsqueeze(2).to_broadcast([P, NBG, HG, MB])
                m = mask[:, :].unsqueeze(1).unsqueeze(3).to_broadcast([P, NBG, HG, MB])
                dve.tensor_tensor(k_fm[:, par, :, :].rearrange("p b (h s) -> p b h s", s=MB), src, m, ALU.mult).then_inc(spread, 1)

            def turn(t, par):
                dve.wait_ge(spread, t + 1)
                dve.transpose(k_tm[:, par, :, :].rearrange("p b k -> p (b k)"),
                              k_fm[:, par, :, :].rearrange("p b k -> p (b k)")).then_inc(turned, 1)

            def step(t, par, final):
                product = lambda bank: B[bank][:, 0:SET * DH0].rearrange("p (b e) -> p b e", e=DH0)
                for i, bgs in enumerate(SETS):
                    dve.wait_ge(z_mm[i], t + 1)
                    dve.tensor_tensor(error[i][:, :, :], product(Z_BANK[i]), read[:, t, :, i, :], ALU.subtract
                                      ).then_inc(error_done[i], 1)
                    if i == 0 and final != 1:
                        turn(t + 1, 1 - par)
                if not final:
                    spread_keys(t + 2, par)
                for i, bgs in enumerate(SETS):
                    dve.wait_ge(error_done[i], t + 1)
                    dve.tensor_scalar(read[:, t, :, i, :], product(Z_BANK[i]), 1.0, None, ALU.mult)
                for i, bgs in enumerate(SETS):
                    dve.wait_ge(change_mm[i], t + 1)
                    dve.wait_ge(state_done[i], t + 1)
                    dve.scalar_tensor_tensor(state[i][:, :, :], product(CHANGE_BANK[i]), -STEP_SCALE,
                                             state[i][:, :, :], ALU.mult, ALU.add).then_inc(state_done[i], 1)

            dve.wait_ge(loaded, 32)
            spread_keys(0, 0)
            spread_keys(1, 1)
            turn(0, 0)
            for i, bgs in enumerate(SETS):
                dve.tensor_copy(state[i][:, :, :], start[:, bgs, :]).then_inc(state_done[i], 1)
            over_pairs(dve, STEPS0, step)

        @block.tensor
        def _(pe):
            def step(t, par, final):
                for i in range(2):
                    pe.wait_ge(state_done[i], t + 1)
                    for b in range(SET):
                        last = pe.matmul(B[Z_BANK[i]][:, b * DH0:(b + 1) * DH0], k_fm[:, par, SET * i + b, :],
                                         state[i][:, b, :], start=True, stop=True)
                    last.then_inc(z_mm[i], 1)
                pe.wait_ge(turned, t + 1)
                for i in range(2):
                    pe.wait_ge(error_done[i], t + 1)
                    for b in range(SET):
                        last = pe.matmul(B[CHANGE_BANK[i]][:, b * DH0:(b + 1) * DH0], k_tm[:, par, SET * i + b, :],
                                         error[i][:, b, :], start=True, stop=True)
                    last.then_inc(change_mm[i], 1)

            over_pairs(pe, STEPS0, step)


def ttt_output(core, z_dram):
    nc, io, X, B = core.nc, core.io, core.X, core.bank
    with ExitStack() as ctx:
        sb = lambda n, shape, dt=F32: ctx.enter_context(nc.sbuf_tensor(f"tout_{n}", shape, dt))
        sem = core.semaphores(ctx, "tout")
        z = sb("z", [P, TILES, D])
        w_o = sb("w_o", [P, DK, D])
        gamma = sb("gamma", [P, DK])
        beta = sb("beta", [P, DK])
        norm = Norm(core, ctx, "tout", sem, z, scale=gamma, shift=beta, keep_xt=False)
        first_in = sem("first_in")
        weights_in = sem("weights_in")
        rest_in = sem("rest_in")
        out_mm = sem("out_mm")
        added = sem("added")
        block = ctx.enter_context(nc.Block())

        @block.sync
        def _(sp):
            rows = z_dram.rearrange("(t p) d -> p t d", p=P)
            sp.dma_start(z[:, 0:GT, :], rows[:, 0:GT, :]).then_inc(first_in, 16)
            for dst, src in ((w_o, "ttt_o"), (gamma, "ttt_gamma"), (beta, "ttt_beta")):
                sp.dma_start(dst[:], io[src]).then_inc(weights_in, 16)
            sp.dma_start(z[:, GT:TILES, :], rows[:, GT:TILES, :]).then_inc(rest_in, 16)

        @block.tensor
        def _(pe):
            def group(g, last_group):
                pe.wait_ge(norm.xg_done, g + 1)
                pe.wait_ge(added, g + 1)
                for j in range(GT):
                    for k in range(DK):
                        last = pe.matmul(B[j // 2][:, (j % 2) * D:(j % 2 + 1) * D],
                                         norm.xg[:, k, j * P:(j + 1) * P], w_o[:, k, :],
                                         start=(k == 0), stop=(k == DK - 1))
                last.then_inc(out_mm, 1)
                if not last_group:
                    norm.tensor(pe, g + 1, norm.banks_read(g))

            norm.tensor(pe, 0)
            pe.wait_ge(weights_in, 48)
            over_groups(pe, group)

        @block.scalar
        def _(act):
            def group(g, last_group):
                if not last_group:
                    norm.scalar_std(act, g + 1)
                    norm.scalar_copies(act, g + 1, [(out_mm, g + 1)])

            norm.scalar_std(act, 0)
            act.wait_ge(weights_in, 48)
            norm.scalar_copies(act, 0)
            over_groups(act, group)

        @block.vector
        def _(dve):
            def group(g, last_group):
                if not last_group:
                    norm.vector(dve, g + 1, [(norm.turned, g + 1)])
                dve.wait_ge(out_mm, g + 1)
                for q in range(2):
                    rows = X[:, bass.ds(GT * g + 2 * q, 2), :]
                    last = dve.tensor_tensor(rows, rows, B[q][:, :].rearrange("p (j d) -> p j d", d=D), ALU.add)
                last.then_inc(added, 1)

            dve.sem_inc(added, 1)
            dve.wait_ge(first_in, 16)
            norm.vector(dve, 0)
            dve.wait_ge(rest_in, 16)
            over_groups(dve, group)




def big_moe_stage(core, name, absorbed=None, final=False):
    nc = core.nc
    with ExitStack() as ctx:
        weight = ctx.enter_context(nc.sbuf_tensor(f"{name}_weight", [P, TILES, K1], F32))
        slot = ctx.enter_context(nc.sbuf_tensor(f"{name}_slot", [P, TILES, K1], U32))
        xt = ctx.enter_context(nc.sbuf_tensor(f"{name}_xt", [P, DK, TOKENS], F32))
        big_moe_route(core, name, weight, slot, xt)
        big_moe_experts(core, name)
        big_moe_combine(core, name, weight, slot, xt, absorbed, final)


def big_moe_route(core, name, weight, slot, xt):
    nc, io, X, B = core.nc, core.io, core.X, core.bank
    FIRST, SECOND = 14, 8
    ROUTE = FIRST + SECOND
    NOWHERE = 1.0e6
    with ExitStack() as ctx:
        sb = lambda n, shape, dt=F32: ctx.enter_context(nc.sbuf_tensor(f"{name}_r_{n}", shape, dt))
        sem = core.semaphores(ctx, f"{name}_r")
        norm = Norm(core, ctx, f"{name}_r", sem, X, buffers=2, xt=xt)
        w_router = sb("w_router", [P, DK, E1])
        iota = sb("iota", [P, E1])
        earlier_f = sb("earlier_f", [P, P])
        earlier = sb("earlier", [P, P], BF16)
        ones = sb("ones", [P, P], BF16)
        score = sb("score", [P, GT, E1])
        top = sb("top", [P, GT, 1])
        total = sb("total", [P, GT, 1])
        inverse = sb("inverse", [P, GT, 1])
        best = sb("best", [P, GT, 8])
        best_at = sb("best_at", [P, GT, 8], U32)
        expert = sb("expert", [P, GT, K1])
        share = sb("share", [P, GT, K1])
        hot = sb("hot", [P, GT, K1, E1])
        taken = sb("taken", [P, GT, E1], BF16)
        before = sb("before", [P, E1])
        before_b = sb("before_b", [P, E1], BF16)
        group_sum = sb("group_sum", [P, E1])
        place = sb("place", [P, GT, K1])
        late = sb("late", [P, GT, K1])
        slot_f = sb("slot_f", [P, GT, K1])
        slot_now = [sb(f"slot_now{i}", [P, GT * K1], U32) for i in range(2)]

        weights_in = sem("weights_in")
        consts = sem("consts")
        score_mm = sem("score_mm")
        routing = sem("routing")
        exp_done = sem("exp_done")
        place_mm = sem("place_mm")
        slots_done = sem("slots_done")
        begun = sem("begun")
        scattered = [sem(f"scattered{i}") for i in range(2)]
        carried = sem("carried")
        block = ctx.enter_context(nc.Block())

        @block.sync
        def _(sp):
            for dst, src in ((w_router, "l1_router"), (iota, "iota64"), (earlier_f, "earlier")):
                sp.dma_start(dst[:], io[src]).then_inc(weights_in, 16)

        @block.tensor
        def _(pe):
            def scores(g):
                pe.wait_ge(norm.xt_done, g + 1)
                for j in range(GT):
                    for k in range(DK):
                        last = pe.matmul(B[6][:, j * E1:(j + 1) * E1], norm.xg[:, k, j * P:(j + 1) * P],
                                         w_router[:, k, :], start=(k == 0), stop=(k == DK - 1))
                last.then_inc(score_mm, 1)

            def places(g):
                pe.wait_ge(routing, ROUTE * g + FIRST)
                pe.wait_ge(carried, 2 * g + 1)
                for j in range(GT):
                    out = B[7][:, j * E1:(j + 1) * E1]
                    pe.matmul(out, earlier[:, :], taken[:, j, :], start=True, stop=False)
                    for i in range(j):
                        pe.matmul(out, ones[:, :], taken[:, i, :], start=False, stop=False)
                    last = pe.matmul(out, ones[:, :], before_b[:, :], start=False, stop=True)
                last.then_inc(place_mm, 1)

            def group(g, par, nth, last_group):
                scores(g)
                places(g)
                if not last_group:
                    norm.tensor(pe, g + 1, [(slots_done, g + 1)], 1 - par)

            norm.tensor(pe, 0)
            pe.wait_ge(weights_in, 48)
            pe.wait_ge(consts, 2)
            over_buffered_groups(pe, group)

        @block.scalar
        def _(act):
            def group(g, par, nth, last_group):
                act.wait_ge(routing, ROUTE * g + 3)
                act.activation(score[:, :, :], score[:, :, :], ACT.Exp).then_inc(exp_done, 1)
                if not last_group:
                    norm.scalar_std(act, g + 1)
                    norm.scalar_copies(act, g + 1, [(score_mm, g + 1)])

            norm.scalar_std(act, 0)
            norm.scalar_copies(act, 0)
            over_buffered_groups(act, group)

        @block.vector
        def _(dve):
            def route(g, par, last_group):
                s = Steps(dve, routing, ROUTE * g)
                dve.wait_ge(score_mm, g + 1)
                s.then(dve.tensor_copy(score[:, :, :], B[6][:, 0:GT * E1].rearrange("p (j e) -> p j e", e=E1)))
                s.then(dve.tensor_reduce(top[:, :, :], score[:, :, :], AX, ALU.max))
                s.then(dve.tensor_tensor(score[:, :, :], score[:, :, :], top[:, :, :].to_broadcast([P, GT, E1]),
                                         ALU.subtract))
                dve.wait_ge(exp_done, g + 1)
                s.then(dve.tensor_reduce(total[:, :, :], score[:, :, :], AX, ALU.add))
                s.then(dve.reciprocal(inverse[:, :, :], total[:, :, :]))
                s.then(dve.tensor_tensor(score[:, :, :], score[:, :, :], inverse[:, :, :].to_broadcast([P, GT, E1]),
                                         ALU.mult), apart=core)
                for j in range(GT):
                    last = dve.max(best[:, j, :], score[:, j, :])
                s.then(last, apart=core)
                for j in range(GT):
                    last = dve.max_index(best_at[:, j, :], best[:, j, :], score[:, j, :])
                s.then(last)
                s.then(dve.tensor_copy(expert[:, :, :], best_at[:, :, 0:K1]))
                s.then(dve.tensor_reduce(total[:, :, :], best[:, :, 0:K1], AX, ALU.add))
                s.then(dve.tensor_scalar(total[:, :, :], total[:, :, :], 1e-20, 2.0, ALU.add, ALU.mult))
                s.then(dve.reciprocal(inverse[:, :, :], total[:, :, :]))
                dve.tensor_tensor(share[:, :, :], best[:, :, 0:K1], inverse[:, :, :].to_broadcast([P, GT, K1]),
                                  ALU.mult)
                for j in range(GT):
                    last = dve.tensor_tensor(hot[:, j, :, :], iota[:, :].unsqueeze(1).to_broadcast([P, K1, E1]),
                                             expert[:, j, :].unsqueeze(2).to_broadcast([P, K1, E1]), ALU.is_equal)
                s.then(last)
                with nc.allow_low_precision("sums of ones"):
                    s.then(dve.tensor_reduce(taken[:, :, :], hot[:, :, :, :].rearrange("p j k e -> p j e k"),
                                             AX, ALU.add))
                assert s.n == FIRST
                if not last_group:
                    norm.vector_moments(dve, g + 1)
                dve.wait_ge(place_mm, g + 1)
                for j in range(GT):
                    at = B[7][:, j * E1:(j + 1) * E1].unsqueeze(1).to_broadcast([P, K1, E1])
                    last = dve.tensor_tensor(hot[:, j, :, :], hot[:, j, :, :], at, ALU.mult)
                s.then(last)
                s.then(dve.tensor_reduce(place[:, :, :], hot[:, :, :, :], AX, ALU.add))
                dve.scalar_tensor_tensor(slot_f[:, :, :], expert[:, :, :], float(CAP), place[:, :, :],
                                         ALU.mult, ALU.add)
                s.then(dve.tensor_scalar(late[:, :, :], place[:, :, :], float(CAP), None, ALU.is_ge))
                s.then(dve.scalar_tensor_tensor(slot_f[:, :, :], late[:, :, :], NOWHERE, slot_f[:, :, :],
                                                ALU.mult, ALU.add))
                s.then(dve.tensor_scalar(late[:, :, :], late[:, :, :], -1.0, 1.0, ALU.mult, ALU.add))
                s.then(dve.tensor_tensor(weight[:, bass.ds(GT * g, GT), :], share[:, :, :], late[:, :, :], ALU.mult))
                s.then(dve.tensor_copy(slot[:, bass.ds(GT * g, GT), :], slot_f[:, :, :]))
                s.then(dve.tensor_reduce(group_sum[:, :], taken[:, :, :].rearrange("p j e -> p e j"), AX, ALU.add))
                assert s.n == ROUTE
                dve.tensor_copy(slot_now[par][:, :].rearrange("p (j k) -> p j k", k=K1), slot_f[:, :, :]
                                ).then_inc(slots_done, 1)
                dve.tensor_tensor(before[:, :], before[:, :], group_sum[:, :], ALU.add).then_inc(carried, 1)
                dve.wait_ge(carried, 2 * g + 2)
                dve.tensor_copy(before_b[:, :], before[:, :]).then_inc(carried, 1)

            def group(g, par, nth, last_group):
                route(g, par, last_group)
                if not last_group:
                    first = isinstance(g, int) and g == 0
                    norm.vector_xn(dve, g + 1, [] if first else
                                   [(norm.turned, g), (scattered[1 - par], 16 * GT * K1 * previous(par, nth))],
                                   1 - par)

            norm.vector(dve, 0)
            dve.memset(ones[:, :], 1.0)
            dve.memset(before[:, :], 0.0)
            dve.memset(before_b[:, :], 0.0).then_inc(carried, 1)
            dve.wait_ge(weights_in, 48)
            dve.tensor_copy(earlier[:, :], earlier_f[:, :]).then_inc(consts, 1)
            dve.wait_ge(carried, 1)
            dve.sem_inc(consts, 1)
            over_buffered_groups(dve, group)
            dve.wait_ge(carried, 2 * GROUPS + 1)

        @block.gpsimd
        def _(pool):
            pool.wait_ge(core.cleared, 16 * E1)

            def group(g, par, nth, last_group):
                pool.wait_ge(slots_done, g + 1)
                pool.sem_inc(begun, 1)
                for j in range(GT):
                    for k in range(K1):
                        at = slot_now[par][:, j * K1 + k:j * K1 + k + 1]
                        pool.indirect_dma_start(out=core.slots_x, out_offset=bass.IndirectOffsetOnAxis(ap=at, axis=0),
                                                in_=norm.xn[par][:, j, :], in_offset=None, bounds_check=SLOTS - 1,
                                                oob_is_err=False).then_inc(scattered[par], 16)

            over_buffered_groups(pool, group)
            for par in range(2):
                pool.wait_ge(scattered[par], 16 * GT * K1 * GROUPS // 2)


def big_moe_experts(core, name):
    nc, io, B = core.nc, core.io, core.bank
    W = 2 * FA + FBM
    with ExitStack() as ctx:
        sb = lambda n, shape, dt=F32: ctx.enter_context(nc.sbuf_tensor(f"{name}_e_{n}", shape, dt))
        two = lambda n, shape, dt=F32: [sb(f"{n}{i}", shape, dt) for i in range(2)]
        sem = core.semaphores(ctx, f"{name}_e")
        x = two("x", [P, CT, D])
        w = two("w", [P, DK, W])
        w_hi = two("w_hi", [P, DK, W], F32R)
        w_lo = two("w_lo", [P, DK, W], F32R)
        rows = two("rows", [P, 2, D])
        rows_hi = two("rows_hi", [P, 2, D], F32R)
        rows_lo = two("rows_lo", [P, 2, D], F32R)
        xt_hi = two("xt_hi", [P, DK, CAP], F32R)
        xt_lo = two("xt_lo", [P, DK, CAP], F32R)
        silu_a = sb("silu_a", [P, CAP])
        silu_b = sb("silu_b", [FB, CAP])
        hidden_a = two("hidden_a", [P, CAP])
        hidden_b = two("hidden_b", [FB, CAP])
        hidden_a_hi = two("hidden_a_hi", [P, CAP], F32R)
        hidden_b_halves = two("hidden_b_halves", [FBM, CAP], F32R)
        hidden_a_lo = two("hidden_a_lo", [P, CAP], F32R)
        y = two("y", [P, CT, D])

        zeroed = sem("zeroed")
        x_in = [sem(f"x_in{i}") for i in range(2)]
        w_in = [sem(f"w_in{i}") for i in range(2)]
        rows_in = [sem(f"rows_in{i}") for i in range(2)]
        w_hi_done = sem("w_hi_done")
        w_lo_done = sem("w_lo_done")
        rows_hi_done = sem("rows_hi_done")
        rows_lo_done = sem("rows_lo_done")
        begun = sem("begun")
        turned = sem("turned")
        xt_hi_done = sem("xt_hi_done")
        xt_lo_done = sem("xt_lo_done")
        a_mm = sem("a_mm")
        b_mm = sem("b_mm")
        silu_done = sem("silu_done")
        hidden_done = sem("hidden_done")
        hidden_hi_done = sem("hidden_hi_done")
        hidden_lo_done = sem("hidden_lo_done")
        down_mm = sem("down_mm")
        y_act = sem("y_act")
        y_dve = sem("y_dve")
        stored = [sem(f"stored{i}") for i in range(2)]
        block = ctx.enter_context(nc.Block())
        x_view = core.slots_x.rearrange("(e p j) d -> p e (j d)", p=P, j=CT)
        y_view = core.slots_y.rearrange("(e p j) d -> p e (j d)", p=P, j=CT)
        gate_up_view = io["l1_gate_up"].rearrange("e p k f -> p e (k f)")
        down_view = io["l1_down"].rearrange("e f d -> f e d")

        def over_steps(eng, step):
            step(0, 0, 1, None)
            with eng.Fori(0, E1 // 2 - 2) as i:
                step(2 * i + 1, 1, i + 1, None)
                step(2 * i + 2, 0, i + 2, None)
            step(E1 - 3, 1, E1 // 2 - 1, 2)
            step(E1 - 2, 0, E1 // 2, 1)
            step(E1 - 1, 1, E1 // 2, 0)

        first = lambda e: isinstance(e, int) and e == 0

        @block.sync
        def _(sp):
            def load_x(e, par):
                sp.dma_start(x[par][:, :, :].rearrange("p j d -> p (j d)"), x_view[:, e, :]).then_inc(x_in[par], 16)

            def load_w(e, par):
                sp.dma_start(w[par][:, :, :].rearrange("p k f -> p (k f)"), gate_up_view[:, e, :]
                             ).then_inc(w_in[par], 16)

            def load_rows(e, par):
                sp.dma_start(rows[par][:, 0, :], down_view[0:FA, e, :]).then_inc(rows_in[par], 16)
                for at in (0, UB):
                    sp.dma_start(rows[par][at:at + FB, 1, :], down_view[FA:F1, e, :]).then_inc(rows_in[par], 16)

            def store_y(e, par):
                sp.wait_ge(y_act, e + 2)
                sp.wait_ge(y_dve, e + 2)
                sp.dma_start(y_view[:, e, :], y[par][:, :, :].rearrange("p a b -> p (a b)")).then_inc(stored[par], 16)

            def step(e, par, nth, last):
                if last is None:
                    sp.wait_ge(turned, e + 2)
                    load_x(e + 3, 1 - par)
                    sp.wait_ge(w_lo_done, e + 2)
                    load_w(e + 3, 1 - par)
                if last is None or last == 2:
                    sp.wait_ge(rows_lo_done, e + 1)
                    load_rows(e + 2, par)
                if not first(e):
                    store_y(e - 1, 1 - par)

            for par in range(2):
                sp.sem_inc(stored[par], 16)
                load_x(par, par)
                load_w(par, par)
            sp.wait_ge(zeroed, 1)
            for par in range(2):
                load_rows(par, par)
            sp.wait_ge(turned, 1)
            load_x(2, 0)
            sp.wait_ge(w_lo_done, 1)
            load_w(2, 0)
            over_steps(sp, step)
            store_y(E1 - 1, 1)
            for par in range(2):
                sp.wait_ge(stored[par], 16 * (E1 // 2) + 16)

        @block.tensor
        def _(pe):
            def turn(e, par, nth):
                pe.wait_ge(x_in[par], 16 * nth)
                if not first(e):
                    pe.wait_ge(xt_lo_done, e)
                for k in range(DK):
                    for j in range(CT):
                        last = pe.transpose(B[6 + k][:, j * P:(j + 1) * P], x[par][:, j, k * P:(k + 1) * P],
                                            core.ident[:, :])
                last.then_inc(turned, 1)

            def gate_up(e, par, nth):
                pe.wait_ge(w_lo_done, e + 1)
                pe.wait_ge(xt_lo_done, e + 1)
                passes = ((w_hi, xt_hi), (w_hi, xt_lo), (w_lo, xt_hi))
                for at, m, b, done in ((0, FA, 0, None), (FA, FA, 1, a_mm), (2 * FA, FBM, 2, b_mm)):
                    if b != 1:
                        pe.wait_ge(hidden_done, 2 * e + (2 if b else 1))
                    for k in range(DK):
                        for i, (weight, token) in enumerate(passes):
                            last = pe.matmul(B[b][0:m, 0:CAP], weight[par][:, k, at:at + m], token[par][:, k, :],
                                             start=(k == 0 and i == 0), stop=(k == DK - 1 and i == 2))
                    if done is not None:
                        last.then_inc(done, 1)

            def down(e, par, nth):
                pe.wait_ge(rows_lo_done, e + 1)
                pe.wait_ge(hidden_lo_done, e + 1)
                pe.wait_ge(y_act, e + 1)
                pe.wait_ge(y_dve, e + 1)
                for j in range(CT):
                    out = B[3 + j // 2][:, (j % 2) * D:(j % 2 + 1) * D]
                    at = slice(j * P, (j + 1) * P)
                    passes = ((hidden_a_hi[par][:, at], rows_hi[par][:, 0, :]),
                              (hidden_a_hi[par][:, at], rows_lo[par][:, 0, :]),
                              (hidden_a_lo[par][:, at], rows_hi[par][:, 0, :]),
                              (hidden_b_halves[par][:, at], rows_hi[par][0:FBM, 1, :]),
                              (hidden_b_halves[par][0:FB, at], rows_lo[par][0:FB, 1, :]))
                    for i, (h, weight) in enumerate(passes):
                        last = pe.matmul(out, h, weight, start=(i == 0), stop=(i == len(passes) - 1))
                last.then_inc(down_mm, 1)

            def step(e, par, nth, last):
                if last != 0:
                    turn(e + 1, 1 - par, following(par, nth))
                gate_up(e, par, nth)
                if not first(e):
                    down(e - 1, 1 - par, previous(par, nth))

            turn(0, 0, 1)
            over_steps(pe, step)
            down(E1 - 1, 1, E1 // 2)

        @block.scalar
        def _(act):
            def split(e, par, nth):
                act.wait_ge(turned, e + 1)
                for k in range(DK):
                    act.copy(xt_hi[par][:, k, :], B[6 + k][:, 0:CAP]).then_inc(xt_hi_done, 1)
                act.wait_ge(w_in[par], 16 * nth)
                act.copy(w_hi[par][:, :, :], w[par][:, :, :]).then_inc(w_hi_done, 1)

            def silu(e, par):
                act.wait_ge(a_mm, e + 1)
                act.activation(silu_a[:, :], B[0][:, 0:CAP], ACT.Silu).then_inc(silu_done, 1)
                act.wait_ge(b_mm, e + 1)
                act.activation(silu_b[:, :], B[2][0:FB, 0:CAP], ACT.Silu).then_inc(silu_done, 1)
                act.wait_ge(hidden_done, 2 * e + 3)
                act.copy(hidden_a_hi[par][:, :], hidden_a[par][:, :]).then_inc(hidden_hi_done, 1)
                act.wait_ge(hidden_done, 2 * e + 4)
                act.copy(hidden_b_halves[par][0:FB, :], hidden_b[par][:, :]).then_inc(hidden_hi_done, 1)

            def output(e, par, nth):
                act.wait_ge(stored[par], 16 * nth)
                act.wait_ge(down_mm, e + 1)
                act.copy(y[par][:, 0:2, :], B[3][:, :].rearrange("p (j d) -> p j d", d=D)).then_inc(y_act, 1)

            def step(e, par, nth, last):
                if last != 0:
                    split(e + 1, 1 - par, following(par, nth))
                silu(e, par)
                if not first(e):
                    output(e - 1, 1 - par, previous(par, nth))

            act.sem_inc(y_act, 1)
            act.wait_ge(zeroed, 1)
            split(0, 0, 1)
            over_steps(act, step)
            output(E1 - 1, 1, E1 // 2)

        @block.gpsimd
        def _(pool):
            def after(sem, value):
                pool.wait_ge(sem, value)
                pool.sem_inc(begun, 1)

            def split_w(e, par):
                after(w_hi_done, e + 1)
                pool.tensor_tensor(w_lo[par][:, :, :], w[par][:, :, :], w_hi[par][:, :, :].bitcast(F32),
                                   ALU.subtract).then_inc(w_lo_done, 1)

            def split_rows(e, par, nth):
                after(rows_in[par], 48 * nth)
                pool.tensor_copy(rows_hi[par][:, :, :], rows[par][:, :, :]).then_inc(rows_hi_done, 1)
                after(rows_hi_done, e + 1)
                pool.tensor_tensor(rows_lo[par][:, :, :], rows[par][:, :, :], rows_hi[par][:, :, :].bitcast(F32),
                                   ALU.subtract).then_inc(rows_lo_done, 1)

            def step(e, par, nth, last):
                if last != 0:
                    split_w(e + 1, 1 - par)
                else:
                    after(down_mm, e - 1)
                split_rows(e, par, nth)

            for i in range(2):
                pool.memset(rows[i][:, 1, :], 0.0)
                last = pool.tensor_copy(hidden_b_halves[i][:, :], core.zero[0:FBM, 0:CAP])
            last.then_inc(zeroed, 1)
            pool.wait_ge(zeroed, 1)
            split_w(0, 0)
            over_steps(pool, step)

        @block.vector
        def _(dve):
            def split(e, par):
                for k in range(DK):
                    dve.wait_ge(xt_hi_done, 2 * e + k + 1)
                    last = dve.tensor_tensor(xt_lo[par][:, k, :], B[6 + k][:, 0:CAP],
                                             xt_hi[par][:, k, :].bitcast(F32), ALU.subtract)
                last.then_inc(xt_lo_done, 1)

            def hidden(e, par):
                dve.wait_ge(silu_done, 2 * e + 1)
                dve.tensor_tensor(hidden_a[par][:, :], silu_a[:, :], B[1][:, 0:CAP], ALU.mult).then_inc(hidden_done, 1)
                dve.wait_ge(silu_done, 2 * e + 2)
                dve.tensor_tensor(hidden_b[par][:, :], silu_b[:, :], B[2][UB:UB + FB, 0:CAP], ALU.mult
                                  ).then_inc(hidden_done, 1)
                dve.wait_ge(hidden_hi_done, 2 * e + 1)
                dve.tensor_tensor(hidden_a_lo[par][:, :], hidden_a[par][:, :], hidden_a_hi[par][:, :].bitcast(F32),
                                  ALU.subtract)
                dve.wait_ge(hidden_hi_done, 2 * e + 2)
                dve.tensor_tensor(hidden_b_halves[par][UB:UB + FB, :], hidden_b[par][:, :],
                                  hidden_b_halves[par][0:FB, :].bitcast(F32), ALU.subtract).then_inc(hidden_lo_done, 1)

            def output(e, par, nth):
                dve.wait_ge(stored[par], 16 * nth)
                dve.wait_ge(down_mm, e + 1)
                dve.tensor_copy(y[par][:, 2, :], B[4][:, 0:D]).then_inc(y_dve, 1)

            def step(e, par, nth, last):
                if last != 0:
                    split(e + 1, 1 - par)
                hidden(e, par)
                if not first(e):
                    output(e - 1, 1 - par, previous(par, nth))

            dve.sem_inc(y_dve, 1)
            dve.sem_inc(hidden_done, 2)
            split(0, 0)
            over_steps(dve, step)
            output(E1 - 1, 1, E1 // 2)


class SharedExpert:

    NC = len(SHARED)

    def __init__(self, core, ctx, name, sem, xt):
        self.core, self.xt = core, xt
        sb = lambda n, shape, dt=F32: ctx.enter_context(core.nc.sbuf_tensor(f"{name}_sh_{n}", shape, dt))
        self.w_gate = sb("w_gate", [P, DK, FS])
        self.w_up = sb("w_up", [P, DK, FS])
        self.w_down = sb("w_down", [P, self.NC, D])
        self.silu = sb("silu", [P, 2, GW])
        self.hidden = sb("hidden", [P, self.NC, GW])
        self.weights_in = sem("weights_in")
        self.gate_up_mm = sem("gate_up_mm")
        self.silu_done = sem("silu_done")
        self.hidden_done = sem("hidden_done")
        self.down_mm = sem("down_mm")
        self.added = sem("added")

    def sync(self, sp):
        io = self.core.io
        sp.dma_start(self.w_gate[:], io["sh_gate"]).then_inc(self.weights_in, 16)
        sp.dma_start(self.w_up[:], io["sh_up"]).then_inc(self.weights_in, 16)
        for c, (at, n) in enumerate(SHARED):
            sp.dma_start(self.w_down[0:n, c, :], io["sh_down"][at:at + n, :]).then_inc(self.weights_in, 16)

    def tensor(self, pe):
        B, NC = self.core.bank, self.NC

        def gate_up(g, c):
            at, n = SHARED[c]
            pe.wait_ge(self.hidden_done, NC * g + (2 if c == 2 else 1))
            for w, b in ((self.w_gate, B[2 * (c % 2)]), (self.w_up, B[2 * (c % 2) + 1])):
                for k in range(DK):
                    last = pe.matmul(b[0:n, :], w[:, k, at:at + n], self.xt[:, k, bass.ds(GW * g, GW)],
                                     start=(k == 0), stop=(k == DK - 1))
            last.then_inc(self.gate_up_mm, 1)

        pe.wait_ge(self.weights_in, 16 * (2 + NC))
        with pe.Fori(0, GROUPS) as g:
            for c in range(NC):
                gate_up(g, c)
            pe.wait_ge(self.hidden_done, NC * g + NC + 1)
            pe.wait_ge(self.added, g + 1)
            for j in range(GT):
                for c, (_, n) in enumerate(SHARED):
                    last = pe.matmul(B[4 + j // 2][:, (j % 2) * D:(j % 2 + 1) * D],
                                     self.hidden[0:n, c, j * P:(j + 1) * P], self.w_down[0:n, c, :],
                                     start=(c == 0), stop=(c == NC - 1))
            last.then_inc(self.down_mm, 1)
        pe.wait_ge(self.hidden_done, NC * GROUPS + 1)
        pe.wait_ge(self.added, GROUPS + 1)

    def scalar(self, act):
        B, NC = self.core.bank, self.NC
        with act.Fori(0, GROUPS) as g:
            for c, (_, n) in enumerate(SHARED):
                act.wait_ge(self.gate_up_mm, NC * g + c + 1)
                act.wait_ge(self.hidden_done, NC * g + (2 if c == 2 else 1))
                act.activation(self.silu[0:n, c % 2, :], B[2 * (c % 2)][0:n, :], ACT.Silu).then_inc(self.silu_done, 1)

    def vector_start(self, dve):
        dve.sem_inc(self.hidden_done, 1)
        dve.sem_inc(self.added, 1)

    def vector_hidden(self, dve, g, c):
        _, n = SHARED[c]
        dve.wait_ge(self.silu_done, self.NC * g + c + 1)
        dve.tensor_tensor(self.hidden[0:n, c, :], self.silu[0:n, c % 2, :], self.core.bank[2 * (c % 2) + 1][0:n, :],
                          ALU.mult).then_inc(self.hidden_done, 1)

    def vector_add(self, dve, g):
        B, X = self.core.bank, self.core.X
        dve.wait_ge(self.down_mm, g + 1)
        for j in range(GT):
            last = dve.scalar_tensor_tensor(X[:, GT * g + j, :], B[4 + j // 2][:, (j % 2) * D:(j % 2 + 1) * D],
                                            0.5, X[:, GT * g + j, :], ALU.mult, ALU.add)
        last.then_inc(self.added, 1)


def big_moe_combine(core, name, weight, slot, xt, absorbed, final):
    nc, X = core.nc, core.X
    with ExitStack() as ctx:
        sb = lambda n, shape, dt=F32: ctx.enter_context(nc.sbuf_tensor(f"{name}_c_{n}", shape, dt))
        sem = core.semaphores(ctx, f"{name}_c")
        at = [sb(f"at{i}", [P, K1], U32) for i in range(2)]
        rows = [sb(f"rows{i}", [P, K1, D]) for i in range(2)]
        begun = sem("begun")
        picked = sem("picked")
        gathered = [sem(f"gathered{i}") for i in range(2)]
        summed = sem("summed")
        stored = sem("stored")
        shared = SharedExpert(core, ctx, name, sem, xt)
        if absorbed:
            absorbed.inputs(ctx, sem)
        block = ctx.enter_context(nc.Block())

        @block.sync
        def _(sp):
            shared.sync(sp)
            if absorbed:
                absorbed.sync(sp)
            if final:
                out = core.io["out"].rearrange("(t p) d -> p t d", p=P)
                with sp.Fori(0, GROUPS) as g:
                    sp.wait_ge(summed, K1 * GT * (g + 1) + 1)
                    rows = bass.ds(GT * g, GT)
                    sp.dma_start(out[:, rows, :], core.X[:, rows, :]).then_inc(stored, 16)
                sp.wait_ge(stored, 16 * GROUPS)

        @block.tensor
        def _(pe):
            shared.tensor(pe)
            if absorbed:
                absorbed.tensor(pe)

        @block.scalar
        def _(act):
            shared.scalar(act)
            if absorbed:
                absorbed.scalar(act)

        @block.gpsimd
        def _(pool):
            def tile(t, par, nth):
                pool.wait_ge(picked, t + 1)
                pool.sem_inc(begun, 1)
                for k in range(K1):
                    pool.indirect_dma_start(out=rows[par][:, k, :], out_offset=None, in_=core.slots_y,
                                            in_offset=bass.IndirectOffsetOnAxis(ap=at[par][:, k:k + 1], axis=0),
                                            bounds_check=SLOTS - 1, oob_is_err=False).then_inc(gathered[par], 16)

            with pool.Fori(0, TILES // 2) as i:
                tile(2 * i, 0, i + 1)
                tile(2 * i + 1, 1, i + 1)

        @block.vector
        def _(dve):
            def pick(t, par):
                dve.tensor_copy(at[par][:, :], slot[:, t, :]).then_inc(picked, 1)

            def tile(t, par, nth, again):
                dve.wait_ge(gathered[par], 16 * K1 * nth)
                for k in range(K1):
                    dve.wait_ge(summed, K1 * t + k + 1)
                    dve.scalar_tensor_tensor(X[:, t, :], rows[par][:, k, :], weight[:, t, k:k + 1], X[:, t, :],
                                             ALU.mult, ALU.add).then_inc(summed, 1)
                if again:
                    dve.wait_ge(summed, K1 * t + K1 + 1)
                    pick(t + 2, par)

            def group(g, last_group):
                for j in range(GT):
                    tile(GT * g + j, j % 2, GT // 2 * g + j // 2 + 1, not last_group or j < 2)
                    if j == 0:
                        shared.vector_hidden(dve, g, 0)
                        shared.vector_hidden(dve, g, 1)
                    if j == 1:
                        shared.vector_hidden(dve, g, 2)
                    if j == 2:
                        dve.wait_ge(summed, K1 * (GT * g + 3) + 1)
                        shared.vector_add(dve, g)
                        dve.wait_ge(shared.added, g + 2)

            dve.memset(rows[0][:, :, :], 0.0)
            dve.memset(rows[1][:, :, :], 0.0).then_inc(summed, 1)
            dve.wait_ge(summed, 1)
            pick(0, 0)
            pick(1, 1)
            shared.vector_start(dve)
            over_groups(dve, group)
            if absorbed:
                absorbed.vector(dve)


def mla_stage(core, absorbed):
    with ExitStack() as ctx:
        sb = lambda n, shape, dt=F32R: ctx.enter_context(core.nc.sbuf_tensor(f"mla_{n}", shape, dt))
        latent = sb("latent", [P, TILES, 2 * RANK])
        keys_hi = sb("keys_hi", [P, TOKENS])
        keys_lo = sb("keys_lo", [P, TOKENS])
        q_latent = sb("q_latent", [P, TOKENS])
        mla_project(core, latent, keys_hi, keys_lo, q_latent)
        mla_attend(core, latent, keys_hi, keys_lo, q_latent, absorbed.q_weight, absorbed.q_swapped, absorbed.o_weight)


def mla_project(core, latent, keys_hi, keys_lo, q_latent):
    nc, io, X, B = core.nc, core.io, core.X, core.bank
    W = 2 * RANK + ROPE
    CHAIN = 9
    with ExitStack() as ctx:
        sb = lambda n, shape, dt=F32: ctx.enter_context(nc.sbuf_tensor(f"mlap_{n}", shape, dt))
        sem = core.semaphores(ctx, "mlap")
        norm = Norm(core, ctx, "mlap", sem, X, keep_xt=False)
        w_a = sb("w_a", [P, DK, W])
        norm_w = sb("norm_w", [P, 2 * RANK])
        cos = sb("cos", [P, TILES, ROPE])
        sin = sb("sin", [P, TILES, ROPE])
        proj = sb("proj", [P, GT, W])
        square = sb("square", [P, GT, 2 * RANK])
        mean_sq = sb("mean_sq", [P, GT, 2])
        rms = sb("rms", [P, GT, 2])
        inverse = sb("inverse", [P, GT, 2])
        scaled = sb("scaled", [P, GT, 2 * RANK])
        q_f = sb("q_f", [P, GT, RANK])
        q_n = sb("q_n", [P, GT, 2 * RANK])
        k_n = sb("k_n", [P, GT, RANK + ROPE])
        crossed = sb("crossed", [P, GT, ROPE])

        weights_in = sem("weights_in")
        proj_mm = sem("proj_mm")
        chain = sem("chain")
        rms_done = sem("rms_done")
        turned = sem("turned")
        keys_copied = sem("keys_copied")
        copied = sem("copied")
        begun = sem("begun")
        kept_hi = sem("kept_hi")
        kept = sem("kept")
        block = ctx.enter_context(nc.Block())

        @block.sync
        def _(sp):
            for dst, src in ((w_a, "mla_a"), (norm_w, "mla_norms"), (cos, "cos_k"), (sin, "sin_k")):
                sp.dma_start(dst[:], io[src]).then_inc(weights_in, 16)

        @block.tensor
        def _(pe):
            def group(g, last_group):
                pe.wait_ge(norm.xg_done, g + 1)
                pe.wait_ge(chain, CHAIN * g + 1)
                for j in range(GT):
                    for k in range(DK):
                        last = pe.matmul(B[j // 2][:, (j % 2) * D:(j % 2) * D + W],
                                         norm.xg[:, k, j * P:(j + 1) * P], w_a[:, k, :],
                                         start=(k == 0), stop=(k == DK - 1))
                last.then_inc(proj_mm, 1)
                if not last_group:
                    norm.tensor(pe, g + 1, norm.banks_read(g))
                pe.wait_ge(chain, CHAIN * g + CHAIN + 1)
                pe.wait_ge(copied, g + 1)
                for j in range(GT):
                    pe.transpose(B[2][:, j * P:(j + 1) * P], q_n[:, j, :], core.ident[:, :])
                for j in range(GT):
                    last = pe.transpose(B[3][:, j * P:(j + 1) * P], k_n[:, j, :], core.ident[:, :])
                last.then_inc(turned, 1)

            pe.sem_inc(turned, 1)
            norm.tensor(pe, 0)
            pe.wait_ge(weights_in, 64)
            over_groups(pe, group)

        @block.scalar
        def _(act):
            def group(g, last_group):
                if not last_group:
                    norm.scalar_std(act, g + 1)
                    norm.scalar_copies(act, g + 1, [(proj_mm, g + 1)])
                act.wait_ge(chain, CHAIN * g + 4)
                act.activation(rms[:, :, :], mean_sq[:, :, :], ACT.Sqrt, bias=core.eps[:, 1:2],
                               scale=1.0 / RANK).then_inc(rms_done, 1)
                act.wait_ge(turned, g + 2)
                act.copy(q_latent[:, bass.ds(GW * g, GW)], B[2][:, :])
                act.copy(keys_hi[:, bass.ds(GW * g, GW)], B[3][:, :]).then_inc(keys_copied, 1)

            norm.scalar_std(act, 0)
            norm.scalar_copies(act, 0)
            over_groups(act, group)

        @block.gpsimd
        def _(pool):
            pool.sem_inc(kept, 1)
            with pool.Fori(0, GROUPS) as g:
                pool.wait_ge(chain, CHAIN * g + CHAIN + 1)
                pool.sem_inc(begun, 1)
                rows = bass.ds(GT * g, GT)
                pool.tensor_copy(latent[:, rows, 0:RANK], k_n[:, :, 0:RANK]).then_inc(kept_hi, 1)
                pool.wait_ge(kept_hi, g + 1)
                pool.sem_inc(begun, 1)
                pool.tensor_tensor(latent[:, rows, RANK:], k_n[:, :, 0:RANK], latent[:, rows, 0:RANK].bitcast(F32),
                                   ALU.subtract).then_inc(kept, 1)
            pool.wait_ge(kept, GROUPS + 1)

        @block.vector
        def _(dve):
            def group(g, last_group):
                if not last_group:
                    norm.vector(dve, g + 1, [(norm.turned, g + 1)])
                s = Steps(dve, chain, CHAIN * g + 1)
                rows = bass.ds(GT * g, GT)
                dve.wait_ge(proj_mm, g + 1)
                for q in range(2):
                    last = dve.tensor_copy(proj[:, 2 * q:2 * q + 2, :],
                                           B[q][:, :].rearrange("p (j d) -> p j d", d=D)[:, :, 0:W])
                s.then(last)
                s.then(dve.tensor_tensor(square[:, :, :], proj[:, :, 0:2 * RANK], proj[:, :, 0:2 * RANK], ALU.mult))
                s.then(dve.tensor_reduce(mean_sq[:, :, :], square[:, :, :].rearrange("p j (n r) -> p j n r", r=RANK),
                                         AX, ALU.add))
                dve.wait_ge(turned, g + 1)
                dve.wait_ge(kept, g + 1)
                half = ROPE // 2
                pe_at = 2 * RANK
                dve.tensor_tensor(crossed[:, :, 0:half], proj[:, :, pe_at + half:pe_at + ROPE],
                                  sin[:, rows, 0:half], ALU.mult)
                dve.tensor_tensor(crossed[:, :, half:ROPE], proj[:, :, pe_at:pe_at + half],
                                  sin[:, rows, half:ROPE], ALU.mult)
                s.then(dve.tensor_tensor(k_n[:, :, RANK:], proj[:, :, pe_at:], cos[:, rows, :], ALU.mult))
                dve.tensor_tensor(k_n[:, :, RANK:], k_n[:, :, RANK:], crossed[:, :, :], ALU.add)
                dve.wait_ge(rms_done, g + 1)
                s.then(dve.reciprocal(inverse[:, :, :], rms[:, :, :]))
                s.then(dve.tensor_tensor(scaled[:, :, :].rearrange("p j (n r) -> p j n r", r=RANK),
                                         proj[:, :, 0:2 * RANK].rearrange("p j (n r) -> p j n r", r=RANK),
                                         inverse[:, :, :].unsqueeze(3).to_broadcast([P, GT, 2, RANK]), ALU.mult))
                wide = lambda w: w.unsqueeze(1).to_broadcast([P, GT, RANK])
                dve.tensor_tensor(k_n[:, :, 0:RANK], scaled[:, :, RANK:], wide(norm_w[:, RANK:]), ALU.mult)
                s.then(dve.tensor_tensor(q_f[:, :, :], scaled[:, :, 0:RANK], wide(norm_w[:, 0:RANK]), ALU.mult))
                s.then(dve.tensor_copy(q_n[:, :, 0:RANK].bitcast(F32R), q_f[:, :, :]))
                s.then(dve.tensor_tensor(q_n[:, :, RANK:].bitcast(F32R), q_f[:, :, :], q_n[:, :, 0:RANK], ALU.subtract))
                assert s.n == CHAIN
                dve.wait_ge(keys_copied, g + 1)
                at = bass.ds(GW * g, GW)
                dve.tensor_tensor(keys_lo[:, at], B[3][:, :], keys_hi[:, at].bitcast(F32), ALU.subtract
                                  ).then_inc(copied, 1)

            dve.sem_inc(chain, 1)
            dve.sem_inc(copied, 1)
            norm.vector(dve, 0)
            dve.wait_ge(weights_in, 64)
            over_groups(dve, group)


class Absorbed:

    def __init__(self, core, ctx):
        self.core = core
        sb = lambda n, shape, dt=F32R: ctx.enter_context(core.nc.sbuf_tensor(f"mla_{n}", shape, dt))
        self.q_weight = [sb(f"q_weight{i}", [P, NH, RANK + ROPE]) for i in range(2)]
        self.q_swapped = [sb(f"q_swapped{i}", [P, NH, ROPE]) for i in range(2)]
        self.o_weight = sb("o_weight", [P, NH // 2, D], F32)

    def inputs(self, ctx, sem):
        sb = lambda n, shape, dt=F32: ctx.enter_context(self.core.nc.sbuf_tensor(f"mlab_{n}", shape, dt))
        self.w_q = sb("w_q", [NOPE, NH, 2 * RANK])
        self.w_k = sb("w_k", [NOPE, NH, RANK])
        self.w_v = sb("w_v", [VD, NH, RANK])
        self.w_o = sb("w_o", [VD, NH, D])
        self.weight = sb("weight", [P, NH, RANK + ROPE])
        self.swapped = sb("swapped", [P, NH, ROPE])
        self.loaded = sem("absorb_in")
        self.q_mm = sem("q_mm")
        self.o_mm = sem("o_mm")
        self.whole = sem("whole")
        self.hi_done = sem("hi_done")

    def sync(self, sp):
        io = self.core.io
        for dst, src in ((self.w_q[:], "mla_q_nope"), (self.w_k[:], "mla_k"), (self.w_v[:], "mla_v"),
                         (self.w_o[:], "mla_o"), (self.weight[0:RANK, :, RANK:], "mla_q_pe"),
                         (self.weight[RANK:, :, RANK:], "mla_q_pe"), (self.swapped[0:RANK], "mla_q_pe_swapped"),
                         (self.swapped[RANK:], "mla_q_pe_swapped")):
            sp.dma_start(dst, io[src]).then_inc(self.loaded, 16)

    def tensor(self, pe):
        B = self.core.bank
        pe.wait_ge(self.loaded, 128)
        for h in range(NH):
            last = pe.matmul(B[h // 8][:, (h % 8) * RANK:(h % 8 + 1) * RANK], self.w_q[:, h, :], self.w_k[:, h, :],
                             start=True, stop=True)
        last.then_inc(self.q_mm, 1)
        for h in range(NH):
            rows = slice(0, RANK) if h % 2 == 0 else slice(RANK, 2 * RANK)
            last = pe.matmul(B[2 + h // 4][rows, (h // 2 % 2) * D:(h // 2 % 2 + 1) * D], self.w_v[:, h, :],
                             self.w_o[:, h, :], start=True, stop=True)
        last.then_inc(self.o_mm, 1)

    def scalar(self, act):
        B = self.core.bank
        act.wait_ge(self.loaded, 128)
        act.wait_ge(self.q_mm, 1)
        for q in range(2):
            last = act.copy(self.weight[:, 8 * q:8 * q + 8, 0:RANK], B[q][:, :].rearrange("r (h c) -> r h c", c=RANK))
        last.then_inc(self.whole, 1)
        act.copy(self.q_swapped[0][:], self.swapped[:])
        act.wait_ge(self.whole, 1)
        act.copy(self.q_weight[0][:], self.weight[:]).then_inc(self.hi_done, 1)
        act.wait_ge(self.o_mm, 1)
        for q in range(4):
            act.copy(self.o_weight[:, 2 * q:2 * q + 2, :], B[2 + q][:, :].rearrange("p (h d) -> p h d", d=D))

    def vector(self, dve):
        dve.wait_ge(self.hi_done, 1)
        dve.tensor_tensor(self.q_weight[1][:], self.weight[:], self.q_weight[0][:].bitcast(F32), ALU.subtract)
        dve.tensor_tensor(self.q_swapped[1][:], self.swapped[:], self.q_swapped[0][:].bitcast(F32), ALU.subtract)


def mla_attend(core, latent, keys_hi, keys_lo, q_latent, q_weight, q_swapped, o_weight):
    nc, io, X, B = core.nc, core.io, core.X, core.bank
    NKT = SEQ // P
    LAST = NH - 1
    SHARES = [(0, 3), (3, 6), (6, 8)]
    ROTATE = 2
    with ExitStack() as ctx:
        sb = lambda n, shape, dt=F32: ctx.enter_context(nc.sbuf_tensor(f"att_{n}", shape, dt))
        sem = core.semaphores(ctx, "att")
        cos = sb("cos", [P, SEQ])
        sin = sb("sin", [P, SEQ])
        q_w = [[sb(f"q_w{i}{k}", [P, RANK + ROPE], F32R) for k in range(2)] for i in range(2)]
        q_s = [[sb(f"q_s{i}{k}", [P, RANK + ROPE], F32R) for k in range(2)] for i in range(2)]
        values = sb("values", [P, NKT, 2 * RANK], F32R)
        crossed = sb("crossed", [P, GW])
        raw = sb("raw", [P, GW])
        query_hi = [sb(f"query_hi{i}", [P, GW], F32R) for i in range(2)]
        query_lo = [sb(f"query_lo{i}", [P, GW], F32R) for i in range(2)]
        top = sb("top", [P, 2])
        bias = sb("bias", [P, 2])
        total = sb("total", [P, NH, GT])
        inverse = sb("inverse", [P, GT])
        probs = [sb(f"probs{i}", [P, SEQ]) for i in range(2)]
        turned_hi = [sb(f"turned_hi{i}", [P, NKT, GW], F32R) for i in range(2)]
        turned_lo = [sb(f"turned_lo{i}", [P, NKT, GW], F32R) for i in range(2)]
        average = sb("average", [P, GW])
        summed = sb("summed", [P, GT, RANK])
        heads = sb("heads", [P, GT, NH * RANK])
        turned_heads = [p[:, :].rearrange("p (c k) -> p c k", k=P) for p in probs]

        loaded = sem("loaded")
        zeroed = sem("zeroed")
        begun = sem("begun")
        values_done = sem("values_done")
        q_w_done = sem("q_w_done")
        cross_mm = sem("cross_mm")
        cross_read = sem("cross_read")
        query_mm = sem("query_mm")
        query_read = sem("query_read")
        rotating = sem("rotating")
        query_done = sem("query_done")
        score_mm = sem("score_mm")
        top_done = sem("top_done")
        bias_done = sem("bias_done")
        exp_done = sem("exp_done")
        turned = [sem(f"turned{q}") for q in range(2)]
        hi_done = [sem(f"hi_done{q}") for q in range(2)]
        lo_done = [sem(f"lo_done{q}") for q in range(2)]
        average_mm = sem("average_mm")
        average_read = sem("average_read")
        back_mm = sem("back_mm")
        sum_done = sem("sum_done")
        inverse_done = sem("inverse_done")
        heads_done = sem("heads_done")
        out_turned = sem("out_turned")
        out_act = sem("out_act")
        out_dve = sem("out_dve")
        out_mm = sem("out_mm")
        added = sem("added")
        block = ctx.enter_context(nc.Block())

        def over_blocks(eng, body):
            with eng.Fori(0, BATCH) as b:
                with eng.Fori(0, 2) as half:
                    body(2 * b + half, b, half)

        def over_heads(eng, n, body):
            for h in (0, 1):
                body(h, NH * n + h, h, h)
            with eng.Fori(0, NH // 2 - 2) as i:
                body(2 * i + 2, NH * n + 2 * i + 2, 0, None)
                body(2 * i + 3, NH * n + 2 * i + 3, 1, None)
            for h in (LAST - 1, LAST):
                body(h, NH * n + h, h % 2, h)

        @block.sync
        def _(sp):
            sp.dma_start(cos[:, :], io["cos_q"]).then_inc(loaded, 16)
            sp.dma_start(sin[:, :], io["sin_q"]).then_inc(loaded, 16)

        @block.tensor
        def _(pe):
            def cross(n, hh, par):
                pe.wait_ge(q_w_done, hh + 1)
                for k in range(2):
                    last = pe.matmul(B[7][:, :], q_s[par][k][:, :], q_latent[:, bass.ds(GW * n, GW)],
                                     start=(k == 0), stop=(k == 1))
                last.then_inc(cross_mm, 1)

            def project(n, hh, par):
                pe.wait_ge(cross_read, hh + 1)
                for k in range(2):
                    last = pe.matmul(B[7][:, :], q_w[par][k][:, :], q_latent[:, bass.ds(GW * n, GW)],
                                     start=(k == 0), stop=(k == 1))
                last.then_inc(query_mm, 1)

            def scores(b, hh, par, j):
                u = GT * hh + j
                pe.wait_ge(query_done, hh + 2)
                pe.wait_ge(exp_done, u + 1)
                at = slice(j * P, (j + 1) * P)
                passes = ((query_hi[par], keys_hi), (query_hi[par], keys_lo), (query_lo[par], keys_hi))
                for c in range(2):
                    for k, (q, key) in enumerate(passes):
                        last = pe.matmul(B[2 * (j % 2) + c][:, :], q[:, at], key[:, bass.ds(SEQ * b + 512 * c, 512)],
                                         start=(k == 0), stop=(k == 2))
                last.then_inc(score_mm, 1)

            def turn(hh, j):
                u = GT * hh + j
                pe.wait_ge(exp_done, u + 3)
                for q in range(2):
                    pe.wait_ge(lo_done[q], u + 1)
                    for c in range(4):
                        last = pe.transpose(B[4 + q][:, c * P:(c + 1) * P],
                                            probs[j % 2][:, (4 * q + c) * P:(4 * q + c + 1) * P], core.ident[:, :])
                    last.then_inc(turned[q], 1)

            def averages(hh, par, first, end):
                if first == 0:
                    pe.wait_ge(lo_done[0], GT * hh + GT + 1)
                    pe.wait_ge(lo_done[1], GT * hh + GT + 1)
                    pe.wait_ge(average_read, hh + 1)
                for c in range(first, end):
                    for part in (turned_hi, turned_lo):
                        last = pe.matmul(B[6][:, :], values[:, c, :], part[par][:, c, :],
                                         start=(c == 0 and part is turned_hi), stop=(c == NKT - 1 and part is turned_lo))
                if end == NKT:
                    last.then_inc(average_mm, 1)

            def back(hh):
                pe.wait_ge(average_read, hh + 2)
                for j in range(GT):
                    last = pe.transpose(B[7][:, j * P:(j + 1) * P], average[:, j * P:(j + 1) * P], core.ident[:, :])
                last.then_inc(back_mm, 1)

            def block_of_queries(n, b, half):
                pe.wait_ge(sum_done, NH * n + 1)
                cross(n, NH * n, 0)
                project(n, NH * n, 0)
                pe.wait_ge(query_read, NH * n + 1)
                cross(n, NH * n + 1, 1)
                scores(b, NH * n, 0, 0)
                project(n, NH * n + 1, 1)
                scores(b, NH * n, 0, 1)
                pe.wait_ge(values_done, n + 1)

                def head(h, hh, par, stage):
                    for j in range(GT):
                        if j < 2:
                            scores(b, hh, par, j + 2)
                        elif stage != LAST:
                            scores(b, hh + 1, 1 - par, j - 2)
                        turn(hh, j)
                        if j == 0 and stage not in (0, 1):
                            pe.wait_ge(query_read, hh + 1 if stage == LAST else hh + 2)
                            back(hh - 2)
                        if stage != 0 and j < 3:
                            averages(hh - 1, 1 - par, *SHARES[j])
                        if j == 1 and stage not in (LAST - 1, LAST):
                            pe.wait_ge(sum_done, hh + 1 if stage == 0 else hh)
                            cross(n, hh + 2, par)
                        if j == 2 and stage not in (LAST - 1, LAST):
                            project(n, hh + 2, par)

                over_heads(pe, n, head)
                back(NH * n + LAST - 1)
                averages(NH * n + LAST, LAST % 2, 0, NKT)
                pe.wait_ge(sum_done, NH * n + NH)
                back(NH * n + LAST)
                pe.wait_ge(heads_done, NH * n + NH + 1)

                def turn_heads(j):
                    t = GT * n + j
                    pe.wait_ge(out_act, t + 1)
                    pe.wait_ge(out_dve, t + 1)
                    for c in range(NKT):
                        last = pe.transpose(B[4 + c // 4][:, (c % 4) * P:(c % 4 + 1) * P],
                                            heads[:, j, c * P:(c + 1) * P], core.ident[:, :])
                    last.then_inc(out_turned, 1)

                turn_heads(0)
                for j in range(GT):
                    t = GT * n + j
                    if j + 1 < GT:
                        turn_heads(j + 1)
                    pe.wait_ge(out_act, t + 2)
                    pe.wait_ge(out_dve, t + 2)
                    pe.wait_ge(added, t + 1)
                    for c in range(NH // 2):
                        last = pe.matmul(B[6][:, 0:D], turned_heads[j % 2][:, c, :], o_weight[:, c, :],
                                         start=(c == 0), stop=(c == NH // 2 - 1))
                    last.then_inc(out_mm, 1)
                pe.wait_ge(added, GT * n + GT + 1)

            pe.sem_inc(query_mm, 2)
            pe.sem_inc(average_mm, 2)
            pe.sem_inc(back_mm, 1)
            pe.sem_inc(out_act, 1)
            pe.sem_inc(out_dve, 1)
            over_blocks(pe, block_of_queries)

        @block.scalar
        def _(act):
            def read_cross(hh):
                act.wait_ge(cross_mm, hh + 1)
                act.wait_ge(query_done, hh + 1)
                act.copy(crossed[:, :], B[7][:, :]).then_inc(cross_read, 1)

            def read_query(hh):
                act.wait_ge(query_mm, hh + 3)
                act.copy(raw[:, :], B[7][:, :]).then_inc(query_read, 1)

            def exps(h, hh, j):
                act.wait_ge(bias_done, GT * hh + j + 1)
                act.activation(probs[j % 2][:, :], core.scores[j % 2][:, :], ACT.Exp, bias=bias[:, j % 2:j % 2 + 1],
                               scale=SM_SCALE, accum_out=total[:, h, j:j + 1]).then_inc(exp_done, 1)

            def read_average(hh):
                act.wait_ge(average_mm, hh + 3)
                act.wait_ge(back_mm, hh + 1)
                act.copy(average[:, :], B[6][:, :]).then_inc(average_read, 1)

            def block_of_queries(n, b, half):
                act.wait_ge(average_mm, NH * n + 2)
                act.copy(values[:, :, :], latent[:, bass.ds(NKT * b, NKT), :]).then_inc(values_done, 1)
                for h in (0, 1):
                    read_cross(NH * n + h)
                    read_query(NH * n + h)
                exps(0, NH * n, 0)
                exps(0, NH * n, 1)

                def head(h, hh, par, stage):
                    act.wait_ge(average_mm, hh + 1)
                    for j in range(GT):
                        for q in range(2):
                            act.wait_ge(turned[q], GT * hh + j + 1)
                            act.copy(turned_hi[par][:, 4 * q:4 * q + 4, j * P:(j + 1) * P],
                                     B[4 + q][:, :].rearrange("p (c k) -> p c k", k=P)).then_inc(hi_done[q], 1)
                        if j < 2:
                            exps(h, hh, j + 2)
                        elif stage != LAST:
                            exps(h + 1, hh + 1, j - 2)
                        if j == 2 and stage != 0:
                            read_average(hh - 1)
                        if j == 1 and stage not in (LAST - 1, LAST):
                            read_cross(hh + 2)
                        if j == 2 and stage not in (LAST - 1, LAST):
                            read_query(hh + 2)

                over_heads(act, n, head)
                read_average(NH * n + LAST)
                for j in range(GT):
                    act.wait_ge(out_turned, GT * n + j + 1)
                    if j >= 2:
                        act.wait_ge(out_mm, GT * n + j - 1)
                    act.copy(turned_heads[j % 2][:, 0:4, :], B[4][:, :].rearrange("p (c k) -> p c k", k=P)).then_inc(out_act, 1)

            act.sem_inc(exp_done, 2)
            act.sem_inc(average_read, 1)
            over_blocks(act, block_of_queries)

        @block.gpsimd
        def _(pool):
            def after(sem, value):
                pool.wait_ge(sem, value)
                pool.sem_inc(begun, 1)

            def weights(h, hh, par):
                after(query_mm, hh + 1)
                for k in range(2):
                    pool.tensor_copy(q_w[par][k][:, :], q_weight[k][:, h, :])
                    last = pool.tensor_copy(q_s[par][k][:, RANK:], q_swapped[k][:, h, :])
                last.then_inc(q_w_done, 1)

            def rotate(hh, par, half):
                at = bass.ds(GW * half, GW)
                s = Steps(pool, rotating, ROTATE * hh)
                after(query_read, hh + 1)
                pool.tensor_tensor(raw[:, :], raw[:, :], cos[:, at], ALU.mult)
                s.then(pool.tensor_tensor(crossed[:, :], crossed[:, :], sin[:, at], ALU.mult))
                pool.tensor_tensor(query_hi[par][:, :], raw[:, :], crossed[:, :], ALU.add)
                s.then(pool.tensor_tensor(raw[:, :], raw[:, :], crossed[:, :], ALU.add))
                pool.tensor_tensor(query_lo[par][:, :], raw[:, :], query_hi[par][:, :].bitcast(F32), ALU.subtract
                                   ).then_inc(query_done, 1)
                assert s.n == ROTATE

            def block_of_queries(n, b, half):
                weights(0, NH * n, 0)
                weights(1, NH * n + 1, 1)
                pool.wait_ge(loaded, 32)
                with pool.Fori(0, NH // 2 - 1) as i:
                    for k in range(2):
                        rotate(NH * n + 2 * i + k, k, half)
                        weights(2 * i + k + 2, NH * n + 2 * i + k + 2, k)
                for k in range(2):
                    rotate(NH * n + NH - 2 + k, k, half)

            for i in range(2):
                for k in range(2):
                    last = pool.tensor_copy(q_s[i][k][:, :], core.zero[:, 0:P])
            last.then_inc(zeroed, 1)
            pool.wait_ge(zeroed, 1)
            pool.sem_inc(query_done, 1)
            over_blocks(pool, block_of_queries)

        @block.vector
        def _(dve):
            def maxima(hh, j):
                u = GT * hh + j
                dve.wait_ge(score_mm, u + 1)
                dve.tensor_reduce(top[:, j % 2:j % 2 + 1], core.scores[j % 2][:, :], AX, ALU.max).then_inc(top_done, 1)
                dve.wait_ge(top_done, u + 1)
                dve.tensor_scalar(bias[:, j % 2:j % 2 + 1], top[:, j % 2:j % 2 + 1], -SM_SCALE, None,
                                  ALU.mult).then_inc(bias_done, 1)

            def normalise(h, hh):
                dve.wait_ge(back_mm, hh + 2)
                dve.wait_ge(heads_done, hh + 1)
                dve.reciprocal(inverse[:, :], total[:, h, :]).then_inc(inverse_done, 1)
                dve.tensor_reduce(summed[:, :, :], B[7][:, :].rearrange("p (j k r) -> p j r k", k=2, r=RANK),
                                  AX, ALU.add).then_inc(sum_done, 1)
                dve.wait_ge(inverse_done, hh + 1)
                dve.wait_ge(sum_done, hh + 2)
                dve.tensor_tensor(heads[:, :, bass.ds(RANK * h, RANK)], summed[:, :, :],
                                  inverse[:, :].unsqueeze(2).to_broadcast([P, GT, RANK]), ALU.mult
                                  ).then_inc(heads_done, 1)

            def block_of_queries(n, b, half):
                maxima(NH * n, 0)
                maxima(NH * n, 1)

                def head(h, hh, par, stage):
                    for j in range(GT):
                        if j < 2:
                            maxima(hh, j + 2)
                        elif stage != LAST:
                            maxima(hh + 1, j - 2)
                        for q in range(2):
                            rows = (slice(None), slice(4 * q, 4 * q + 4), slice(j * P, (j + 1) * P))
                            dve.wait_ge(hi_done[q], GT * hh + j + 1)
                            dve.tensor_tensor(turned_lo[par][rows], B[4 + q][:, :].rearrange("p (c k) -> p c k", k=P),
                                              turned_hi[par][rows].bitcast(F32), ALU.subtract).then_inc(lo_done[q], 1)
                        if j == 0 and stage not in (0, 1):
                            normalise(h - 2, hh - 2)

                over_heads(dve, n, head)
                normalise(LAST - 1, NH * n + LAST - 1)
                normalise(LAST, NH * n + LAST)

                def copy_heads(j):
                    dve.wait_ge(out_turned, GT * n + j + 1)
                    if j >= 2:
                        dve.wait_ge(out_mm, GT * n + j - 1)
                    dve.tensor_copy(turned_heads[j % 2][:, 4:8, :], B[5][:, :].rearrange("p (c k) -> p c k", k=P)
                                    ).then_inc(out_dve, 1)

                copy_heads(0)
                for j in range(GT):
                    t = GT * n + j
                    if j + 1 < GT:
                        copy_heads(j + 1)
                    dve.wait_ge(out_mm, t + 1)
                    dve.tensor_tensor(X[:, t, :], X[:, t, :], B[6][:, 0:D], ALU.add).then_inc(added, 1)

            dve.sem_inc(lo_done[0], 1)
            dve.sem_inc(lo_done[1], 1)
            dve.sem_inc(heads_done, 1)
            dve.sem_inc(sum_done, 1)
            dve.sem_inc(added, 1)
            over_blocks(dve, block_of_queries)


def moe_mla_stage(core):
    with ExitStack() as ctx:
        absorbed = Absorbed(core, ctx)
        big_moe_stage(core, "moe_a", absorbed)
        mla_stage(core, absorbed)


STAGES = [lambda c: small_moe_stage(c, "ffn_a", clear=True), ttt_stage, lambda c: small_moe_stage(c, "ffn_b"),
          moe_mla_stage, lambda c: big_moe_stage(c, "moe_b", final=True)]


def macaron(nc, io):
    with ExitStack() as ctx:
        core = Core(nc, ctx, io)
        load_stage(core)
        for stage in STAGES:
            stage(core)


def rope_tables():
    t = np.arange(SEQ, dtype=np.float32)
    inv = (1.0 / np.float32(10000.0) ** (np.arange(0, DH0, 2, dtype=np.float32) / np.float32(DH0))).astype(np.float32)
    freqs = (t[:, None] * inv[None, :]).astype(np.float32)
    cos0, sin0 = np.cos(freqs), np.sin(freqs)
    two = lambda a, b: np.concatenate([a, b], axis=1)
    cos_a = np.tile(two(cos0, cos0).T, (HG, BATCH))
    sin_a = np.tile(two(-sin0, sin0).T, (HG, BATCH))
    dim, factor, orig = ROPE, 40.0, 512
    ex = np.arange(0, dim, 2, dtype=np.float64) / dim
    extra, inter = 1.0 / 10000.0 ** ex, 1.0 / (factor * 10000.0 ** ex)
    corr = lambda rot: dim * np.log(orig / (rot * 2 * np.pi)) / (2 * np.log(10000.0))
    low, high = max(np.floor(corr(32.0)), 0), min(np.ceil(corr(1.0)), dim - 1)
    ramp = np.clip((np.arange(dim // 2) - low) / (high - low if high != low else 0.001), 0.0, 1.0)
    inv = inter * ramp + extra * (1.0 - ramp)
    fr = np.outer(np.arange(SEQ, dtype=np.float64), inv)
    msc = (0.1 * 0.707 * np.log(factor) + 1.0) / 1.0
    cos1, sin1 = (np.cos(fr) * msc).astype(np.float32), (np.sin(fr) * msc).astype(np.float32)
    tok = lambda a: a.reshape(KT_TILES, P, -1).transpose(1, 0, 2)
    return {
        "cos_a": cos_a, "sin_a": sin_a,
        "cos_q": np.concatenate([np.ones((RANK, SEQ), np.float32), two(cos1, cos1).T]),
        "sin_q": np.concatenate([np.zeros((RANK, SEQ), np.float32), two(-sin1, sin1).T]),
        "cos_k": np.tile(tok(two(cos1, cos1)), (1, BATCH, 1)), "sin_k": np.tile(tok(two(-sin1, sin1)), (1, BATCH, 1)),
    }


def laid_out(i):
    rows = lambda w: w.reshape(DK, P, *w.shape[1:]).swapaxes(0, 1)
    half = DH0 // 2
    k_w = i["L0_attn_Wk"].reshape(HG, H0 // HG, DH0, D).swapaxes(0, 1)
    k_rot = np.concatenate([k_w[:, :, half:], k_w[:, :, :half]], axis=2)
    a = {
        "x": i["L0_attn_x"].reshape(TOKENS, D),
        "l0_router": rows(i["L0_ffn_w_gate_router"].T),
        "l0_gate": rows(i["L0_ffn_w_gate_proj"].transpose(2, 0, 1)).reshape(P, DK, C0 * P),
        "l0_up": rows(i["L0_ffn_w_up_proj"].transpose(2, 0, 1)).reshape(P, DK, C0 * P),
        "l0_down": i["L0_ffn_w_down_proj"].transpose(0, 2, 1).reshape(C0, P, D).transpose(1, 0, 2),
        "ttt_k": rows(k_w.reshape(D, D).T), "ttt_k_rot": rows(k_rot.reshape(D, D).T), "ttt_v": rows(i["L0_attn_Wv"].T),
        "ttt_o": rows(i["L0_attn_Wo"].T),
        "ttt_gamma": i["L0_attn_ln_gamma"].reshape(DK, P).T, "ttt_beta": i["L0_attn_ln_beta"].reshape(DK, P).T,
    }
    gate, up = i["L1_ffn_w_gate"].transpose(0, 2, 1), i["L1_ffn_w_up"].transpose(0, 2, 1)
    gap = np.zeros((E1, D, UB - FB), np.float32)
    packed = np.concatenate([gate[:, :, :FA], up[:, :, :FA], gate[:, :, FA:], gap, up[:, :, FA:]], axis=2)
    a["l1_gate_up"] = packed.reshape(E1, DK, P, 2 * FA + FBM).transpose(0, 2, 1, 3)
    a["l1_down"] = i["L1_ffn_w_down"].transpose(0, 2, 1)
    a["l1_router"] = rows(i["L1_ffn_gate_w"].T)
    a["sh_gate"] = rows(i["L1_ffn_sh_gate"].T)
    a["sh_up"] = rows(i["L1_ffn_sh_up"].T)
    a["sh_down"] = i["L1_ffn_sh_down"].T
    apart = np.concatenate([np.arange(0, ROPE, 2), np.arange(1, ROPE, 2)])
    swapped = np.roll(apart, ROPE // 2)
    wkv = i["L1_attn_wkv_a"]
    a["mla_a"] = rows(np.concatenate([i["L1_attn_wq_a"], wkv[:, :RANK], wkv[:, RANK:][:, apart]], axis=1))
    a["mla_norms"] = np.tile(np.concatenate([i["L1_attn_q_a_norm_w"], i["L1_attn_kv_a_norm_w"]])[None], (P, 1))
    wq = i["L1_attn_wq_b"].reshape(RANK, NH, NOPE + ROPE)
    kv = i["L1_attn_wkv_b"].reshape(RANK, NH, NOPE + VD)
    a["mla_q_nope"] = np.tile(wq[:, :, :NOPE].transpose(2, 1, 0), (1, 1, 2))
    a["mla_q_pe"] = wq[:, :, NOPE:][:, :, apart]
    a["mla_q_pe_swapped"] = wq[:, :, NOPE:][:, :, swapped]
    a["mla_k"] = kv[:, :, :NOPE].transpose(2, 1, 0)
    a["mla_v"] = kv[:, :, NOPE:].transpose(2, 1, 0)
    a["mla_o"] = i["L1_attn_wo"].reshape(NH, VD, D).transpose(1, 0, 2)
    a.update(rope_tables())
    a["ident"] = np.eye(P, dtype=np.float32)
    experts = np.kron(np.eye(E0, dtype=np.float32), np.ones((1, F0), np.float32))
    a["spread"] = np.concatenate([experts, experts, np.zeros((P - 2 * E0, E0 * F0), np.float32)])
    a["iota8"] = np.tile(np.arange(E0, dtype=np.float32), (P, 1))
    a["iota64"] = np.tile(np.arange(E1, dtype=np.float32), (P, 1))
    a["earlier"] = np.triu(np.ones((P, P), np.float32), 1)
    a["head_mask"] = np.kron(np.eye(HG, dtype=np.float32), np.ones((DH0, 1), np.float32))
    a["w_start"] = np.tile(np.eye(DH0, dtype=np.float32), (HG, NBG))
    return a


def kernel(**inputs):
    import concourse.bacc as bacc
    from concourse.bass_utils import run_bass_kernel_spmd

    nc = bacc.Bacc("TRN2", target_bir_lowering=False, num_devices=1)
    arrays = {f"in_{n}": np.ascontiguousarray(a) for n, a in laid_out({k: np.asarray(v) for k, v in inputs.items()}).items()}
    io = {n.removeprefix("in_"): nc.dram_tensor(n, a.shape, mybir.dt.from_np(a.dtype), kind="ExternalInput").ap()
          for n, a in arrays.items()}
    io["out"] = nc.dram_tensor("out", (TOKENS, D), F32, kind="ExternalOutput").ap()
    macaron(nc, io)
    r = run_bass_kernel_spmd(nc, [arrays], core_ids=[0])
    return r.results[0]["out"].reshape(BATCH, SEQ, D)
```
